# Optimizing a Trainium2 kernel written in Bass

```python
import numpy as np
import jax
import jax.numpy as jnp

def _softmax(x, axis=-1):
    return jax.nn.softmax(x, axis=axis)

def _gelu(x):
    return jax.nn.gelu(x, approximate=True)

def _silu(x):
    return jax.nn.silu(x)

def _sigmoid(x):
    return jax.nn.sigmoid(x)

def _layernorm(x, axis=-1, eps=1e-05):
    m = jnp.mean(x, axis=axis, keepdims=True)
    v = jnp.var(x, axis=axis, keepdims=True)
    return (x - m) / jnp.sqrt(v + eps)

def _scatter_add(tgt, idx, src, axis=0):
    return tgt.at[idx].add(src)

def _segment_sum(src, seg, n):
    return jax.ops.segment_sum(src, seg, n)
kernel_name = 'mk_macaron_d1_jaxref_r8_e11100'

def setup_inputs(seed: int=0):
    np.random.seed(seed)
    _w = jnp.asarray

    def _L0_attn_setup():
        import jax, jax.numpy as jnp
        import numpy as np
        N_HEADS = 16
        D_HEAD = 128
        D_MODEL = 256
        MAXLEN = 256
        key = jax.random.key(seed)
        ks = jax.random.split(key, 9)
        b, t = (2, 256)
        hd = N_HEADS * D_HEAD
        init = 0.02
        return {'x': jax.random.normal(ks[0], (b, t, D_MODEL), dtype=jnp.float32), 'Wq': jax.random.normal(ks[1], (D_MODEL, hd), dtype=jnp.float32) * init, 'bq': jnp.zeros((hd,), dtype=jnp.float32), 'Wk': jax.random.normal(ks[2], (D_MODEL, hd), dtype=jnp.float32) * init, 'bk': jnp.zeros((hd,), dtype=jnp.float32), 'Wv': jax.random.normal(ks[3], (D_MODEL, hd), dtype=jnp.float32) * init, 'bv': jnp.zeros((hd,), dtype=jnp.float32), 'Wo': jax.random.normal(ks[4], (hd, D_MODEL), dtype=jnp.float32) * init, 'bo': jnp.zeros((D_MODEL,), dtype=jnp.float32)}
    _L0_attn_in = _L0_attn_setup()

    def _L0_ffn_setup():
        import jax, jax.numpy as jnp
        import numpy as np
        B, S, D = (4, 512, 256)
        E, K, I, J = (8, 2, 176, 704)
        CAP_FACTOR = 1.25
        STD = 0.02

        def _moe_routed(x_flat, router, w_up_gate, w_down):
            T, d = x_flat.shape
            logits = jnp.einsum('td,de->te', x_flat, router)
            topk_logits, sel = jax.lax.top_k(logits, K)
            cw = jax.nn.softmax(topk_logits, axis=-1).astype(x_flat.dtype)
            C = int(np.ceil(T * K / E * CAP_FACTOR))
            e_flat = sel.reshape(-1)
            oh = jax.nn.one_hot(e_flat, E, dtype=jnp.int32)
            pos_all = jnp.cumsum(oh, axis=0) - oh
            pos = jnp.take_along_axis(pos_all, e_flat[:, None], axis=1)[:, 0]
            valid = pos < C
            safe_pos = jnp.where(valid, pos, C)
            tok = jnp.repeat(jnp.arange(T), K)
            buf = jnp.zeros((E, C, d), x_flat.dtype).at[e_flat, safe_pos].set(x_flat[tok], mode='drop')
            gate_up = jnp.einsum('ecd,edm->ecm', buf, w_up_gate)
            gate, up = jnp.split(gate_up, [I], axis=-1)
            h = jax.nn.silu(gate) * up
            out_buf = jnp.einsum('eci,eid->ecd', h, w_down)
            gathered = out_buf[e_flat, jnp.minimum(safe_pos, C - 1)]
            gathered = gathered * valid[:, None].astype(x_flat.dtype)
            w = cw.reshape(-1)
            y = jnp.zeros((T, d), x_flat.dtype).at[tok].add(w[:, None] * gathered)
            return y

        def _shared_mlp(x_flat, shared_w_up_gate, shared_w_down):
            gu = jnp.einsum('td,dm->tm', x_flat, shared_w_up_gate)
            gate, up = jnp.split(gu, [J], axis=-1)
            return jnp.einsum('tm,md->td', jax.nn.silu(gate) * up, shared_w_down)
        key = jax.random.key(seed)
        kx, kr, ku, kd, ksu, ksd = jax.random.split(key, 6)
        x = jax.random.normal(kx, (B, S, D), dtype=jnp.float32)
        router = STD * jax.random.truncated_normal(kr, -3, 3, (D, E), dtype=jnp.float32)
        w_up_gate = STD * jax.random.truncated_normal(ku, -3, 3, (E, D, 2 * I), dtype=jnp.float32)
        w_down = STD * jax.random.truncated_normal(kd, -3, 3, (E, I, D), dtype=jnp.float32)
        shared_w_up_gate = STD * jax.random.truncated_normal(ksu, -3, 3, (D, 2 * J), dtype=jnp.float32)
        shared_w_down = STD * jax.random.truncated_normal(ksd, -3, 3, (J, D), dtype=jnp.float32)
        return {'x': x, 'router': router, 'w_up_gate': w_up_gate, 'w_down': w_down, 'shared_w_up_gate': shared_w_up_gate, 'shared_w_down': shared_w_down}
    _L0_ffn_in = _L0_ffn_setup()
    _d = {'L0_attn_x': _L0_attn_in['x'], 'L0_attn_Wq': _L0_attn_in['Wq'], 'L0_attn_bq': _L0_attn_in['bq'], 'L0_attn_Wk': _L0_attn_in['Wk'], 'L0_attn_bk': _L0_attn_in['bk'], 'L0_attn_Wv': _L0_attn_in['Wv'], 'L0_attn_bv': _L0_attn_in['bv'], 'L0_attn_Wo': _L0_attn_in['Wo'], 'L0_attn_bo': _L0_attn_in['bo'], 'L0_ffn_router': _L0_ffn_in['router'], 'L0_ffn_w_up_gate': _L0_ffn_in['w_up_gate'], 'L0_ffn_w_down': _L0_ffn_in['w_down'], 'L0_ffn_shared_w_up_gate': _L0_ffn_in['shared_w_up_gate'], 'L0_ffn_shared_w_down': _L0_ffn_in['shared_w_down']}
    _x0 = _d['L0_attn_x']
    _d['L0_attn_x'] = jax.random.normal(jax.random.fold_in(jax.random.key(seed), 1), (8, 256, 256), dtype=_x0.dtype)
    del _x0
    return _d

def reference(L0_attn_x, L0_attn_Wq, L0_attn_bq, L0_attn_Wk, L0_attn_bk, L0_attn_Wv, L0_attn_bv, L0_attn_Wo, L0_attn_bo, L0_ffn_router, L0_ffn_w_up_gate, L0_ffn_w_down, L0_ffn_shared_w_up_gate, L0_ffn_shared_w_down):

    def _L0_attn_ref(x, Wq, bq, Wk, bk, Wv, bv, Wo, bo):
        import jax, jax.numpy as jnp
        import numpy as np
        N_HEADS = 16
        D_HEAD = 128
        D_MODEL = 256
        MAXLEN = 256
        b, t, _ = x.shape
        h, dh = (N_HEADS, D_HEAD)
        scale = 1.0 / np.sqrt(dh).astype(np.float32)
        q = (x @ Wq + bq).reshape(b, h, t, dh)
        k = (x @ Wk + bk).reshape(b, t, h, dh).transpose(0, 2, 3, 1)
        v = (x @ Wv + bv).reshape(b, t, h, dh).transpose(0, 2, 1, 3)
        logits = jnp.einsum('bhtd,bhds->bhts', q, k) * scale
        mask = jnp.triu(jnp.full((t, t), -jnp.inf, dtype=x.dtype), k=1)
        weights = jax.nn.softmax(logits + mask, axis=-1)
        out = jnp.einsum('bhts,bhsd->bhtd', weights, v)
        out = out.transpose(0, 2, 1, 3).reshape(b, t, h * dh)
        return out @ Wo + bo

    def _L0_ffn_ref(x, router, w_up_gate, w_down, shared_w_up_gate, shared_w_down):
        import jax, jax.numpy as jnp
        import numpy as np
        B, S, D = (4, 512, 256)
        E, K, I, J = (8, 2, 176, 704)
        CAP_FACTOR = 1.25
        STD = 0.02

        def _moe_routed(x_flat, router, w_up_gate, w_down):
            T, d = x_flat.shape
            logits = jnp.einsum('td,de->te', x_flat, router)
            topk_logits, sel = jax.lax.top_k(logits, K)
            cw = jax.nn.softmax(topk_logits, axis=-1).astype(x_flat.dtype)
            C = int(np.ceil(T * K / E * CAP_FACTOR))
            e_flat = sel.reshape(-1)
            oh = jax.nn.one_hot(e_flat, E, dtype=jnp.int32)
            pos_all = jnp.cumsum(oh, axis=0) - oh
            pos = jnp.take_along_axis(pos_all, e_flat[:, None], axis=1)[:, 0]
            valid = pos < C
            safe_pos = jnp.where(valid, pos, C)
            tok = jnp.repeat(jnp.arange(T), K)
            buf = jnp.zeros((E, C, d), x_flat.dtype).at[e_flat, safe_pos].set(x_flat[tok], mode='drop')
            gate_up = jnp.einsum('ecd,edm->ecm', buf, w_up_gate)
            gate, up = jnp.split(gate_up, [I], axis=-1)
            h = jax.nn.silu(gate) * up
            out_buf = jnp.einsum('eci,eid->ecd', h, w_down)
            gathered = out_buf[e_flat, jnp.minimum(safe_pos, C - 1)]
            gathered = gathered * valid[:, None].astype(x_flat.dtype)
            w = cw.reshape(-1)
            y = jnp.zeros((T, d), x_flat.dtype).at[tok].add(w[:, None] * gathered)
            return y

        def _shared_mlp(x_flat, shared_w_up_gate, shared_w_down):
            gu = jnp.einsum('td,dm->tm', x_flat, shared_w_up_gate)
            gate, up = jnp.split(gu, [J], axis=-1)
            return jnp.einsum('tm,md->td', jax.nn.silu(gate) * up, shared_w_down)
        b, s, d = x.shape
        x_flat = x.reshape(b * s, d)
        routed = _moe_routed(x_flat, router, w_up_gate, w_down)
        shared = _shared_mlp(x_flat, shared_w_up_gate, shared_w_down)
        return (routed + shared).reshape(b, s, d)
    x = L0_attn_x
    x = x + 0.5 * _L0_ffn_ref(_layernorm(x, axis=-1), L0_ffn_router, L0_ffn_w_up_gate, L0_ffn_w_down, L0_ffn_shared_w_up_gate, L0_ffn_shared_w_down)
    x = x + _L0_attn_ref(_layernorm(x, axis=-1), L0_attn_Wq, L0_attn_bq, L0_attn_Wk, L0_attn_bk, L0_attn_Wv, L0_attn_bv, L0_attn_Wo, L0_attn_bo)
    x = x + 0.5 * _L0_ffn_ref(_layernorm(x, axis=-1), L0_ffn_router, L0_ffn_w_up_gate, L0_ffn_w_down, L0_ffn_shared_w_up_gate, L0_ffn_shared_w_down)
    return x

_drawn_inputs = setup_inputs


def setup_inputs(seed=0):
    import zlib

    import numpy as np

    out = dict(_drawn_inputs(seed))
    spreads = {'L0_attn_bq': (0.0, 0.8),
     'L0_attn_bk': (0.0, 0.8),
     'L0_attn_bv': (0.0, 0.1),
     'L0_attn_bo': (0.0, 0.1)}
    factors = {'L0_attn_Wq': 8.0,
     'L0_attn_Wk': 8.0,
     'L0_ffn_router': 7.106,
     'L0_ffn_w_up_gate': 6.032,
     'L0_ffn_w_down': 6.03}
    for name, (base, spread) in spreads.items():
        noise = np.random.default_rng([zlib.crc32(name.encode()), seed]).standard_normal(out[name].shape)
        drawn = base * np.exp(spread * noise) if base else spread * noise
        out[name] = jnp.asarray(drawn.astype(out[name].dtype))
    for name, factor in factors.items():
        out[name] = (out[name] * factor).astype(out[name].dtype)
    return out
```

```python
from contextlib import ExitStack

import concourse.bass as bass
from concourse import mybir

P = 128
F32 = mybir.dt.float32
F32R = mybir.dt.float32r
BF16 = mybir.dt.bfloat16
U32 = mybir.dt.uint32
ALU = mybir.AluOpType
ACT = mybir.ActivationFunctionType
AX_X = mybir.AxisListType.X

LN_EPS = 1e-5
MASKED = -3.0e38
CHUNK = 512
CT = CHUNK // P
CAP_FACTOR = 1.25
TOP_K = 2
D_HEAD = 128


class Split:

    def __init__(self, ctx, nc, name, shape):
        self.hi = ctx.enter_context(nc.sbuf_tensor(name + "_hi", shape, F32R))
        self.lo = ctx.enter_context(nc.sbuf_tensor(name + "_lo", shape, F32R))


def matmul3(nc, out, stationary, moving, first, last, **kw):
    (s_hi, s_lo), (m_hi, m_lo) = stationary, moving
    nc.tensor.matmul(out, s_hi, m_hi, start=first, stop=False, **kw)
    nc.tensor.matmul(out, s_hi, m_lo, start=False, stop=False, **kw)
    return nc.tensor.matmul(out, s_lo, m_hi, start=False, stop=last, **kw)


def pair(split, *at):
    return split.hi[at], split.lo[at]


def sub_rounded(eng, out_lo, full, hi):
    return eng.tensor_tensor(out_lo, full, hi.bitcast(F32), ALU.subtract)


def open_at_one(eng, *sems):
    for s in sems:
        eng.nop().then_inc(s, 1)


def hold(eng, sem, value):
    eng.wait_ge(sem, value)
    eng.nop(nofuse=True)


class Consts:

    def __init__(self, ctx, nc, n_experts):
        sb = lambda name, shape, dt: ctx.enter_context(nc.sbuf_tensor(name, shape, dt))
        self.ident = sb("ident", [P, P], F32)
        self.ident_bf = sb("ident_bf", [P, P], BF16)
        self.before = sb("before", [P, P], BF16)
        self.ones = sb("ones", [P, P], BF16)
        self.causal = sb("causal", [P, P], BF16)
        self.fold = sb("fold", [64, n_experts], F32)
        self.expert_id = sb("expert_id", [P, n_experts], F32)
        self.minus_half = sb("minus_half", [P, CT], F32)
        self.zeros = sb("zeros", [P, 2 * P], F32)

    def build(self, pool, sem):
        E = self.expert_id.shape[1]
        pool.memset(self.ident[:], 0.0)
        pool.memset(self.ident_bf[:], 0.0)
        pool.memset(self.before[:], 1.0)
        pool.memset(self.ones[:], 1.0)
        pool.memset(self.causal[:], 0.0)
        pool.memset(self.fold[:], 0.0)
        pool.memset(self.minus_half[:], -0.5)
        pool.iota(self.expert_id[:], pattern=[[1, E]], base=0, channel_multiplier=0,
                  allow_small_or_imprecise_dtypes=True)
        pool.memset(self.zeros[:], 0.0).then_inc(sem, 1)
        pool.wait_ge(sem, 1)
        for m in (self.ident, self.ident_bf):
            pool.affine_select(out=m[:], in_=m[:], compare_op=ALU.not_equal, fill=1.0, base=0,
                               pattern=[[-1, P]], channel_multiplier=1)
        pool.affine_select(out=self.before[:], in_=self.before[:], compare_op=ALU.is_gt, fill=0.0,
                           base=0, pattern=[[1, P]], channel_multiplier=-1)
        pool.affine_select(out=self.causal[:], in_=self.causal[:], compare_op=ALU.is_ge, fill=MASKED,
                           base=0, pattern=[[-1, P]], channel_multiplier=1)
        pool.affine_select(out=self.fold[:], in_=self.fold[:], compare_op=ALU.not_equal, fill=1.0,
                           base=0, pattern=[[-1, E]], channel_multiplier=1).then_inc(sem, 1)
        pool.wait_ge(sem, 2)
        pool.affine_select(out=self.fold[:], in_=self.fold[:], compare_op=ALU.not_equal, fill=1.0,
                           base=-32, pattern=[[-1, E]], channel_multiplier=1).then_inc(sem, 1)


class Sems:

    def __init__(self, nc):
        self.nc, self.all = nc, []

    def new(self, name):
        self.all.append(self.nc.alloc_semaphore(name))
        return self.all[-1]

    def clear(self):
        self.nc.clear_and_free_semaphores(self.all)
        self.nc.all_engine_barrier()


class LayerNorm:

    def __init__(self, ctx, sems, nc, tag, D):
        sb = lambda name, shape: ctx.enter_context(nc.sbuf_tensor(tag + name, shape, F32))
        self.stats = sb("stats", [P, CT, 6])
        self.mean_var = sb("mean_var", [P, CT, 2])
        self.var_eps = sb("var_eps", [P, CT])
        self.rstd = sb("rstd", [P, CT])
        self.xn = [sb(f"xn{u}", [P, CT, D]) for u in range(2)]
        sem = lambda name: sems.new(tag + name)
        self.s_step = sem("ln_step")
        self.s_rstd = sem("ln_rstd")
        self.s_xn = sem("ln_xn")
        self.s_tp = sem("xT_psum")
        self.s_hi = sem("xT_hi")
        self.s_lo = sem("xT_lo")
        self.KD = D // P

    def vector(self, dve, X, c, u):
        for a in range(CT):
            ins = dve.bn_stats(self.stats[:, a, :], X[:, bass.ds(c * CT + a, 1), :])
        ins.then_inc(self.s_step, 1)
        hold(dve, self.s_step, 3 * c + 1)
        for a in range(CT):
            ins = dve.bn_aggr(self.mean_var[:, a, :], self.stats[:, a, :])
        ins.then_inc(self.s_step, 1)
        dve.wait_ge(self.s_step, 3 * c + 2)
        dve.tensor_scalar(self.var_eps[:], self.mean_var[:, :, 1], LN_EPS, None,
                          ALU.add).then_inc(self.s_step, 1)
        dve.wait_ge(self.s_rstd, c + 1)
        for a in range(CT):
            ins = dve.tensor_scalar(self.xn[u][:, a, :], X[:, bass.ds(c * CT + a, 1), :],
                                    self.mean_var[:, a, 0:1], self.rstd[:, a:a + 1],
                                    ALU.subtract, ALU.mult)
        ins.then_inc(self.s_xn, 1)

    def pool(self, pool, consts, c):
        pool.wait_ge(self.s_step, 3 * c + 3)
        pool.tensor_tensor(self.rstd[:], self.var_eps[:], consts.minus_half[:],
                           ALU.pow).then_inc(self.s_rstd, 1)


    def transpose(self, nc, pe, consts, ps, c, u):
        pe.wait_ge(self.s_xn, c + 1)
        for k in range(self.KD):
            for a in range(CT):
                at = (4 + 2 * u + k) * CHUNK + a * P
                ins = nc.tensor.transpose(ps[:, at:at + P], self.xn[u][:, a, k * P:(k + 1) * P], consts.ident[:])
            ins.then_inc(self.s_tp, 1)

    def split_hi(self, nc, act, XT, ps, c, u):
        for k in range(self.KD):
            act.wait_ge(self.s_tp, 1 + 2 * c + k + 1)
            b = (4 + 2 * u + k) * CHUNK
            nc.scalar.activation(XT.hi[:, k, bass.ds(c * CHUNK, CHUNK)], ps[:, b:b + CHUNK], ACT.Copy).then_inc(self.s_hi, 1)

    def split_lo(self, nc, dve, XT, ps, c, u):
        for k in range(self.KD):
            dve.wait_ge(self.s_hi, 2 * c + k + 1)
            b = (4 + 2 * u + k) * CHUNK
            cols = bass.ds(c * CHUNK, CHUNK)
            sub_rounded(nc.vector, XT.lo[:, k, cols], ps[:, b:b + CHUNK], XT.hi[:, k, cols]).then_inc(self.s_lo, 1)


def ffn_block(sems, nc, tag, ps, C, X, w, x_in, out, xbuf, ybuf, fill_xbuf):
    D, E = w["router"].shape
    I = w["w_down"].shape[1]
    J = w["shared_w_down"].shape[0]
    NT = X.shape[1]
    T = NT * P
    NCH = NT // CT
    KD = D // P
    CAP = -(-int(T * TOP_K * CAP_FACTOR) // E)
    ST = CAP // P
    assert CAP % P == 0 and KD == 2 and NCH % 2 == 0
    JF, JR = J // P, J % P
    NJ = JF + 1
    IR = I - P
    UPW = 2 * P + 64 + IR
    HALF = CAP // 2
    NOSLOT = 4 * E * CAP
    UPS = 2 * NJ - 1

    with ExitStack() as ctx:
        sb = lambda name, shape, dt=F32: ctx.enter_context(nc.sbuf_tensor(tag + name, shape, dt))
        sem = lambda name: sems.new(tag + name)
        ln = LayerNorm(ctx, sems, nc, tag, D)
        XT = Split(ctx, nc, tag + "xT", [P, KD, T])
        raw_up = sb("raw_up", [P, KD, 2 * J])
        raw_dn = sb("raw_down", [P, NJ, D])
        SU = Split(ctx, nc, tag + "sh_up", [P, KD, 2 * J])
        SD = Split(ctx, nc, tag + "sh_down", [P, NJ, D])
        raw_r = sb("raw_router", [P, KD, E])
        RT = sb("router", [P, KD, 64], F32R)
        H = Split(ctx, nc, tag + "hidden", [P, NJ * CHUNK])
        SG = sb("silu", [P, 2, CHUNK])
        HF = sb("prod", [P, 2, CHUNK])
        LT = sb("logitsT", [64, 2, CHUNK])
        LG = sb("logits", [P, CT, E])
        TOP = sb("top8", [P, CT, 8])
        IX = sb("top8_ix", [P, CT, 8], U32)
        IXF = sb("expert_of", [P, TOP_K, CT])
        OH = [sb(f"onehot{u}", [P, TOP_K * CT, E]) for u in range(2)]
        BASE = [sb(f"slot_base{u}", [P, TOP_K * CT]) for u in range(2)]
        M = [sb(f"chosen{u}", [P, CT, E], BF16) for u in range(2)]
        CARRY = [sb(f"carry{u}", [P, E], BF16) for u in range(2)]
        MS = sb("chosen_sum", [P, E])
        PK = sb("pos", [P, TOP_K * CT])
        POS = sb("onehot_pos", [P, TOP_K * CT, E])
        OVER = sb("over", [P, TOP_K * CT])
        SLOT = sb("slot", [P, TOP_K * CT])
        SCI = [sb(f"scatter_ix{u}", [P, TOP_K * CT], U32) for u in range(2)]
        GIX = sb("gather_ix_all", [P, NCH, TOP_K * CT], U32)
        GS = sb("gather_ix", [P, 4, TOP_K], U32)
        VALID = sb("valid", [P, NCH, TOP_K * CT])
        GAP = sb("gap", [P, NCH, CT])
        CW = sb("combine_w", [P, NCH, TOP_K * CT])
        G = sb("gathered", [P, 4, TOP_K, D])
        raw_wu = sb("raw_wu", [P, KD, UPW])
        raw_wd = sb("raw_wd", [P, 2, D])
        WU = Split(ctx, nc, tag + "ex_up", [P, KD, UPW])
        WD = Split(ctx, nc, tag + "ex_down", [P, 2, D])
        XE = sb("ex_rows", [P, ST, D])
        XET = Split(ctx, nc, tag + "ex_xT", [P, KD, CAP])
        OE = sb("ex_out", [P, ST, D])

        s_const = sem("const")
        s_x = sem("x")
        s_wr = sem("w_router")
        s_wu_raw, s_wd_raw = sem("sh_up_raw"), sem("sh_down_raw")
        s_fill = sem("fill")
        s_rt = sem("router_split")
        s_su_hi, s_su_lo = sem("sh_up_hi"), sem("sh_up_lo")
        s_sd_hi, s_sd_lo = sem("sh_down_hi"), sem("sh_down_lo")
        s_ltp, s_lt, s_lgp = sem("logitsT_psum"), sem("logitsT"), sem("logits_psum")
        s_rank, s_chosen = sem("rank"), sem("chosen")
        s_carry = sem("carry")
        s_pos, s_slot = sem("pos_psum"), sem("slot")
        s_scat = [sem(f"scatter{u}") for u in range(2)]
        s_up = sem("up_psum")
        s_sg, s_prod, s_hhi, s_hlo = sem("silu"), sem("prod"), sem("h_hi"), sem("h_lo")
        s_dn, s_y = sem("down_psum"), sem("y")
        s_ex_pad = sem("ex_pad")
        s_ewu, s_ewd, s_xe = sem("ex_wu_raw"), sem("ex_wd_raw"), sem("ex_rows")
        s_ewu_hi, s_ewu_lo, s_ewd_hi, s_ewd_lo = sem("ex_wu_hi"), sem("ex_wu_lo"), sem("ex_wd_hi"), sem("ex_wd_lo")
        s_etp, s_ext_hi, s_ext_lo = sem("ex_xT_psum"), sem("ex_xT_hi"), sem("ex_xT_lo")
        s_eup = sem("ex_up_psum")
        s_esg, s_eprod, s_ehhi, s_ehlo = sem("ex_silu"), sem("ex_prod"), sem("ex_h_hi"), sem("ex_h_lo")
        s_edn, s_eo = sem("ex_down_psum"), sem("ex_out")
        s_ybuf = sem("ybuf")
        s_oe_free, s_xn_free = sem("oe_free"), sem("xn_free")
        s_exp, s_cw = sem("gap_exp"), sem("combine_w")
        s_gix = sem("gather_ix")
        s_gat = [sem(f"gather{s}") for s in range(4)]
        s_comb = sem("combined")
        s_out = sem("out")

        bank = lambda b, n=CHUNK, p=P: ps[0:p, b * CHUNK:b * CHUNK + n]
        EH = [[m[:, i * CAP:(i + 1) * CAP] for i in range(2)] for m in (H.hi, H.lo)]
        hcols = lambda q: slice(q * CHUNK, (q + 1) * CHUNK)
        jrows = lambda q: P if q < JF else JR
        TG = [(0, 2), (2, 2), (4, 1)]
        assert ST == 5

        def pe_up(pe, n, c):
            for q in range(NJ):
                pe.wait_ge(s_prod, 1 + NJ * n + max(q - 1, 0))
                tiles = [(q * 2 * P, P, 2 * (q % 2)), (q * 2 * P + P, P, 2 * (q % 2) + 1)] if q < JF else \
                        [(q * 2 * P, 2 * JR, 2 * (q % 2))]
                for col, m, b in tiles:
                    for k in range(KD):
                        ins = matmul3(nc, bank(b, p=m), pair(SU, slice(None), k, slice(col, col + m)),
                                      pair(XT, slice(None), k, bass.ds(c * CHUNK, CHUNK)),
                                      k == 0, k == KD - 1)
                    ins.then_inc(s_up, 1)

        def act_silu(act, n):
            for q in range(NJ):
                act.wait_ge(s_up, UPS * n + 2 * q + 1)
                act.wait_ge(s_prod, 1 + NJ * n + max(q - 1, 0))
                m = jrows(q)
                nc.scalar.activation(SG[0:m, q % 2, :], bank(2 * (q % 2), p=m), ACT.Silu).then_inc(s_sg, 1)

        def dve_prod(dve, n, q):
            dve.wait_ge(s_sg, NJ * n + q + 1)
            dve.wait_ge(s_up, UPS * n + min(2 * q + 2, UPS))
            dve.wait_ge(s_hhi, 1 + NJ * n + max(q - 1, 0))
            dve.wait_ge(s_hlo, 1 + NJ * n + max(q - 1, 0))
            b = 2 * (q % 2)
            up = ps[0:P, (b + 1) * CHUNK:(b + 2) * CHUNK] if q < JF else ps[JR:2 * JR, b * CHUNK:(b + 1) * CHUNK]
            m = jrows(q)
            nc.vector.tensor_tensor(HF[0:m, q % 2, :], SG[0:m, q % 2, :], up, ALU.mult).then_inc(s_prod, 1)

        def pool_hhi(pool, n, q):
            if q == 0:
                pool.wait_ge(s_dn, 1 + CT * n)
            hold(pool, s_prod, 1 + NJ * n + q + 1)
            m = jrows(q)
            nc.gpsimd.tensor_copy(H.hi[0:m, hcols(q)], HF[0:m, q % 2, :]).then_inc(s_hhi, 1)

        def dve_hlo(dve, n, q):
            dve.wait_ge(s_hhi, 1 + NJ * n + q + 1)
            m = jrows(q)
            sub_rounded(nc.vector, H.lo[0:m, hcols(q)], HF[0:m, q % 2, :],
                        H.hi[0:m, hcols(q)]).then_inc(s_hlo, 1)

        def pe_down(pe, n):
            pe.wait_ge(s_hlo, 1 + NJ * (n + 1))
            pe.wait_ge(s_hhi, 1 + NJ * (n + 1))
            for a in range(CT):
                pe.wait_ge(s_y, 1 + CT * n + max(a - 1, 0))
                o = bank(4 + a % 2, D)
                for q in range(NJ):
                    m = jrows(q)
                    cols = slice(q * CHUNK + a * P, q * CHUNK + (a + 1) * P)
                    ins = matmul3(nc, o, pair(H, slice(0, m), cols), pair(SD, slice(0, m), q),
                                  q == 0, q == NJ - 1)
                ins.then_inc(s_dn, 1)

        def dve_y(dve, n, c):
            for a in range(CT):
                dve.wait_ge(s_dn, 1 + CT * n + a + 1)
                x = X[:, bass.ds(c * CT + a, 1), :]
                nc.vector.scalar_tensor_tensor(out=x, in0=bank(4 + a % 2, D),
                                               scalar=0.5, in1=x, op0=ALU.mult, op1=ALU.add).then_inc(s_y, 1)

        block = ctx.enter_context(nc.Block())

        @block.sync
        def _(sp):
            open_at_one(sp, s_oe_free)
            if x_in is not None:
                for c in range(NCH):
                    sp.dma_start(X[:, c * CT:(c + 1) * CT, :],
                                 x_in[c * CHUNK:(c + 1) * CHUNK, :].rearrange("(a p) d -> p a d", p=P)).then_inc(s_x, 16)
                    sp.wait_ge(s_x, 16 * (c + 1))
            sp.dma_start(raw_r[:], w["router"].rearrange("(k p) e -> p k e", p=P)).then_inc(s_wr, 16)
            for k in range(KD):
                for z in range(2):
                    src = w["shared_w_up_gate"][k * P:(k + 1) * P, z * J:(z + 1) * J]
                    sp.dma_start(raw_up[:, k, 0:2 * P * JF].rearrange("p (j z n) -> p j z n", z=2, n=P)[:, :, z, :],
                                 src[:, 0:P * JF].rearrange("p (j n) -> p j n", n=P)).then_inc(s_wu_raw, 16)
                    sp.dma_start(raw_up[:, k, 2 * P * JF + z * JR:2 * P * JF + (z + 1) * JR],
                                 src[:, P * JF:J]).then_inc(s_wu_raw, 16)
            sp.dma_start(raw_dn[:, 0:JF, :], w["shared_w_down"][0:JF * P, :].rearrange("(j p) d -> p j d", p=P)
                         ).then_inc(s_wd_raw, 16)
            sp.dma_start(raw_dn[0:JR, JF, :], w["shared_w_down"][JF * P:J, :]).then_inc(s_wd_raw, 16)
            if fill_xbuf:
                sp.wait_ge(s_const, 1)
                rows = E * CAP // P
                half = rows // 2
                for z in range(2):
                    sp.dma_start(xbuf[z * half * P:(z + 1) * half * P, :].rearrange("(p r) d -> p r d", p=P),
                                 C.zeros[:, None, :].broadcast_to([P, half, D])).then_inc(s_fill, 16)

            def load_up(e):
                src = w["w_up_gate"][bass.ds(e, 1), :, :].rearrange("a (k p) n -> p (a k) n", p=P)
                for dst, at, n in ((0, 0, P), (P, I, P), (2 * P, P, IR), (2 * P + 64, I + P, IR)):
                    sp.dma_start(raw_wu[:, :, dst:dst + n], src[:, :, at:at + n]).then_inc(s_ewu, 16)

            def load_down(e):
                src = w["w_down"][bass.ds(e, 1), :, :].rearrange("a i d -> (a i) d")
                sp.dma_start(raw_wd[:, 0, :], src[0:P, :]).then_inc(s_ewd, 16)
                sp.dma_start(raw_wd[0:IR, 1, :], src[P:I, :]).then_inc(s_ewd, 16)

            def load_rows(e):
                sp.dma_start(XE[:], xbuf[bass.ds(e * CAP, CAP), :].rearrange("(s p) d -> p s d", p=P)).then_inc(s_xe, 16)

            def store_rows(e):
                sp.wait_ge(s_eo, 1 + ST * (e + 1))
                sp.dma_start(ybuf[bass.ds(e * CAP, CAP), :].rearrange("(s p) d -> p s d", p=P), OE[:]).then_inc(s_ybuf, 16)
                sp.wait_ge(s_ybuf, 16 * (e + 1))
                sp.nop().then_inc(s_oe_free, 1)

            sp.wait_ge(s_ex_pad, 2)
            load_up(0)
            load_down(0)
            for u in range(2):
                sp.wait_ge(s_scat[u], 16 * TOP_K * CT * NCH // 2)
            load_rows(0)
            with sp.Fori(0, E - 1) as e:
                sp.wait_ge(s_ewu_hi, e + 1)
                sp.wait_ge(s_ewu_lo, e + 1)
                load_up(e + 1)
                sp.wait_ge(s_etp, 3 * e + 3)
                load_rows(e + 1)
                sp.wait_ge(s_ewd_hi, e + 1)
                sp.wait_ge(s_ewd_lo, e + 1)
                load_down(e + 1)
                store_rows(e)
            store_rows(E - 1)
            if out is not None:
                dst = out.rearrange("(c p) d -> p c d", p=P)
                half = NT // 2
                sp.wait_ge(s_comb, 1 + 2 * half)
                sp.dma_start(dst[:, 0:half, :], X[:, 0:half, :]).then_inc(s_out, 16)
                sp.wait_ge(s_comb, 1 + 2 * NT)
                for a in range(NT - half):
                    sp.wait_ge(s_y, 1 + CT * (NCH // 2) + a + 1)
                    sp.dma_start(dst[:, half + a:half + a + 1, :], X[:, half + a:half + a + 1, :]).then_inc(s_out, 16)
                sp.wait_ge(s_out, 16 * (1 + NT - half))

        @block.gpsimd
        def _(pool):
            open_at_one(pool, s_hhi, s_ehhi, s_xn_free)
            if fill_xbuf:
                C.build(pool, s_const)
                pool.wait_ge(s_const, 3)
            nc.gpsimd.memset(raw_wu[:, :, 2 * P:UPW], 0.0).then_inc(s_ex_pad, 1)
            nc.gpsimd.memset(raw_wd[:, 1, :], 0.0).then_inc(s_ex_pad, 1)
            with pool.Fori(0, NCH // 2) as i:
                for u in range(2):
                    ln.pool(nc.gpsimd, C, 2 * i + u)
                for q in range(NJ):
                    pool_hhi(pool, i, q)
                if fill_xbuf:
                    pool.wait_ge(s_fill, 32)
                for u in range(2):
                    hold(pool, s_slot, 1 + 5 * (2 * i + u) + 5)
                    for k in range(TOP_K):
                        for a in range(CT):
                            z = k * CT + a
                            nc.gpsimd.indirect_dma_start(
                                out=xbuf, out_offset=bass.IndirectOffsetOnAxis(ap=SCI[u][:, z:z + 1], axis=0),
                                in_=ln.xn[u][:, a, :], in_offset=None,
                                bounds_check=E * CAP - 1, oob_is_err=False).then_inc(s_scat[u], 16)
                for u in range(2):
                    pool.wait_ge(s_scat[u], 16 * TOP_K * CT * (i + 1))
                pool.nop().then_inc(s_xn_free, 1)

            def expert(e):
                for z in range(4):
                    m = P if z % 2 == 0 else IR
                    if z == 0:
                        pool.wait_ge(s_edn, 1 + ST * e)
                    hold(pool, s_eprod, 1 + 4 * e + z + 1)
                    cols = slice((z // 2) * HALF, (z // 2 + 1) * HALF)
                    nc.gpsimd.tensor_copy(EH[0][z % 2][0:m, cols], HF[0:m, z % 2, 0:HALF]).then_inc(s_ehhi, 1)

            pool.wait_ge(s_dn, 1 + CT * NCH // 2)
            with pool.Fori(0, E) as e:
                expert(e)
            pool.wait_ge(s_edn, 1 + ST * E)
            pool.wait_ge(s_ybuf, 16 * E)

            def gather(j, r):
                t = (NT // 2) * j + r
                s = r % 4
                hold(pool, s_comb, 1 + (2 * (NT // 2) * j if r < 4 else 2 * (t - 3)))
                c = (NCH // 2) * j + r // CT
                nc.gpsimd.tensor_copy(GS[:, s, :], GIX[:, bass.ds(c, 1), r % CT::CT]).then_inc(s_gix, 1)
                hold(pool, s_gix, t + 1)
                for k in range(TOP_K):
                    nc.gpsimd.indirect_dma_start(
                        out=G[:, s, k, :], out_offset=None, in_=ybuf,
                        in_offset=bass.IndirectOffsetOnAxis(ap=GS[:, s, k:k + 1], axis=0),
                        bounds_check=E * CAP - 1, oob_is_err=True).then_inc(s_gat[s], 16)

            with pool.Fori(0, NCH // 2) as j:
                for r in range(4):
                    gather(j, r)
                for q in range(NJ):
                    pool_hhi(pool, NCH // 2 + j, q)
                    if q in (2, 3):
                        gather(j, 2 * q)
                        gather(j, 2 * q + 1)

        @block.scalar
        def _(act):
            open_at_one(act, s_eo)

            def split_hi(dst, src):
                return nc.scalar.activation(dst, src, ACT.Copy)

            act.wait_ge(s_wu_raw, 16 * 4 * KD)
            for k in range(KD):
                split_hi(SU.hi[:, k, :], raw_up[:, k, :]).then_inc(s_su_hi, 1)
            act.wait_ge(s_wd_raw, 32)
            split_hi(SD.hi[:, 0:JF, :], raw_dn[:, 0:JF, :]).then_inc(s_sd_hi, 1)
            split_hi(SD.hi[0:JR, JF, :], raw_dn[0:JR, JF, :]).then_inc(s_sd_hi, 1)
            with act.Fori(0, NCH // 2) as i:
                for u in range(2):
                    ln.split_hi(nc, act, XT, ps, 2 * i + u, u)
                for u in range(2):
                    act.wait_ge(s_ltp, 2 * i + u + 1)
                    nc.scalar.activation(LT[:, u, :], bank(4 + u, p=64), ACT.Copy).then_inc(s_lt, 1)
                act_silu(act, i)
            act.wait_ge(s_slot, 1 + 5 * NCH)
            nc.scalar.activation(GAP[:], GAP[:], ACT.Exp).then_inc(s_exp, 1)

            def weights_up(e):
                act.wait_ge(s_ewu, 64 * (e + 1))
                act.wait_ge(s_eup, 1 + 6 * e)
                split_hi(WU.hi[:], raw_wu[:]).then_inc(s_ewu_hi, 1)

            def weights_down(e):
                act.wait_ge(s_ewd, 32 * (e + 1))
                act.wait_ge(s_edn, 1 + ST * e)
                split_hi(WD.hi[:], raw_wd[:]).then_inc(s_ewd_hi, 1)

            def rows(e):
                for g, (s0, ns) in enumerate(TG):
                    act.wait_ge(s_etp, 3 * e + g + 1)
                    src = bank(4 + g, ns * D).rearrange("p (s k t) -> p k s t", k=KD, t=P)
                    dst = XET.hi[:, :, s0 * P:(s0 + ns) * P].rearrange("p k (s t) -> p k s t", t=P)
                    split_hi(dst, src).then_inc(s_ext_hi, 1)

            def silus(e):
                for z in range(4):
                    m = P if z % 2 == 0 else IR
                    act.wait_ge(s_eup, 1 + 6 * e + (1, 3, 4, 6)[z])
                    act.wait_ge(s_eprod, 1 + 4 * e + max(z - 1, 0))
                    nc.scalar.activation(SG[0:m, z % 2, 0:HALF], bank((0, 2, 3, 1)[z], HALF, m), ACT.Silu).then_inc(s_esg, 1)

            def outs(e):
                act.wait_ge(s_oe_free, 1 + e)
                for s in range(ST):
                    act.wait_ge(s_edn, 1 + ST * e + s + 1)
                    nc.scalar.activation(OE[:, s, :], bank(7 - 4 * (s % 2), D), ACT.Copy).then_inc(s_eo, 1)

            weights_up(0)
            weights_down(0)
            rows(0)
            with act.Fori(0, E - 1) as e:
                silus(e)
                rows(e + 1)
                weights_up(e + 1)
                outs(e)
                weights_down(e + 1)
            silus(E - 1)
            outs(E - 1)
            with act.Fori(0, NCH // 2) as j:
                act_silu(act, NCH // 2 + j)

        @block.vector
        def _(dve):
            open_at_one(dve, s_prod, s_hlo, s_y, s_eprod, s_ehlo, s_ext_lo, s_carry, s_slot, s_comb)
            nc.vector.memset(RT[:].bitcast(F32), 0.0)
            for u in range(2):
                nc.vector.memset(CARRY[u][:], 0.0).then_inc(s_rt, 1)
            dve.wait_ge(s_rt, 2)
            dve.wait_ge(s_wr, 16)
            nc.vector.tensor_copy(RT[:, :, 0:E], raw_r[:]).then_inc(s_rt, 1)
            dve.wait_ge(s_rt, 3)
            sub_rounded(nc.vector, RT[:, :, 32:32 + E], raw_r[:], RT[:, :, 0:E]).then_inc(s_rt, 1)
            dve.wait_ge(s_su_hi, KD)
            for k in range(KD):
                sub_rounded(nc.vector, SU.lo[:, k, :], raw_up[:, k, :], SU.hi[:, k, :]).then_inc(s_su_lo, 1)
            dve.wait_ge(s_sd_hi, 2)
            sub_rounded(nc.vector, SD.lo[:, 0:JF, :], raw_dn[:, 0:JF, :], SD.hi[:, 0:JF, :]).then_inc(s_sd_lo, 1)
            sub_rounded(nc.vector, SD.lo[0:JR, JF, :], raw_dn[0:JR, JF, :], SD.hi[0:JR, JF, :]).then_inc(s_sd_lo, 1)
            if x_in is not None:
                dve.wait_ge(s_x, 16 * NCH)

            def rank(c, u):
                dve.wait_ge(s_lgp, c + 2 - u)
                lg = bank(6, CT * 2 * E).rearrange("p (v a e) -> p v a e", v=2, e=E)[:, u]
                nc.vector.tensor_copy(LG[:], lg).then_inc(s_rank, 1)
                hold(dve, s_rank, 6 * c + 1)
                for a in range(CT):
                    ins = nc.vector.max(TOP[:, a, :], LG[:, a, :])
                ins.then_inc(s_rank, 1)
                hold(dve, s_rank, 6 * c + 2)
                for a in range(CT):
                    ins = nc.vector.max_index(IX[:, a, :], TOP[:, a, :], LG[:, a, :])
                ins.then_inc(s_rank, 1)
                nc.vector.tensor_tensor(GAP[:, bass.ds(c, 1), :], TOP[:, :, 1], TOP[:, :, 0], ALU.subtract)
                dve.wait_ge(s_rank, 6 * c + 3)
                nc.vector.tensor_copy(IXF[:], IX[:, :, 0:TOP_K].rearrange("p a k -> p k a")).then_inc(s_rank, 1)
                dve.wait_ge(s_rank, 6 * c + 4)
                ixf = IXF[:].rearrange("p k a -> p (k a)")
                nc.vector.tensor_scalar(BASE[u][:], ixf, float(CAP), None, ALU.mult)
                nc.vector.tensor_tensor(OH[u][:], C.expert_id[:, None, :].broadcast_to([P, TOP_K * CT, E]),
                                        ixf[:, :, None].broadcast_to([P, TOP_K * CT, E]), ALU.is_equal).then_inc(s_rank, 1)
                dve.wait_ge(s_rank, 6 * c + 5)
                nc.vector.tensor_tensor(M[u][:], OH[u][:, 0:CT, :], OH[u][:, CT:2 * CT, :], ALU.add).then_inc(s_chosen, 1)
                dve.wait_ge(s_chosen, c + 1)
                nc.vector.tensor_reduce(MS[:], M[u][:].rearrange("p a e -> p e a"), AX_X, ALU.add).then_inc(s_rank, 1)

            def slots(c, u):
                dve.wait_ge(s_pos, 1 + c + 2 - u)
                pos = bank(7, 2 * CT * E).rearrange("p (v a e) -> p v a e", v=2, e=E)[:, u]
                nc.vector.tensor_tensor(POS[:].rearrange("p (k a) e -> p k a e", a=CT),
                                        OH[u][:].rearrange("p (k a) e -> p k a e", a=CT),
                                        pos[:, None, :, :].broadcast_to([P, TOP_K, CT, E]), ALU.mult).then_inc(s_slot, 1)
                dve.wait_ge(s_slot, 1 + 5 * c + 1)
                nc.vector.tensor_reduce(PK[:], POS[:], AX_X, ALU.add).then_inc(s_slot, 1)
                dve.wait_ge(s_slot, 1 + 5 * c + 2)
                nc.vector.tensor_scalar(OVER[:], PK[:], float(CAP), float(NOSLOT), ALU.is_ge, ALU.mult)
                nc.vector.tensor_scalar(VALID[:, bass.ds(c, 1), :], PK[:], float(CAP), None, ALU.is_lt)
                nc.vector.scalar_tensor_tensor(out=SLOT[:], in0=PK[:], scalar=float(CAP - 1), in1=BASE[u][:],
                                               op0=ALU.min, op1=ALU.add).then_inc(s_slot, 1)
                dve.wait_ge(s_slot, 1 + 5 * c + 3)
                nc.vector.tensor_copy(GIX[:, bass.ds(c, 1), :], SLOT[:]).then_inc(s_slot, 1)
                nc.vector.tensor_tensor(SCI[u][:], SLOT[:], OVER[:], ALU.add).then_inc(s_slot, 1)

            with dve.Fori(0, NCH // 2) as i:
                for u in range(2):
                    dve.wait_ge(s_xn_free, 1 + i)
                    dve.wait_ge(ln.s_tp, 1 + 4 * i)
                    ln.vector(nc.vector, X, 2 * i + u, u)
                for u in range(2):
                    ln.split_lo(nc, dve, XT, ps, 2 * i + u, u)
                for u in range(2):
                    rank(2 * i + u, u)
                    if u == 0:
                        dve.wait_ge(s_rank, 6 * (2 * i) + 6)
                        dve.wait_ge(s_pos, 1 + 2 * i)
                        nc.vector.tensor_tensor(CARRY[1][:], CARRY[0][:], MS[:], ALU.add).then_inc(s_carry, 1)
                for q in range(NJ):
                    dve_prod(dve, i, q)
                    if q:
                        dve_hlo(dve, i, q - 1)
                dve_hlo(dve, i, NJ - 1)
                for u in range(2):
                    slots(2 * i + u, u)
                nc.vector.tensor_tensor(CARRY[0][:], CARRY[1][:], MS[:], ALU.add).then_inc(s_carry, 1)
                dve_y(dve, i, i)

            gap = GAP[:].rearrange("p c a -> p (c a)")
            inv = LG[:].rearrange("p a e -> p (a e)")[:, 0:NT]
            dve.wait_ge(s_exp, 1)
            nc.vector.tensor_scalar(inv, gap, 1.0, None, ALU.add).then_inc(s_cw, 1)
            dve.wait_ge(s_cw, 1)
            nc.vector.reciprocal(inv, inv).then_inc(s_cw, 1)
            dve.wait_ge(s_cw, 2)
            inv_c = inv.rearrange("p (c a) -> p c a", a=CT)
            nc.vector.scalar_tensor_tensor(out=CW[:, :, 0:CT], in0=inv_c, scalar=0.5, in1=VALID[:, :, 0:CT],
                                           op0=ALU.mult, op1=ALU.mult)
            nc.vector.tensor_tensor(gap, gap, inv, ALU.mult).then_inc(s_cw, 1)
            dve.wait_ge(s_cw, 3)
            nc.vector.scalar_tensor_tensor(out=CW[:, :, CT:2 * CT], in0=GAP[:], scalar=0.5, in1=VALID[:, :, CT:2 * CT],
                                           op0=ALU.mult, op1=ALU.mult).then_inc(s_cw, 1)

            def weights_up(e):
                dve.wait_ge(s_ewu_hi, e + 1)
                sub_rounded(nc.vector, WU.lo[:], raw_wu[:], WU.hi[:]).then_inc(s_ewu_lo, 1)

            def weights_down(e):
                dve.wait_ge(s_ewd_hi, e + 1)
                sub_rounded(nc.vector, WD.lo[:], raw_wd[:], WD.hi[:]).then_inc(s_ewd_lo, 1)

            def rows(e):
                for g, (s0, ns) in enumerate(TG):
                    dve.wait_ge(s_ext_hi, 3 * e + g + 1)
                    for k in range(KD):
                        src = bank(4 + g, ns * D).rearrange("p (s k t) -> p k s t", k=KD, t=P)[:, k]
                        cols = slice(s0 * P, (s0 + ns) * P)
                        hi = XET.hi[:, k, cols].rearrange("p (s t) -> p s t", t=P)
                        ins = sub_rounded(nc.vector, XET.lo[:, k, cols].rearrange("p (s t) -> p s t", t=P), src, hi)
                    ins.then_inc(s_ext_lo, 1)

            def prod(e, z):
                m = P if z % 2 == 0 else IR
                dve.wait_ge(s_esg, 4 * e + z + 1)
                dve.wait_ge(s_eup, 1 + 6 * e + (2, 3, 5, 6)[z])
                dve.wait_ge(s_ehhi, 1 + 4 * e + max(z - 1, 0))
                dve.wait_ge(s_ehlo, 1 + 4 * e + max(z - 1, 0))
                b, p0 = ((1, 0), (2, 64), (0, 0), (1, 64))[z]
                nc.vector.tensor_tensor(HF[0:m, z % 2, 0:HALF], SG[0:m, z % 2, 0:HALF],
                                        ps[p0:p0 + m, b * CHUNK:b * CHUNK + HALF], ALU.mult).then_inc(s_eprod, 1)

            def h_lo(e, z):
                m = P if z % 2 == 0 else IR
                cols = slice((z // 2) * HALF, (z // 2 + 1) * HALF)
                dve.wait_ge(s_ehhi, 1 + 4 * e + z + 1)
                sub_rounded(nc.vector, EH[1][z % 2][0:m, cols], HF[0:m, z % 2, 0:HALF],
                            EH[0][z % 2][0:m, cols]).then_inc(s_ehlo, 1)

            def hidden(e):
                for z in range(4):
                    prod(e, z)
                    if z:
                        h_lo(e, z - 1)
                h_lo(e, 3)

            weights_up(0)
            weights_down(0)
            rows(0)
            with dve.Fori(0, E - 1) as e:
                hidden(e)
                rows(e + 1)
                weights_up(e + 1)
                weights_down(e + 1)
            hidden(E - 1)

            def combine(j, r):
                t, s = (NT // 2) * j + r, r % 4
                c = (NCH // 2) * j + r // CT
                x = X[:, bass.ds(t, 1), :]
                dve.wait_ge(s_gat[s], 32 * (2 * j + r // 4 + 1))
                dve.wait_ge(s_y, 1 + CT * (NCH // 2 + j))
                for k in range(TOP_K):
                    dve.wait_ge(s_comb, 1 + 2 * t + k)
                    nc.vector.scalar_tensor_tensor(out=x, in0=G[:, s, k, :], scalar=CW[:, bass.ds(c, 1), k * CT + r % CT],
                                                   in1=x, op0=ALU.mult, op1=ALU.add).then_inc(s_comb, 1)

            with dve.Fori(0, NCH // 2) as j:
                n = NCH // 2 + j
                for q in range(NJ):
                    dve_prod(dve, n, q)
                    if q:
                        dve_hlo(dve, n, q - 1)
                    if q >= 2:
                        combine(j, 2 * (q - 2))
                        combine(j, 2 * (q - 2) + 1)
                dve_hlo(dve, n, NJ - 1)
                dve.wait_ge(s_comb, 1 + NT * (j + 1))
                dve_y(dve, n, n)

        @block.tensor
        def _(pe):
            open_at_one(pe, s_dn, s_edn, s_eup, s_pos, ln.s_tp)
            pe.wait_ge(s_rt, 4)
            if fill_xbuf:
                pe.wait_ge(s_const, 3)
            with pe.Fori(0, NCH // 2) as i:
                pe.wait_ge(s_y, 1 + CT * i)
                ln.transpose(nc, pe, C, ps, 2 * i, 0)
                pe.wait_ge(s_slot, 1 + 5 * 2 * i)
                ln.transpose(nc, pe, C, ps, 2 * i + 1, 1)
                for u in range(2):
                    c = 2 * i + u
                    pe.wait_ge(ln.s_lo, 2 * c + 2)
                    for k in range(KD):
                        for z, m in enumerate((XT.hi, XT.lo)):
                            ins = nc.tensor.matmul(bank(4 + u, p=64), RT[:, k, :], m[:, k, bass.ds(c * CHUNK, CHUNK)],
                                                   start=(k == 0 and z == 0), stop=(k == KD - 1 and z == 1))
                    ins.then_inc(s_ltp, 1)
                for u in range(2):
                    pe.wait_ge(s_lt, 2 * i + u + 1)
                    for a in range(CT):
                        at = 6 * CHUNK + (u * CT + a) * E
                        ins = nc.tensor.matmul(ps[:, at:at + E], LT[:, u, a * P:(a + 1) * P], C.fold[:], start=True, stop=True)
                    ins.then_inc(s_lgp, 1)
                pe.wait_ge(s_su_lo, KD)
                pe_up(pe, i, i)
                for u in range(2):
                    c = 2 * i + u
                    pe.wait_ge(s_chosen, c + 1)
                    pe.wait_ge(s_carry, 1 + c)
                    for a in range(CT):
                        at = 7 * CHUNK + (u * CT + a) * E
                        o = ps[:, at:at + E]
                        nc.tensor.matmul(o, C.before[:], M[u][:, a, :], start=True, stop=False)
                        for b in range(a):
                            nc.tensor.matmul(o, C.ones[:], M[u][:, b, :], start=False, stop=False)
                        ins = nc.tensor.matmul(o, C.ones[:], CARRY[u][:], start=False, stop=True)
                    ins.then_inc(s_pos, 1)
                pe.wait_ge(s_sd_lo, 2)
                pe_down(pe, i)

            def transposes(e):
                pe.wait_ge(s_xe, 16 * (e + 1))
                pe.wait_ge(s_ext_lo, 1 + 3 * e)
                for g, (s0, ns) in enumerate(TG):
                    for s in range(ns):
                        for k in range(KD):
                            at = (4 + g) * CHUNK + s * D + k * P
                            ins = nc.tensor.transpose(ps[:, at:at + P], XE[:, s0 + s, k * P:(k + 1) * P], C.ident[:])
                    ins.then_inc(s_etp, 1)

            def up(e):
                pe.wait_ge(s_ewu_lo, e + 1)
                pe.wait_ge(s_ext_lo, 1 + 3 * e + 3)
                for z, (col, m, b) in enumerate([(0, P, 0), (P, P, 1), (2 * P, 64 + IR, 2),
                                                 (0, P, 3), (P, P, 0), (2 * P, 64 + IR, 1)]):
                    h = z // 3
                    pe.wait_ge(s_eprod, 1 + 4 * e + (1 if z >= 4 else 0))
                    if z == 3:
                        pe.wait_ge(s_eo, 1 + ST * e)
                    for k in range(KD):
                        ins = matmul3(nc, bank(b, HALF, m), pair(WU, slice(None), k, slice(col, col + m)),
                                      pair(XET, slice(None), k, slice(h * HALF, (h + 1) * HALF)), k == 0, k == KD - 1)
                    ins.then_inc(s_eup, 1)

            def down(e):
                pe.wait_ge(s_ewd_lo, e + 1)
                pe.wait_ge(s_ehlo, 1 + 4 * e + 4)
                for s in range(ST):
                    pe.wait_ge(s_eo, 1 + ST * e + max(s - 1, 0))
                    o = bank(7 - 4 * (s % 2), D)
                    for i, m in enumerate((P, IR)):
                        ins = matmul3(nc, o, (EH[0][i][0:m, s * P:(s + 1) * P], EH[1][i][0:m, s * P:(s + 1) * P]),
                                      pair(WD, slice(0, m), i), i == 0, i == 1)
                    ins.then_inc(s_edn, 1)

            pe.wait_ge(s_lt, NCH)
            pe.wait_ge(s_slot, 1 + 5 * NCH)
            pe.wait_ge(s_y, 1 + CT * NCH // 2)
            transposes(0)
            with pe.Fori(0, E - 1) as e:
                up(e)
                transposes(e + 1)
                down(e)
            up(E - 1)
            down(E - 1)
            pe.wait_ge(s_eo, 1 + ST * E)
            with pe.Fori(0, NCH // 2) as j:
                pe_up(pe, NCH // 2 + j, NCH // 2 + j)
                pe_down(pe, NCH // 2 + j)


def attention_block(sems, nc, tag, ps, C, X, io):
    T, D = X.shape[1] * P, X.shape[2]
    HD = io["L0_attn_Wq"].shape[1]
    NB, S = io["L0_attn_x"].shape[0:2]
    NH = HD // D_HEAD
    KD = D // P
    HG = 4
    NG = NH // HG
    NPAIR = NB // 2
    NIT = NG * NPAIR
    GW = HG * D_HEAD
    NCH = T // CHUNK
    SCALE = 1.0 / float(D_HEAD) ** 0.5
    assert 2 * S == CHUNK == GW and S == 2 * P and KD == 2 and NCH == NPAIR and D == 2 * P

    with ExitStack() as ctx:
        sb = lambda name, shape, dt=F32: ctx.enter_context(nc.sbuf_tensor(tag + name, shape, dt))
        sem = lambda name: sems.new(tag + name)
        ln = LayerNorm(ctx, sems, nc, tag, D)
        XT = Split(ctx, nc, tag + "xT", [P, KD, T])
        XV = Split(ctx, nc, tag + "xT_pair", [P, KD, CHUNK])
        RK = sb("raw_k", [P, HG, KD, D_HEAD])
        RV = sb("raw_v", [P, KD, GW])
        RO = sb("raw_o", [P, HG, D])
        RQ = sb("raw_q", [P, 2, KD, CHUNK])
        WQ = Split(ctx, nc, tag + "wq", [P, KD, HD])
        WK = Split(ctx, nc, tag + "wk", [P, HG, KD, D_HEAD])
        WV = Split(ctx, nc, tag + "wv", [P, KD, GW])
        WO = Split(ctx, nc, tag + "wo", [P, HG, D])
        BIAS = sb("bias", [P, 3, NH])
        BROW = sb("bias_rows", [3 * NH, P])
        BO = sb("bo", [P, D])
        Q = Split(ctx, nc, tag + "q", [P, 2, HG * S])
        QF = sb("q_full", [P, 2, CHUNK])
        K = Split(ctx, nc, tag + "k", [P, CHUNK])
        V = Split(ctx, nc, tag + "v", [P, CT, GW])
        PR = sb("weights", [P, 2, 2, 3 * P])
        PT = Split(ctx, nc, tag + "weightsT", [P, 2, 3 * P])
        O = Split(ctx, nc, tag + "headT", [P, CHUNK])
        MX = sb("max", [P, 2, 3])
        NM = sb("neg_max", [P, 2, 2])
        SUM = sb("sum", [P, 2, 2])
        RS = sb("rsum", [P, 2, 2, 2])

        s_bias, s_bt, s_bcol = sem("bias_in"), sem("biasT_psum"), sem("bias_cols")
        s_rk = [sem(f"raw_k_in{j}") for j in range(HG)]
        s_wq_in = [sem(f"wq_in{u}") for u in range(2)]
        s_wq_hi, s_wq_lo = sem("wq_hi"), sem("wq_lo")
        s_rv, s_ro = sem("raw_v_in"), sem("raw_o_in")
        s_wk, s_wv, s_wo = sem("wk"), sem("wv"), sem("wo")
        s_bo = sem("bo_added")
        s_xv = sem("xv_in")
        s_sc = sem("scores")
        s_mx, s_nm = sem("max"), sem("neg_max")
        s_exp = sem("exp")
        s_rs = sem("rsum")
        s_norm = sem("norm")
        s_pt = sem("weightsT_psum")
        s_pt_hi, s_pt_lo = sem("weightsT_hi"), sem("weightsT_lo")
        s_pr, s_pr_hi, s_pr_lo = sem("proj_psum"), sem("proj_hi"), sem("proj_lo")
        s_qf = sem("q_full")
        s_eh = sem("out_steps")
        s_ya = sem("y_added")

        bank = lambda b, n=CHUNK: ps[:, b * CHUNK:b * CHUNK + n]
        SB, TB, YB, PB = (0, 1), (2, 3), 4, 6
        QB = HD // D_HEAD
        QT = S // QB
        NQ = QB * 2 * HG * QT // CHUNK
        QC = QB // NQ
        NPR = 2 * HG + CT + NQ
        assert NPR % 2 == 0 and HG == CT == NQ == 4

        def key_tile(it, j, first=False):
            return NQ + NPR * it + (0, 2 + CT, 4 + CT, 6 + CT)[j] + (first and j == 0)

        def query_tile(it):
            return 1 if isinstance(it, int) and it == 0 else NPR * it - 1

        def head_tile(it, j, last=False):
            return NQ + NPR * it + (1, 3 + CT, 5 + CT, 7 + CT + NQ)[j] - ((1 + NQ) * (last and j == HG - 1))

        def value_tile(it):
            return NQ + NPR * it + 2

        bank_of = lambda m: PB + m % 2
        q_full = lambda r: QF[:, r % 2, :].rearrange("p (c b i) -> p c b i", c=QC, b=2)
        q_cols = lambda q, r: q[:].rearrange("p b (i c) -> p c b i", c=QB)[:, r * QC:(r + 1) * QC]

        block = ctx.enter_context(nc.Block())

        @block.sync
        def _(sp):
            def load_k(g, j):
                sp.dma_start(RK[:, j, :, :], io["L0_attn_Wk"][:, bass.ds(g * GW + j * D_HEAD, D_HEAD)]
                             .rearrange("(k p) n -> p k n", p=P)).then_inc(s_rk[j], 16)

            def load_v(g):
                sp.dma_start(RV[:], io["L0_attn_Wv"][:, bass.ds(g * GW, GW)]
                             .rearrange("(k p) n -> p k n", p=P)).then_inc(s_rv, 16)

            def load_o(g):
                sp.dma_start(RO[:], io["L0_attn_Wo"][bass.ds(g * GW, GW), :]
                             .rearrange("(h p) n -> p h n", p=P)).then_inc(s_ro, 16)

            def load_pair(p):
                cols = bass.ds(p * CHUNK, CHUNK)
                for to, at in ((XV.hi, XT.hi), (XV.lo, XT.lo)):
                    sp.dma_start(to[:].bitcast(F32), at[:, :, cols].bitcast(F32)).then_inc(s_xv, 16)

            def load_q(r):
                sp.dma_start(RQ[:, r % 2, :, :], io["L0_attn_Wq"][:, r * QC * P:(r + 1) * QC * P]
                             .rearrange("(k p) n -> p k n", p=P)).then_inc(s_wq_in[r % 2], 16)

            load_q(0)
            load_q(1)
            for j in range(HG):
                load_k(0, j)
            load_v(0)
            load_o(0)
            for z, name in enumerate(("L0_attn_bq", "L0_attn_bk", "L0_attn_bv")):
                sp.dma_start(BROW[z * NH:(z + 1) * NH, :], io[name].rearrange("(h p) -> h p", p=P)).then_inc(s_bias, 16)
            sp.dma_start(BO[:], io["L0_attn_bo"][None, :].broadcast_to([P, D])).then_inc(s_bias, 16)
            for r in range(2, NQ):
                sp.wait_ge(s_wq_lo, r - 1)
                load_q(r)
            sp.wait_ge(ln.s_lo, 2)
            sp.wait_ge(ln.s_hi, 2)
            load_pair(0)

            def pairs(g, n):
                with sp.Fori(0, n) as p:
                    sp.wait_ge(s_pr, value_tile(NPAIR * g + p) + CT)
                    sp.wait_ge(ln.s_lo, 2 * NCH)
                    load_pair((p + 1) % NPAIR)

            with sp.Fori(0, NG - 1) as g:
                sp.wait_ge(s_wk, 2 * HG * (g + 1))
                for j in range(HG):
                    load_k(g + 1, j)
                sp.wait_ge(s_wv, 2 * (g + 1))
                load_v(g + 1)
                pairs(g, NPAIR)
                sp.wait_ge(s_wo, 2 * HG * (g + 1))
                load_o(g + 1)
            pairs(NG - 1, NPAIR - 1)
            sp.wait_ge(s_xv, 32 * NIT)

        @block.gpsimd
        def _(pool):
            def split(dst_hi, dst_lo, raw, sem, count):
                nc.gpsimd.tensor_copy(dst_hi, raw).then_inc(sem, 1)
                pool.wait_ge(sem, count + 1)
                sub_rounded(nc.gpsimd, dst_lo, raw, dst_hi).then_inc(sem, 1)

            def split_k(g, j):
                hold(pool, s_rk[j], 16 * (g + 1))
                split(WK.hi[:, j], WK.lo[:, j], RK[:, j], s_wk, 2 * (HG * g + j))

            def split_v(g):
                hold(pool, s_rv, 16 * (g + 1))
                split(WV.hi[:], WV.lo[:], RV[:], s_wv, 2 * g)

            def split_o(g, j):
                hold(pool, s_ro, 16 * (g + 1))
                split(WO.hi[:, j], WO.lo[:, j], RO[:, j], s_wo, 2 * (HG * g + j))

            def norms(n, u):
                for b in range(2):
                    hold(pool, s_rs, 2 * n + b + 1)
                    for t, cols in enumerate((slice(0, P), slice(P, 3 * P))):
                        nc.gpsimd.tensor_scalar(PR[:, u, b, cols], PR[:, u, b, cols], RS[:, u, b, t:t + 1], None,
                                                ALU.mult).then_inc(s_norm, 1)

            for i in range(NCH // 2):
                for u in range(2):
                    ln.pool(nc.gpsimd, C, 2 * i + u)
                if i == 0:
                    for j in range(HG):
                        split_k(0, j)
                    split_v(0)
                for u in range(2):
                    c = 2 * i + u
                    pool.wait_ge(s_bias, 64)
                    pool.wait_ge(ln.s_xn, c + 1)
                    x = X[:, c * CT:(c + 1) * CT, :]
                    nc.gpsimd.tensor_tensor(x, x, BO[:, None, :].broadcast_to([P, CT, D]), ALU.add).then_inc(s_bo, 1)
            split_o(0, 0)

            def group(g, last):
                n0 = HG * NPAIR * g
                for j in range(HG):
                    norms(n0 + j, j % 2)
                    if j:
                        pool.wait_ge(s_eh, HG + n0 + j - HG + 1)
                        split_o(g, j)
                with pool.Fori(1, NPAIR - 1) as p:
                    for j in range(HG):
                        norms(n0 + HG * p + j, j % 2)
                for j in range(HG):
                    n = n0 + HG * (NPAIR - 1) + j
                    norms(n, j % 2)
                    if not last:
                        split_k(g + 1, j)
                        if j == 1:
                            split_v(g + 1)
                        if j == HG - 1:
                            pool.wait_ge(s_eh, HG + n - 2)
                            split_o(g + 1, 0)

            with pool.Fori(0, NG - 1) as g:
                group(g, False)
            group(NG - 1, True)

        @block.scalar
        def _(act):
            for i in range(NCH // 2):
                for r in range(i * NQ // 2, (i + 1) * NQ // 2):
                    act.wait_ge(s_wq_in[r % 2], 16 * (r // 2 + 1))
                    cols = slice(r * QC * P, (r + 1) * QC * P)
                    nc.scalar.activation(WQ.hi[:, :, cols], RQ[:, r % 2, :, :], ACT.Copy).then_inc(s_wq_hi, 1)
                for u in range(2):
                    ln.split_hi(nc, act, XT, ps, 2 * i + u, u)
            act.wait_ge(s_bcol, 1)

            def weightsT(n):
                for b in range(2):
                    act.wait_ge(s_pt, 2 * n + b + 1)
                    nc.scalar.activation(PT.hi[:, b, :], bank(TB[b], 3 * P), ACT.Copy).then_inc(s_pt_hi, 1)

            def exps(n, u):
                if not (isinstance(n, int) and n < 2):
                    act.wait_ge(s_pt, 2 * n - 2)
                hold(act, s_nm, n + 1)
                for b in range(2):
                    for t, cols in enumerate((slice(0, P), slice(P, 3 * P))):
                        src = bank(SB[b], 3 * P)[:, cols]
                        nc.scalar.activation(PR[:, u, b, cols], src, ACT.Exp, bias=NM[:, b, t:t + 1], scale=SCALE,
                                             accum_out=SUM[:, b, t:t + 1]).then_inc(s_exp, 1)

            def keys(m, b, h):
                hold(act, s_pr, m + 1)
                nc.scalar.activation(K.hi[:], bank(b), ACT.Identity, bias=BIAS[:, 1, bass.ds(h, 1)]).then_inc(s_pr_hi, 1)

            def queries(it):
                for r in range(NQ):
                    act.wait_ge(s_qf, NQ * it + r + 1)
                    nc.scalar.activation(q_cols(Q.hi, r), q_full(r), ACT.Copy).then_inc(s_pr_hi, 1)

            def head(m, b, h):
                hold(act, s_pr, m + 1)
                nc.scalar.activation(O.hi[:], bank(b), ACT.Identity, bias=BIAS[:, 2, bass.ds(h, 1)]).then_inc(s_pr_hi, 1)

            def values(it):
                for a in range(CT):
                    act.wait_ge(s_pr, value_tile(it) + a + 1)
                    nc.scalar.activation(V.hi[:, a, :], bank(bank_of(value_tile(0) + a)), ACT.Copy).then_inc(s_pr_hi, 1)

            def steps(it, first, last):
                g = it // NPAIR
                for j in range(HG):
                    n = HG * it + j
                    if not (first and j == 0):
                        weightsT(n - 1)
                    exps(n, j % 2)
                    if not (last and j == HG - 1):
                        keys(key_tile(it, j, first), bank_of(key_tile(0, j, first)),
                             g * HG + j + 1 if j < HG - 1 else ((it + 1) // NPAIR) * HG)
                        if j == HG - 1:
                            queries(it + 1)
                    if not (first and j == 0):
                        head(head_tile(it, j, last), bank_of(head_tile(0, j, last)),
                             g * HG + j - 1 if j else ((it - 1) // NPAIR) * HG + HG - 1)
                    if j == 0:
                        values(it)

            keys(0, bank_of(0), 0)
            queries(0)
            steps(0, True, False)
            with act.Fori(1, NIT - 1) as it:
                steps(it, False, False)
            steps(NIT - 1, False, True)
            weightsT(HG * NIT - 1)
            m = head_tile(NIT - 1, HG - 1, True) + 1
            head(m, bank_of(m), NH - 1)

        @block.vector
        def _(dve):
            for i in range(NCH // 2):
                for u in range(2):
                    if i:
                        dve.wait_ge(ln.s_tp, 1 + 4 * i)
                    ln.vector(nc.vector, X, 2 * i + u, u)
                for u in range(2):
                    ln.split_lo(nc, dve, XT, ps, 2 * i + u, u)
                for r in range(i * NQ // 2, (i + 1) * NQ // 2):
                    cols = slice(r * QC * P, (r + 1) * QC * P)
                    dve.wait_ge(s_wq_hi, r + 1)
                    sub_rounded(nc.vector, WQ.lo[:, :, cols], RQ[:, r % 2, :, :],
                                WQ.hi[:, :, cols]).then_inc(s_wq_lo, 1)
            dve.wait_ge(s_bt, 1)
            nc.vector.tensor_copy(BIAS[:].rearrange("p z h -> p (z h)"), bank(TB[0], 3 * NH)).then_inc(s_bcol, 1)
            dve.wait_ge(s_bcol, 1)

            def weightsT(n):
                for b in range(2):
                    dve.wait_ge(s_pt_hi, 2 * n + b + 1)
                    sub_rounded(nc.vector, PT.lo[:, b, :], bank(TB[b], 3 * P), PT.hi[:, b, :]).then_inc(s_pt_lo, 1)

            def maxes(n):
                dve.wait_ge(s_sc, n + 1)
                nc.vector.tensor_reduce(MX[:], ps[:, 0:2 * CHUNK].rearrange("p (b n) -> p b n", b=2)[:, :, 0:3 * P]
                                        .rearrange("p b (t s) -> p b t s", s=P), AX_X, ALU.max).then_inc(s_mx, 1)
                dve.wait_ge(s_mx, 2 * n + 1)
                nc.vector.tensor_tensor(MX[:, :, 1], MX[:, :, 1], MX[:, :, 2], ALU.max).then_inc(s_mx, 1)
                dve.wait_ge(s_mx, 2 * n + 2)
                nc.vector.tensor_scalar(NM[:], MX[:, :, 0:2], -SCALE, None, ALU.mult).then_inc(s_nm, 1)

            def sums(n, u):
                for b in range(2):
                    dve.wait_ge(s_exp, 4 * n + 2 * b + 2)
                    nc.vector.reciprocal(RS[:, u, b, :], SUM[:, b, :]).then_inc(s_rs, 1)

            def biased_lo(m, lo, b, bias, hi):
                dve.wait_ge(s_pr_hi, m + 1)
                nc.vector.scalar_tensor_tensor(out=lo, in0=bank(b), scalar=bias, in1=hi.bitcast(F32),
                                               op0=ALU.add, op1=ALU.subtract).then_inc(s_pr_lo, 1)

            def query_bias(it, r):
                m = query_tile(it) + r
                dve.wait_ge(s_pr, m + 1)
                if not (isinstance(it, int) and it == 0 and r == 0):
                    dve.wait_ge(s_pr_lo, m - 1)
                nc.vector.tensor_tensor(QF[:, r % 2, :].rearrange("p (c t) -> p c t", c=QC),
                                        bank(bank_of(query_tile(0) + r)).rearrange("p (c t) -> p c t", c=QC),
                                        BIAS[:, 0, r * QC:(r + 1) * QC, None].broadcast_to([P, QC, CHUNK // QC]),
                                        ALU.add).then_inc(s_qf, 1)

            def queries(it):
                query_bias(it, 0)
                for r in range(NQ):
                    if r < NQ - 1:
                        query_bias(it, r + 1)
                    dve.wait_ge(s_pr_hi, query_tile(it) + r + 1)
                    sub_rounded(nc.vector, q_cols(Q.lo, r), q_full(r), q_cols(Q.hi, r)).then_inc(s_pr_lo, 1)

            def head(m, b, h):
                biased_lo(m, O.lo[:], b, BIAS[:, 2, bass.ds(h, 1)], O.hi[:])

            def values(it):
                for a in range(CT):
                    dve.wait_ge(s_pr_hi, value_tile(it) + a + 1)
                    sub_rounded(nc.vector, V.lo[:, a, :], bank(bank_of(value_tile(0) + a)), V.hi[:, a, :]).then_inc(s_pr_lo, 1)

            def add_y(it):
                if isinstance(it, int) and it == 0:
                    dve.wait_ge(s_bo, NCH)
                dve.wait_ge(s_eh, HG + HG * (it + 1))
                x = X[:, bass.ds((it % NPAIR) * CT, CT), :].rearrange("p c d -> p (c d)")
                nc.vector.tensor_tensor(x, x, ps[:, YB * CHUNK:(YB + 2) * CHUNK], ALU.add).then_inc(s_ya, 1)

            def keys(m, b, h):
                biased_lo(m, K.lo[:], b, BIAS[:, 1, bass.ds(h, 1)], K.hi[:])

            def steps(it, first, last):
                g = it // NPAIR
                for j in range(HG):
                    n = HG * it + j
                    maxes(n)
                    if not (first and j == 0):
                        weightsT(n - 1)
                    sums(n, j % 2)
                    if not (last and j == HG - 1):
                        keys(key_tile(it, j, first), bank_of(key_tile(0, j, first)),
                             g * HG + j + 1 if j < HG - 1 else ((it + 1) // NPAIR) * HG)
                        if j == HG - 1:
                            queries(it + 1)
                    if j == 1 and not first:
                        add_y(it - 1)
                    if not (first and j == 0):
                        head(head_tile(it, j, last), bank_of(head_tile(0, j, last)),
                             g * HG + j - 1 if j else ((it - 1) // NPAIR) * HG + HG - 1)
                    if j == 0:
                        values(it)

            keys(0, bank_of(0), 0)
            queries(0)
            steps(0, True, False)
            with dve.Fori(1, NIT - 1) as it:
                steps(it, False, False)
            steps(NIT - 1, False, True)
            weightsT(HG * NIT - 1)
            m = head_tile(NIT - 1, HG - 1, True) + 1
            head(m, bank_of(m), NH - 1)
            add_y(NIT - 1)

        @block.tensor
        def _(pe):
            open_at_one(pe, ln.s_tp, *[s_eh] * HG)
            pe.wait_ge(s_bias, 64)
            nc.tensor.transpose(bank(TB[0], 3 * NH), BROW[:], C.ident[0:3 * NH, 0:3 * NH]).then_inc(s_bt, 1)
            for i in range(NCH // 2):
                for u in range(2):
                    if i:
                        pe.wait_ge(ln.s_lo, 2 * (2 * i + u) - 2)
                    ln.transpose(nc, pe, C, ps, 2 * i + u, u)

            def scores(n, j, count):
                pe.wait_ge(s_pr_lo, count)
                if not (isinstance(n, int) and n == 0):
                    pe.wait_ge(s_exp, 4 * n)
                for b in range(2):
                    q = lambda t: pair(Q, slice(None), b, slice(j * S + t * P, j * S + (t + 1) * P))
                    k = lambda t: pair(K, slice(None), slice(b * S, b * S + (t + 1) * P))
                    for t in range(2):
                        at = SB[b] * CHUNK + t * P
                        o, width = ps[:, at:at + (t + 1) * P], (t + 1) * P
                        matmul3(nc, o, q(t), k(t), True, False)
                        ins = nc.tensor.matmul(o[:, width - P:width], C.ident_bf[:], C.causal[:], start=False, stop=True)
                ins.then_inc(s_sc, 1)

            def keys(m, b, j, p):
                if not (isinstance(m, int) and m == 0):
                    pe.wait_ge(s_pr_lo, m - 1)
                for k in range(KD):
                    ins = matmul3(nc, bank(b), pair(WK, slice(None), j, k),
                                  pair(XT, slice(None), k, bass.ds(p * CHUNK, CHUNK)), k == 0, k == KD - 1)
                ins.then_inc(s_pr, 1)

            def queries(it):
                m = query_tile(it)
                p, g = it % NPAIR, it // NPAIR
                xt = [a[:].rearrange("p k (q b g i) -> p k q b g i", q=NPAIR, b=2, g=NG) for a in (XT.hi, XT.lo)]
                for r in range(NQ):
                    if r >= 2:
                        pe.wait_ge(s_qf, NQ * it + r - 1)
                    elif not (isinstance(it, int) and it == 0 and r == 0):
                        pe.wait_ge(s_pr_lo, m + r - 1)
                    for c in range(QC):
                        o = bank(bank_of(query_tile(0) + r))[:, c * P:(c + 1) * P]
                        col = (r * QC + c) * P
                        for k in range(KD):
                            moving = tuple(a[:, k, bass.ds(p, 1), :, bass.ds(g, 1), :] for a in xt)
                            ins = matmul3(nc, o, pair(WQ, slice(None), k, slice(col, col + P)), moving,
                                          k == 0, k == KD - 1)
                    ins.then_inc(s_pr, 1)

            pe.wait_ge(s_bcol, 1)

            def head(n, j, m, b):
                pe.wait_ge(s_pt_lo, 2 * n + 2)
                pe.wait_ge(s_pr_lo, m - 1)
                for z in range(2):
                    v = lambda t: pair(V, slice(None), 2 * z + t, slice(j * D_HEAD, (j + 1) * D_HEAD))
                    o = bank(b)[:, z * S:(z + 1) * S]
                    matmul3(nc, o, v(0), pair(PT, slice(None), z, slice(0, S)), True, False)
                    ins = matmul3(nc, o[:, P:S], v(1), pair(PT, slice(None), z, slice(S, 3 * P)), False, True)
                ins.then_inc(s_pr, 1)

            def values(it):
                pe.wait_ge(s_xv, 32 * (it + 1))
                for a in range(CT):
                    m = value_tile(it) + a
                    pe.wait_ge(s_pr_lo, m - 1)
                    for k in range(KD):
                        ins = matmul3(nc, bank(bank_of(value_tile(0) + a)), pair(XV, slice(None), k, slice(a * P, (a + 1) * P)),
                                      pair(WV, slice(None), k), k == 0, k == KD - 1)
                    ins.then_inc(s_pr, 1)

            def transposes(n, u):
                if not (isinstance(n, int) and n == 0):
                    pe.wait_ge(s_pt_lo, 2 * n)
                for b in range(2):
                    pe.wait_ge(s_norm, 4 * n + 2 * b + 2)
                    for i in range(3):
                        at = TB[b] * CHUNK + i * P
                        ins = nc.tensor.transpose(ps[:, at:at + P], PR[:, u, b, i * P:(i + 1) * P], C.ident[:])
                    ins.then_inc(s_pt, 1)

            def outputs(n, j, m):
                pe.wait_ge(s_pr_lo, m + 1)
                for a in range(CT):
                    o = ps[:, YB * CHUNK + a * D:YB * CHUNK + (a + 1) * D]
                    ins = matmul3(nc, o, pair(O, slice(None), slice(a * P, (a + 1) * P)), pair(WO, slice(None), j),
                                  j == 0 and a % 2 == 0, j == HG - 1 and a % 2 == 1, skip_group_check=True)
                ins.then_inc(s_eh, 1)

            def steps(it, first, last):
                g = it // NPAIR
                for j in range(HG):
                    n = HG * it + j
                    scores(n, j, key_tile(it, j - 1, first) + 1 if j else query_tile(it) + NQ)
                    if not (first and j == 0):
                        transposes(n - 1, (j - 1) % 2)
                    if not (last and j == HG - 1):
                        m, b = key_tile(it, j, first), bank_of(key_tile(0, j, first))
                        if j < HG - 1:
                            pe.wait_ge(s_wk, 2 * (HG * g + j + 2))
                            keys(m, b, j + 1, it % NPAIR)
                        else:
                            pe.wait_ge(s_wk, 2 * (HG * ((it + 1) // NPAIR) + 1))
                            keys(m, b, 0, (it + 1) % NPAIR)
                            queries(it + 1)
                    if j >= 2:
                        if j == 2 and not first:
                            pe.wait_ge(s_ya, it)
                        pe.wait_ge(s_wo, 2 * (HG * g + j - 1))
                        outputs(n - 2, j - 2, head_tile(it, j - 1))
                    elif not first:
                        pe.wait_ge(s_wo, 2 * (HG * ((it - 1) // NPAIR) + j + 3))
                        outputs(n - 2, j + 2, head_tile(it, 0) if j else head_tile(it - 1, HG - 1))
                    if j == 1:
                        pe.wait_ge(s_pr_lo, value_tile(it) + CT)
                    if not (first and j == 0):
                        head(n - 1, (j - 1) % HG, head_tile(it, j, last), bank_of(head_tile(0, j, last)))
                    if j == 0:
                        pe.wait_ge(s_wv, 2 * (g + 1))
                        values(it)

            pe.wait_ge(s_wk, 2)
            pe.wait_ge(ln.s_lo, 2 * NCH)
            keys(0, bank_of(0), 0, 0)
            pe.wait_ge(s_wq_lo, NQ)
            queries(0)
            steps(0, True, False)
            with pe.Fori(1, NIT - 1) as it:
                steps(it, False, False)
            steps(NIT - 1, False, True)
            m = head_tile(NIT - 1, HG - 1, True)
            transposes(HG * NIT - 1, (HG - 1) % 2)
            outputs(HG * NIT - 2, HG - 2, m)
            head(HG * NIT - 1, HG - 1, m + 1, bank_of(m + 1))
            outputs(HG * NIT - 1, HG - 1, m + 1)


def macaron(nc, io, out):
    x = io["L0_attn_x"].rearrange("b t d -> (b t) d")
    T, D = x.shape
    w = {k: io["L0_ffn_" + k] for k in ("router", "w_up_gate", "w_down", "shared_w_up_gate", "shared_w_down")}
    E = w["router"].shape[1]
    CAP = -(-int(T * TOP_K * CAP_FACTOR) // E)
    o = out.rearrange("b t d -> (b t) d")
    xbuf = nc.dram_tensor("expert_in", (E * CAP, D), F32, kind="Internal").ap()
    ybuf = nc.dram_tensor("expert_out", (E * CAP, D), F32, kind="Internal").ap()
    with ExitStack() as ctx:
        ps = ctx.enter_context(nc.psum_tensor("ps", [P, 8 * CHUNK], F32))
        X = ctx.enter_context(nc.sbuf_tensor("x", [P, T // P, D], F32))
        C = Consts(ctx, nc, E)
        first_sems = Sems(nc)
        ffn_block(first_sems, nc, "f1_", ps, C, X, w, x, None, xbuf, ybuf, True)
        first_sems.clear()
        attention_block(Sems(nc), nc, "at_", ps, C, X, io)
        ffn_block(Sems(nc), nc, "f2_", ps, C, X, w, None, o, xbuf, ybuf, False)


_INS = ["L0_attn_x", "L0_attn_Wq", "L0_attn_bq", "L0_attn_Wk", "L0_attn_bk", "L0_attn_Wv", "L0_attn_bv",
        "L0_attn_Wo", "L0_attn_bo", "L0_ffn_router", "L0_ffn_w_up_gate", "L0_ffn_w_down",
        "L0_ffn_shared_w_up_gate", "L0_ffn_shared_w_down"]


def kernel(**inputs):
    import numpy as _np
    import concourse.bacc as _bacc
    from concourse import mybir as _mybir
    from concourse.bass_utils import run_bass_kernel_spmd as _run

    nc = _bacc.Bacc("TRN2", target_bir_lowering=False, num_devices=1)
    arrays, io = {}, {}
    for name in _INS:
        a = _np.ascontiguousarray(inputs[name])
        arrays["in_" + name] = a
        io[name] = nc.dram_tensor("in_" + name, a.shape, _mybir.dt.from_np(a.dtype), kind="ExternalInput").ap()
    out = nc.dram_tensor("out", arrays["in_L0_attn_x"].shape, _mybir.dt.float32, kind="ExternalOutput").ap()
    macaron(nc, io, out)
    r = _run(nc, [arrays], core_ids=[0])
    return r.results[0]["out"]
```

```python
from contextlib import ExitStack

import concourse.bass as bass
from concourse import mybir

P = 128
F32 = mybir.dt.float32
F32R = mybir.dt.float32r
BF16 = mybir.dt.bfloat16
U32 = mybir.dt.uint32
ALU = mybir.AluOpType
ACT = mybir.ActivationFunctionType
AX_X = mybir.AxisListType.X

LN_EPS = 1e-5
MASKED = -3.0e38
CHUNK = 512
CT = CHUNK // P
CAP_FACTOR = 1.25
TOP_K = 2
D_HEAD = 128


class Split:

    def __init__(self, ctx, nc, name, shape):
        self.hi = ctx.enter_context(nc.sbuf_tensor(name + "_hi", shape, F32R))
        self.lo = ctx.enter_context(nc.sbuf_tensor(name + "_lo", shape, F32R))


def matmul3(nc, out, stationary, moving, first, last, **kw):
    (s_hi, s_lo), (m_hi, m_lo) = stationary, moving
    nc.tensor.matmul(out, s_hi, m_hi, start=first, stop=False, **kw)
    nc.tensor.matmul(out, s_hi, m_lo, start=False, stop=False, **kw)
    return nc.tensor.matmul(out, s_lo, m_hi, start=False, stop=last, **kw)


def pair(split, *at):
    return split.hi[at], split.lo[at]


def sub_rounded(eng, out_lo, full, hi):
    return eng.tensor_tensor(out_lo, full, hi.bitcast(F32), ALU.subtract)


def open_at_one(eng, *sems):
    for s in sems:
        eng.nop().then_inc(s, 1)


def wait_past(eng, sem, count):
    if not (isinstance(count, int) and count <= 0):
        eng.wait_ge(sem, count)


def hold(eng, sem, value):
    eng.wait_ge(sem, value)
    eng.nop(nofuse=True)


class Consts:

    def __init__(self, ctx, nc, n_experts):
        sb = lambda name, shape, dt: ctx.enter_context(nc.sbuf_tensor(name, shape, dt))
        self.ident = sb("ident", [P, P], F32)
        self.ident_bf = sb("ident_bf", [P, P], BF16)
        self.before = sb("before", [P, P], BF16)
        self.ones = sb("ones", [P, P], BF16)
        self.causal = sb("causal", [P, P], BF16)
        self.fold = sb("fold", [64, n_experts], F32)
        self.expert_id = sb("expert_id", [P, n_experts], F32)
        self.minus_half = sb("minus_half", [P, CT], F32)
        self.zeros = sb("zeros", [P, 2 * P], F32)

    def build(self, pool, sem):
        E = self.expert_id.shape[1]
        pool.memset(self.ident[:], 0.0)
        pool.memset(self.ident_bf[:], 0.0)
        pool.memset(self.before[:], 1.0)
        pool.memset(self.ones[:], 1.0)
        pool.memset(self.causal[:], 0.0)
        pool.memset(self.fold[:], 0.0)
        pool.memset(self.minus_half[:], -0.5)
        pool.iota(self.expert_id[:], pattern=[[1, E]], base=0, channel_multiplier=0,
                  allow_small_or_imprecise_dtypes=True)
        pool.memset(self.zeros[:], 0.0).then_inc(sem, 1)
        pool.wait_ge(sem, 1)
        for m in (self.ident, self.ident_bf):
            pool.affine_select(out=m[:], in_=m[:], compare_op=ALU.not_equal, fill=1.0, base=0,
                               pattern=[[-1, P]], channel_multiplier=1)
        pool.affine_select(out=self.before[:], in_=self.before[:], compare_op=ALU.is_gt, fill=0.0,
                           base=0, pattern=[[1, P]], channel_multiplier=-1)
        pool.affine_select(out=self.causal[:], in_=self.causal[:], compare_op=ALU.is_ge, fill=MASKED,
                           base=0, pattern=[[-1, P]], channel_multiplier=1)
        pool.affine_select(out=self.fold[:], in_=self.fold[:], compare_op=ALU.not_equal, fill=1.0,
                           base=0, pattern=[[-1, E]], channel_multiplier=1).then_inc(sem, 1)
        pool.wait_ge(sem, 2)
        pool.affine_select(out=self.fold[:], in_=self.fold[:], compare_op=ALU.not_equal, fill=1.0,
                           base=-32, pattern=[[-1, E]], channel_multiplier=1).then_inc(sem, 1)


class Sems:

    def __init__(self, nc):
        self.nc, self.all = nc, []

    def new(self, name):
        self.all.append(self.nc.alloc_semaphore(name))
        return self.all[-1]

    def clear(self):
        self.nc.clear_and_free_semaphores(self.all)
        self.nc.all_engine_barrier()


class LayerNorm:

    def __init__(self, ctx, sems, nc, tag, D, n_xn):
        sb = lambda name, shape: ctx.enter_context(nc.sbuf_tensor(tag + name, shape, F32))
        self.stats = [sb(f"stats{u}", [P, CT, 6]) for u in range(2)]
        self.mean_var = [sb(f"mean_var{u}", [P, CT, 2]) for u in range(2)]
        self.var_eps = [sb(f"var_eps{u}", [P, CT]) for u in range(2)]
        self.rstd = [sb(f"rstd{u}", [P, CT]) for u in range(2)]
        self.xn = [sb(f"xn{u}", [P, CT, D]) for u in range(n_xn)]
        sem = lambda name: sems.new(tag + name)
        self.s_step = sem("ln_step")
        self.s_rstd = sem("ln_rstd")
        self.s_xn = sem("ln_xn")
        self.s_tp = sem("xT_psum")
        self.s_hi = sem("xT_hi")
        self.s_lo = sem("xT_lo")
        self.KD = D // P

    def moments(self, dve, X, c):
        u = c % 2
        for a in range(CT):
            ins = dve.bn_stats(self.stats[u][:, a, :], X[:, c * CT + a, :])
        ins.then_inc(self.s_step, 1)
        dve.wait_ge(self.s_step, 3 * c + 1)
        for a in range(CT):
            ins = dve.bn_aggr(self.mean_var[u][:, a, :], self.stats[u][:, a, :])
        ins.then_inc(self.s_step, 1)
        dve.wait_ge(self.s_step, 3 * c + 2)
        dve.tensor_scalar(self.var_eps[u][:], self.mean_var[u][:, :, 1], LN_EPS, None,
                          ALU.add).then_inc(self.s_step, 1)

    def normalise(self, dve, X, c):
        u = c % 2
        if c >= len(self.xn):
            dve.wait_ge(self.s_tp, 2 * (c - len(self.xn) + 1))
        dve.wait_ge(self.s_rstd, c + 1)
        for a in range(CT):
            ins = dve.tensor_scalar(self.xn[c % len(self.xn)][:, a, :], X[:, c * CT + a, :],
                                    self.mean_var[u][:, a, 0:1], self.rstd[u][:, a:a + 1],
                                    ALU.subtract, ALU.mult)
        ins.then_inc(self.s_xn, 1)

    def inverse_root(self, pool, consts, c):
        pool.wait_ge(self.s_step, 3 * c + 3)
        pool.tensor_tensor(self.rstd[c % 2][:], self.var_eps[c % 2][:], consts.minus_half[:],
                           ALU.pow).then_inc(self.s_rstd, 1)

    def transpose(self, nc, pe, consts, ps, c, bank):
        pe.wait_ge(self.s_xn, c + 1)
        for k in range(self.KD):
            for a in range(CT):
                at = (bank + k) * CHUNK + a * P
                xn = self.xn[c % len(self.xn)]
                ins = nc.tensor.transpose(ps[:, at:at + P], xn[:, a, k * P:(k + 1) * P], consts.ident[:])
            ins.then_inc(self.s_tp, 1)

    def split_hi(self, nc, act, XT, ps, c, bank):
        for k in range(self.KD):
            act.wait_ge(self.s_tp, 2 * c + k + 1)
            b = (bank + k) * CHUNK
            nc.scalar.activation(XT.hi[:, k, c * CHUNK:(c + 1) * CHUNK], ps[:, b:b + CHUNK], ACT.Copy).then_inc(self.s_hi, 1)

    def split_lo(self, nc, dve, XT, ps, c, bank):
        for k in range(self.KD):
            dve.wait_ge(self.s_hi, 2 * c + k + 1)
            b = (bank + k) * CHUNK
            cols = slice(c * CHUNK, (c + 1) * CHUNK)
            sub_rounded(nc.vector, XT.lo[:, k, cols], ps[:, b:b + CHUNK], XT.hi[:, k, cols]).then_inc(self.s_lo, 1)


def ffn_block(sems, nc, tag, ps, C, X, w, x_in, out, xbuf, ybuf, fill_xbuf):
    D, E = w["router"].shape
    I = w["w_down"].shape[1]
    J = w["shared_w_down"].shape[0]
    NT = X.shape[1]
    T = NT * P
    NCH = NT // CT
    KD = D // P
    CAP = -(-int(T * TOP_K * CAP_FACTOR) // E)
    ST = CAP // P
    assert CAP % P == 0 and KD == 2 and NCH % 2 == 0
    JF, JR = J // P, J % P
    NJ = JF + 1
    IR = I - P
    UPW = 2 * P + 64 + IR
    HALF = CAP // 2
    NOSLOT = 4 * E * CAP
    UPS = 2 * NJ - 1
    HS = 3
    SUG = 3

    with ExitStack() as ctx:
        sb = lambda name, shape, dt=F32: ctx.enter_context(nc.sbuf_tensor(tag + name, shape, dt))
        sem = lambda name: sems.new(tag + name)
        ln = LayerNorm(ctx, sems, nc, tag, D, NCH)
        XT = Split(ctx, nc, tag + "xT", [P, KD, T])
        raw_up = sb("raw_up", [P, KD, 2 * J])
        raw_dn = sb("raw_down", [P, NJ, D])
        SU = Split(ctx, nc, tag + "sh_up", [P, KD, 2 * J])
        SD = Split(ctx, nc, tag + "sh_down", [P, NJ, D])
        raw_r = sb("raw_router", [P, KD, E])
        RT = sb("router", [P, KD, 64], F32R)
        H = Split(ctx, nc, tag + "hidden", [P, HS * CHUNK])
        SG = sb("silu", [P, 2, CHUNK])
        HF = sb("prod", [P, 2, CHUNK])
        LT = sb("logitsT", [64, 2, CHUNK])
        LG = sb("logits", [P, CT, E])
        TOP = sb("top8", [P, CT, 8])
        IX = sb("top8_ix", [P, CT, 8], U32)
        IXF = sb("expert_of", [P, TOP_K, CT])
        OH = [sb(f"onehot{u}", [P, TOP_K * CT, E]) for u in range(2)]
        BASE = [sb(f"slot_base{u}", [P, TOP_K * CT]) for u in range(2)]
        M = [sb(f"chosen{u}", [P, CT, E], BF16) for u in range(2)]
        CARRY = [sb(f"carry{u}", [P, E], BF16) for u in range(2)]
        MS = sb("chosen_sum", [P, E])
        PK = sb("pos", [P, TOP_K * CT])
        POS = sb("onehot_pos", [P, TOP_K * CT, E])
        OVER = sb("over", [P, TOP_K * CT])
        SLOT = sb("slot", [P, TOP_K * CT])
        SCI = [sb(f"scatter_ix{c}", [P, TOP_K * CT], U32) for c in range(NCH)]
        GIX = sb("gather_ix_all", [P, NCH, TOP_K * CT], U32)
        GS = sb("gather_ix", [P, 4, TOP_K], U32)
        VALID = sb("valid", [P, NCH, TOP_K * CT])
        GAP = sb("gap", [P, NCH, CT])
        CW = sb("combine_w", [P, NCH, TOP_K * CT])
        G = sb("gathered", [P, 4, TOP_K, D])
        raw_wu = sb("raw_wu", [P, KD, UPW])
        raw_wd = sb("raw_wd", [P, 2, D])
        WU = Split(ctx, nc, tag + "ex_up", [P, KD, UPW])
        WD = Split(ctx, nc, tag + "ex_down", [P, 2, D])
        XE = sb("ex_rows", [P, ST, D])
        XET = Split(ctx, nc, tag + "ex_xT", [P, KD, CAP])
        OE = sb("ex_out", [P, ST, D])

        s_const = sem("const")
        s_x = [sem(f"x{c}") for c in range(NCH)]
        s_wr = sem("w_router")
        s_wu_raw, s_wd_raw = sem("sh_up_raw"), sem("sh_down_raw")
        s_fill = sem("fill")
        s_rt = sem("router_split")
        s_su_hi, s_su_lo = sem("sh_up_hi"), sem("sh_up_lo")
        s_sd_hi, s_sd_lo = sem("sh_down_hi"), sem("sh_down_lo")
        s_ltp, s_lt, s_lgp = sem("logitsT_psum"), sem("logitsT"), sem("logits_psum")
        s_rank, s_chosen = sem("rank"), sem("chosen")
        s_carry = sem("carry")
        s_pos, s_slot = sem("pos_psum"), sem("slot")
        s_scat = [sem(f"scatter{c}") for c in range(NCH)]
        s_up = sem("up_psum")
        s_sg, s_prod, s_hhi, s_hlo = sem("silu"), sem("prod"), sem("h_hi"), sem("h_lo")
        s_dn, s_y = sem("down_psum"), sem("y")
        s_ex_pad = sem("ex_pad")
        s_ewu, s_ewd, s_xe = sem("ex_wu_raw"), sem("ex_wd_raw"), sem("ex_rows")
        s_ewu_hi, s_ewu_lo, s_ewd_hi, s_ewd_lo = sem("ex_wu_hi"), sem("ex_wu_lo"), sem("ex_wd_hi"), sem("ex_wd_lo")
        s_etp, s_ext_hi, s_ext_lo = sem("ex_xT_psum"), sem("ex_xT_hi"), sem("ex_xT_lo")
        s_eup = sem("ex_up_psum")
        s_esg, s_eprod, s_ehhi, s_ehlo = sem("ex_silu"), sem("ex_prod"), sem("ex_h_hi"), sem("ex_h_lo")
        s_edn, s_eo = sem("ex_down_psum"), sem("ex_out")
        s_ybuf = sem("ybuf")
        s_oe_free = sem("oe_free")
        s_exp, s_cw = sem("gap_exp"), sem("combine_w")
        s_gix = sem("gather_ix")
        s_gat = [sem(f"gather{s}") for s in range(4)]
        s_comb = sem("combined")
        s_out = sem("out")

        bank = lambda b, n=CHUNK, p=P: ps[0:p, b * CHUNK:b * CHUNK + n]
        EH = [[m[:, i * CAP:(i + 1) * CAP] for i in range(2)] for m in (H.hi, H.lo)]
        hcols = lambda q: slice(q % HS * CHUNK, (q % HS + 1) * CHUNK)
        assert NJ % HS == 0 and NJ % 2 == 0 and 2 * CAP <= HS * CHUNK
        jrows = lambda q: P if q < JF else JR
        TG = [(0, 2), (2, 2), (4, 1)]
        assert ST == 5
        TPB, LTB, LGB, POB = (6, 4, 6, 6), (6, 4, 6, 6), (7, 5, 7, 7), (6, 7, 6, 6)
        upc = 2 * J // SUG + (-(2 * J // SUG)) % P
        assert NCH == 4 and 2 * NJ >= 12

        def pe_up(pe, n, q):
            wait_past(pe, s_prod, NJ * n + q - 1)
            tiles = [(q * 2 * P, P, 2 * (q % 2)), (q * 2 * P + P, P, 2 * (q % 2) + 1)] if q < JF else \
                    [(q * 2 * P, 2 * JR, 2 * (q % 2))]
            for col, m, b in tiles:
                for k in range(KD):
                    ins = matmul3(nc, bank(b, p=m), pair(SU, slice(None), k, slice(col, col + m)),
                                  pair(XT, slice(None), k, bass.ds(n * CHUNK, CHUNK)),
                                  k == 0, k == KD - 1)
                ins.then_inc(s_up, 1)

        def pe_down(pe, n, q):
            pe.wait_ge(s_hlo, NJ * n + q + 1)
            if q == 0:
                wait_past(pe, s_y, n)
            m = jrows(q)
            for a in range(CT):
                cols = slice(q % HS * CHUNK + a * P, q % HS * CHUNK + (a + 1) * P)
                ins = matmul3(nc, ps[:, 4 * CHUNK + a * D:4 * CHUNK + (a + 1) * D], pair(H, slice(0, m), cols),
                              pair(SD, slice(0, m), q), q == 0 and a % 2 == 0, q == NJ - 1 and a % 2 == 1,
                              skip_group_check=True)
            ins.then_inc(s_dn, 1)

        def act_silu(act, n, q):
            act.wait_ge(s_up, UPS * n + 2 * q + 1)
            wait_past(act, s_prod, NJ * n + q - 1)
            m = jrows(q)
            nc.scalar.activation(SG[0:m, q % 2, :], bank(2 * (q % 2), p=m), ACT.Silu).then_inc(s_sg, 1)

        def act_hhi(act, n, q):
            wait_past(act, s_dn, NJ * n + q - HS + 1)
            act.wait_ge(s_prod, NJ * n + q + 1)
            m = jrows(q)
            nc.scalar.activation(H.hi[0:m, hcols(q)], HF[0:m, q % 2, :], ACT.Copy).then_inc(s_hhi, 1)

        def dve_prod(dve, n, q):
            dve.wait_ge(s_sg, NJ * n + q + 1)
            dve.wait_ge(s_up, UPS * n + min(2 * q + 2, UPS))
            wait_past(dve, s_hlo, NJ * n + q - 1)
            b = 2 * (q % 2)
            up = ps[0:P, (b + 1) * CHUNK:(b + 2) * CHUNK] if q < JF else ps[JR:2 * JR, b * CHUNK:(b + 1) * CHUNK]
            m = jrows(q)
            nc.vector.tensor_tensor(HF[0:m, q % 2, :], SG[0:m, q % 2, :], up, ALU.mult).then_inc(s_prod, 1)

        def dve_hlo(dve, n, q):
            dve.wait_ge(s_hhi, NJ * n + q + 1)
            m = jrows(q)
            sub_rounded(nc.vector, H.lo[0:m, hcols(q)], HF[0:m, q % 2, :],
                        H.hi[0:m, hcols(q)]).then_inc(s_hlo, 1)

        def dve_y(dve, n):
            dve.wait_ge(s_dn, NJ * (n + 1))
            x = X[:, bass.ds(n * CT, CT), :].rearrange("p c d -> p (c d)")
            nc.vector.scalar_tensor_tensor(out=x, in0=ps[:, 4 * CHUNK:6 * CHUNK], scalar=0.5, in1=x,
                                           op0=ALU.mult, op1=ALU.add).then_inc(s_y, 1)

        def at_slot(engine_slot):
            for k in range(2 * NJ):
                engine_slot(k, k // NJ, k % NJ)

        def up_cols(g):
            return slice(g * upc, min((g + 1) * upc, 2 * J))

        block = ctx.enter_context(nc.Block())

        @block.sync
        def _(sp):
            def load_x(c):
                if x_in is not None:
                    sp.dma_start(X[:, c * CT:(c + 1) * CT, :],
                                 x_in[c * CHUNK:(c + 1) * CHUNK, :].rearrange("(a p) d -> p a d", p=P)).then_inc(s_x[c], 16)

            load_x(0)
            sp.dma_start(raw_r[:], w["router"].rearrange("(k p) e -> p k e", p=P)).then_inc(s_wr, 16)
            load_x(1)
            for k in range(KD):
                for z in range(2):
                    src = w["shared_w_up_gate"][k * P:(k + 1) * P, z * J:(z + 1) * J]
                    sp.dma_start(raw_up[:, k, 0:2 * P * JF].rearrange("p (j z n) -> p j z n", z=2, n=P)[:, :, z, :],
                                 src[:, 0:P * JF].rearrange("p (j n) -> p j n", n=P)).then_inc(s_wu_raw, 16)
                    sp.dma_start(raw_up[:, k, 2 * P * JF + z * JR:2 * P * JF + (z + 1) * JR],
                                 src[:, P * JF:J]).then_inc(s_wu_raw, 16)
            load_x(2)
            load_x(3)
            sp.dma_start(raw_dn[:, 0:JF, :], w["shared_w_down"][0:JF * P, :].rearrange("(j p) d -> p j d", p=P)
                         ).then_inc(s_wd_raw, 16)
            sp.dma_start(raw_dn[0:JR, JF, :], w["shared_w_down"][JF * P:J, :]).then_inc(s_wd_raw, 16)
            if fill_xbuf:
                sp.wait_ge(s_const, 1)
                rows = E * CAP // P
                half = rows // 2
                for z in range(2):
                    sp.dma_start(xbuf[z * half * P:(z + 1) * half * P, :].rearrange("(p r) d -> p r d", p=P),
                                 C.zeros[:, None, :].broadcast_to([P, half, D])).then_inc(s_fill, 16)

            def load_up(e):
                src = w["w_up_gate"][bass.ds(e, 1), :, :].rearrange("a (k p) n -> p (a k) n", p=P)
                for dst, at, n in ((0, 0, P), (P, I, P), (2 * P, P, IR), (2 * P + 64, I + P, IR)):
                    sp.dma_start(raw_wu[:, :, dst:dst + n], src[:, :, at:at + n]).then_inc(s_ewu, 16)

            def load_down(e):
                src = w["w_down"][bass.ds(e, 1), :, :].rearrange("a i d -> (a i) d")
                sp.dma_start(raw_wd[:, 0, :], src[0:P, :]).then_inc(s_ewd, 16)
                sp.dma_start(raw_wd[0:IR, 1, :], src[P:I, :]).then_inc(s_ewd, 16)

            def load_rows(e):
                sp.dma_start(XE[:], xbuf[bass.ds(e * CAP, CAP), :].rearrange("(s p) d -> p s d", p=P)).then_inc(s_xe, 16)

            sp.wait_ge(s_ex_pad, 2)
            load_up(0)
            load_down(0)
            for c in range(NCH):
                sp.wait_ge(s_scat[c], 16 * TOP_K * CT)
            load_rows(0)
            with sp.Fori(0, E - 1) as e:
                sp.wait_ge(s_ewu_hi, e + 1)
                sp.wait_ge(s_ewu_lo, e + 1)
                load_up(e + 1)
                sp.wait_ge(s_etp, 3 * e + 3)
                load_rows(e + 1)
                sp.wait_ge(s_ewd_hi, e + 1)
                sp.wait_ge(s_ewd_lo, e + 1)
                load_down(e + 1)
            if out is not None:
                dst = out.rearrange("(c p) d -> p c d", p=P)
                for t0, t1 in ((0, NT // 2), (NT // 2, NT - CT), (NT - CT, NT)):
                    sp.wait_ge(s_comb, 1 + 2 * t1)
                    if t1 == NT:
                        sp.wait_ge(s_y, NCH)
                    sp.dma_start(dst[:, t0:t1, :], X[:, t0:t1, :]).then_inc(s_out, 16)
                sp.wait_ge(s_out, 48)

        @block.gpsimd
        def _(pool):
            open_at_one(pool, s_oe_free)
            if fill_xbuf:
                C.build(pool, s_const)
                pool.wait_ge(s_const, 3)
            nc.gpsimd.memset(raw_wu[:, :, 2 * P:UPW], 0.0).then_inc(s_ex_pad, 1)
            nc.gpsimd.memset(raw_wd[:, 1, :], 0.0).then_inc(s_ex_pad, 1)
            ln.inverse_root(nc.gpsimd, C, 0)
            ln.inverse_root(nc.gpsimd, C, 1)
            ln.inverse_root(nc.gpsimd, C, 2)
            if fill_xbuf:
                pool.wait_ge(s_fill, 32)
            for c in range(NCH):
                pool.wait_ge(s_slot, 1 + 5 * c + 5)
                for k in range(TOP_K):
                    for a in range(CT):
                        z = k * CT + a
                        nc.gpsimd.indirect_dma_start(
                            out=xbuf, out_offset=bass.IndirectOffsetOnAxis(ap=SCI[c][:, z:z + 1], axis=0),
                            in_=ln.xn[c][:, a, :], in_offset=None,
                            bounds_check=E * CAP - 1, oob_is_err=False).then_inc(s_scat[c], 16)
                if c == 0:
                    ln.inverse_root(nc.gpsimd, C, 3)
            with pool.Fori(0, E) as e:
                pool.wait_ge(s_ybuf, 16 * (e + 1))
                pool.nop().then_inc(s_oe_free, 1)

            def gather(j, r):
                t = (NT // 2) * j + r
                s = r % 4
                hold(pool, s_comb, 1 + (2 * (NT // 2) * j if r < 4 else 2 * (t - 3)))
                c = (NCH // 2) * j + r // CT
                nc.gpsimd.tensor_copy(GS[:, s, :], GIX[:, bass.ds(c, 1), r % CT::CT]).then_inc(s_gix, 1)
                hold(pool, s_gix, t + 1)
                for k in range(TOP_K):
                    nc.gpsimd.indirect_dma_start(
                        out=G[:, s, k, :], out_offset=None, in_=ybuf,
                        in_offset=bass.IndirectOffsetOnAxis(ap=GS[:, s, k:k + 1], axis=0),
                        bounds_check=E * CAP - 1, oob_is_err=True).then_inc(s_gat[s], 16)

            with pool.Fori(0, NCH // 2) as j:
                for r in range(NT // 2):
                    gather(j, r)

        @block.scalar
        def _(act):
            open_at_one(act, s_eo, s_ehhi)

            def split_hi(dst, src):
                return nc.scalar.activation(dst, src, ACT.Copy)

            def up_hi(g):
                act.wait_ge(s_wu_raw, 16 * 4 * KD)
                split_hi(SU.hi[:, :, up_cols(g)], raw_up[:, :, up_cols(g)]).then_inc(s_su_hi, 1)

            def logits(c):
                act.wait_ge(s_ltp, c + 1)
                nc.scalar.activation(LT[:, c % 2, :], bank(LTB[c], p=64), ACT.Copy).then_inc(s_lt, 1)

            ln.split_hi(nc, act, XT, ps, 0, TPB[0])
            ln.split_hi(nc, act, XT, ps, 1, TPB[1])
            up_hi(0)
            logits(0)
            logits(1)
            up_hi(1)
            up_hi(2)
            act.wait_ge(s_wd_raw, 32)
            split_hi(SD.hi[:, 0:JF, :], raw_dn[:, 0:JF, :]).then_inc(s_sd_hi, 1)
            split_hi(SD.hi[0:JR, JF, :], raw_dn[0:JR, JF, :]).then_inc(s_sd_hi, 1)

            def slot(k, n, q):
                act_silu(act, n, q)
                if k in (3, 6):
                    logits({3: 2, 6: 3}[k])
                if k:
                    act_hhi(act, (k - 1) // NJ, (k - 1) % NJ)
                if k in (2, 5):
                    c = {2: 2, 5: 3}[k]
                    ln.split_hi(nc, act, XT, ps, c, TPB[c])

            at_slot(slot)
            act_hhi(act, 1, NJ - 1)
            act.wait_ge(s_slot, 1 + 5 * NCH)
            nc.scalar.activation(GAP[:], GAP[:], ACT.Exp).then_inc(s_exp, 1)

            def weights_up(e):
                act.wait_ge(s_ewu, 64 * (e + 1))
                act.wait_ge(s_eup, 1 + 6 * e)
                split_hi(WU.hi[:], raw_wu[:]).then_inc(s_ewu_hi, 1)

            def weights_down(e):
                act.wait_ge(s_ewd, 32 * (e + 1))
                act.wait_ge(s_edn, 1 + ST * e)
                split_hi(WD.hi[:], raw_wd[:]).then_inc(s_ewd_hi, 1)

            def rows(e):
                for g, (s0, ns) in enumerate(TG):
                    act.wait_ge(s_etp, 3 * e + g + 1)
                    src = bank(4 + g, ns * D).rearrange("p (s k t) -> p k s t", k=KD, t=P)
                    dst = XET.hi[:, :, s0 * P:(s0 + ns) * P].rearrange("p k (s t) -> p k s t", t=P)
                    split_hi(dst, src).then_inc(s_ext_hi, 1)

            def silu(e, z):
                m = P if z % 2 == 0 else IR
                act.wait_ge(s_eup, 1 + 6 * e + (1, 3, 4, 6)[z])
                act.wait_ge(s_eprod, 1 + 4 * e + max(z - 1, 0))
                nc.scalar.activation(SG[0:m, z % 2, 0:HALF], bank((0, 2, 3, 1)[z], HALF, m), ACT.Silu).then_inc(s_esg, 1)

            def h_hi(e, z):
                m = P if z % 2 == 0 else IR
                if z == 0:
                    act.wait_ge(s_edn, 1 + ST * e)
                act.wait_ge(s_eprod, 1 + 4 * e + z + 1)
                cols = slice((z // 2) * HALF, (z // 2 + 1) * HALF)
                split_hi(EH[0][z % 2][0:m, cols], HF[0:m, z % 2, 0:HALF]).then_inc(s_ehhi, 1)

            def hidden(e):
                for z in range(4):
                    silu(e, z)
                    if z:
                        h_hi(e, z - 1)
                h_hi(e, 3)

            def outs(e):
                act.wait_ge(s_oe_free, 1 + e)
                for s in range(ST):
                    act.wait_ge(s_edn, 1 + ST * e + s + 1)
                    nc.scalar.activation(OE[:, s, :], bank(7 - 4 * (s % 2), D), ACT.Copy).then_inc(s_eo, 1)
                act.wait_ge(s_eo, 1 + ST * (e + 1))
                act.dma_start(ybuf[bass.ds(e * CAP, CAP), :].rearrange("(s p) d -> p s d", p=P), OE[:]).then_inc(s_ybuf, 16)

            weights_up(0)
            weights_down(0)
            rows(0)
            with act.Fori(0, E - 1) as e:
                hidden(e)
                rows(e + 1)
                weights_up(e + 1)
                outs(e)
                weights_down(e + 1)
            hidden(E - 1)
            outs(E - 1)
            act.wait_ge(s_edn, 1 + ST * E)
            with act.Fori(NCH // 2, NCH) as n:
                for q in range(NJ):
                    act_silu(act, n, q)
                    if q:
                        act_hhi(act, n, q - 1)
                act_hhi(act, n, NJ - 1)

        @block.vector
        def _(dve):
            open_at_one(dve, s_eprod, s_ehlo, s_ext_lo, s_slot, s_comb)
            nc.vector.memset(RT[:].bitcast(F32), 0.0)
            nc.vector.memset(CARRY[0][:], 0.0).then_inc(s_rt, 1)
            dve.wait_ge(s_rt, 1)
            dve.wait_ge(s_wr, 16)
            nc.vector.tensor_copy(RT[:, :, 0:E], raw_r[:]).then_inc(s_rt, 1)
            dve.wait_ge(s_rt, 2)
            sub_rounded(nc.vector, RT[:, :, 32:32 + E], raw_r[:], RT[:, :, 0:E]).then_inc(s_rt, 1)

            def moments(c):
                if x_in is not None:
                    dve.wait_ge(s_x[c], 16)
                ln.moments(nc.vector, X, c)

            def up_lo(g):
                dve.wait_ge(s_su_hi, g + 1)
                sub_rounded(nc.vector, SU.lo[:, :, up_cols(g)], raw_up[:, :, up_cols(g)], SU.hi[:, :, up_cols(g)]
                            ).then_inc(s_su_lo, 1)

            def rank(c, u):
                dve.wait_ge(s_lgp, c + 1)
                lg = bank(LGB[c], CT * E).rearrange("p (a e) -> p a e", e=E)
                nc.vector.tensor_copy(LG[:], lg).then_inc(s_rank, 1)
                hold(dve, s_rank, 6 * c + 1)
                for a in range(CT):
                    ins = nc.vector.max(TOP[:, a, :], LG[:, a, :])
                ins.then_inc(s_rank, 1)
                hold(dve, s_rank, 6 * c + 2)
                for a in range(CT):
                    ins = nc.vector.max_index(IX[:, a, :], TOP[:, a, :], LG[:, a, :])
                ins.then_inc(s_rank, 1)
                nc.vector.tensor_tensor(GAP[:, c, :], TOP[:, :, 1], TOP[:, :, 0], ALU.subtract)
                dve.wait_ge(s_rank, 6 * c + 3)
                nc.vector.tensor_copy(IXF[:], IX[:, :, 0:TOP_K].rearrange("p a k -> p k a")).then_inc(s_rank, 1)
                dve.wait_ge(s_rank, 6 * c + 4)
                ixf = IXF[:].rearrange("p k a -> p (k a)")
                nc.vector.tensor_scalar(BASE[u][:], ixf, float(CAP), None, ALU.mult)
                nc.vector.tensor_tensor(OH[u][:], C.expert_id[:, None, :].broadcast_to([P, TOP_K * CT, E]),
                                        ixf[:, :, None].broadcast_to([P, TOP_K * CT, E]), ALU.is_equal).then_inc(s_rank, 1)
                dve.wait_ge(s_rank, 6 * c + 5)
                nc.vector.tensor_tensor(M[u][:], OH[u][:, 0:CT, :], OH[u][:, CT:2 * CT, :], ALU.add).then_inc(s_chosen, 1)
                dve.wait_ge(s_chosen, c + 1)
                nc.vector.tensor_reduce(MS[:], M[u][:].rearrange("p a e -> p e a"), AX_X, ALU.add).then_inc(s_rank, 1)
                if c < NCH - 1:
                    dve.wait_ge(s_rank, 6 * c + 6)
                    wait_past(dve, s_pos, c)
                    nc.vector.tensor_tensor(CARRY[(c + 1) % 2][:], CARRY[u][:], MS[:], ALU.add).then_inc(s_carry, 1)

            def slots(c, u):
                dve.wait_ge(s_pos, c + 1)
                pos = bank(POB[c], CT * E).rearrange("p (a e) -> p a e", e=E)
                nc.vector.tensor_tensor(POS[:].rearrange("p (k a) e -> p k a e", a=CT),
                                        OH[u][:].rearrange("p (k a) e -> p k a e", a=CT),
                                        pos[:, None, :, :].broadcast_to([P, TOP_K, CT, E]), ALU.mult).then_inc(s_slot, 1)
                dve.wait_ge(s_slot, 1 + 5 * c + 1)
                nc.vector.tensor_reduce(PK[:], POS[:], AX_X, ALU.add).then_inc(s_slot, 1)
                dve.wait_ge(s_slot, 1 + 5 * c + 2)
                nc.vector.tensor_scalar(OVER[:], PK[:], float(CAP), float(NOSLOT), ALU.is_ge, ALU.mult)
                nc.vector.tensor_scalar(VALID[:, c, :], PK[:], float(CAP), None, ALU.is_lt)
                nc.vector.scalar_tensor_tensor(out=SLOT[:], in0=PK[:], scalar=float(CAP - 1), in1=BASE[u][:],
                                               op0=ALU.min, op1=ALU.add).then_inc(s_slot, 1)
                dve.wait_ge(s_slot, 1 + 5 * c + 3)
                nc.vector.tensor_copy(GIX[:, c, :], SLOT[:]).then_inc(s_slot, 1)
                nc.vector.tensor_tensor(SCI[c][:], SLOT[:], OVER[:], ALU.add).then_inc(s_slot, 1)

            moments(0)
            moments(1)
            ln.normalise(nc.vector, X, 0)
            ln.normalise(nc.vector, X, 1)
            ln.split_lo(nc, dve, XT, ps, 0, TPB[0])
            ln.split_lo(nc, dve, XT, ps, 1, TPB[1])
            up_lo(0)
            rank(0, 0)
            rank(1, 1)
            up_lo(1)
            up_lo(2)
            moments(2)
            dve.wait_ge(s_sd_hi, 2)
            sub_rounded(nc.vector, SD.lo[:, 0:JF, :], raw_dn[:, 0:JF, :], SD.hi[:, 0:JF, :]).then_inc(s_sd_lo, 1)
            sub_rounded(nc.vector, SD.lo[0:JR, JF, :], raw_dn[0:JR, JF, :], SD.hi[0:JR, JF, :]).then_inc(s_sd_lo, 1)

            def slot(k, n, q):
                if k == 4:
                    rank(2, 0)
                elif k == 5:
                    slots(2, 0)
                elif k == 6:
                    ln.split_lo(nc, dve, XT, ps, 3, TPB[3])
                elif k == 7:
                    rank(3, 1)
                elif k == NJ + 2:
                    dve_y(dve, 0)
                    slots(3, 1)
                dve_prod(dve, n, q)
                if k:
                    dve_hlo(dve, (k - 1) // NJ, (k - 1) % NJ)
                if k == 0:
                    ln.normalise(nc.vector, X, 2)
                elif k == 1:
                    slots(0, 0)
                    slots(1, 1)
                elif k == 2:
                    ln.split_lo(nc, dve, XT, ps, 2, TPB[2])
                    moments(3)
                elif k == 3:
                    ln.normalise(nc.vector, X, 3)

            at_slot(slot)
            dve_hlo(dve, 1, NJ - 1)
            dve_y(dve, 1)

            gap = GAP[:].rearrange("p c a -> p (c a)")
            inv = LG[:].rearrange("p a e -> p (a e)")[:, 0:NT]
            dve.wait_ge(s_exp, 1)
            nc.vector.tensor_scalar(inv, gap, 1.0, None, ALU.add).then_inc(s_cw, 1)
            dve.wait_ge(s_cw, 1)
            nc.vector.reciprocal(inv, inv).then_inc(s_cw, 1)
            dve.wait_ge(s_cw, 2)
            inv_c = inv.rearrange("p (c a) -> p c a", a=CT)
            nc.vector.scalar_tensor_tensor(out=CW[:, :, 0:CT], in0=inv_c, scalar=0.5, in1=VALID[:, :, 0:CT],
                                           op0=ALU.mult, op1=ALU.mult)
            nc.vector.tensor_tensor(gap, gap, inv, ALU.mult).then_inc(s_cw, 1)
            dve.wait_ge(s_cw, 3)
            nc.vector.scalar_tensor_tensor(out=CW[:, :, CT:2 * CT], in0=GAP[:], scalar=0.5, in1=VALID[:, :, CT:2 * CT],
                                           op0=ALU.mult, op1=ALU.mult).then_inc(s_cw, 1)

            def weights_up(e):
                dve.wait_ge(s_ewu_hi, e + 1)
                sub_rounded(nc.vector, WU.lo[:], raw_wu[:], WU.hi[:]).then_inc(s_ewu_lo, 1)

            def weights_down(e):
                dve.wait_ge(s_ewd_hi, e + 1)
                sub_rounded(nc.vector, WD.lo[:], raw_wd[:], WD.hi[:]).then_inc(s_ewd_lo, 1)

            def rows(e):
                for g, (s0, ns) in enumerate(TG):
                    dve.wait_ge(s_ext_hi, 3 * e + g + 1)
                    for k in range(KD):
                        src = bank(4 + g, ns * D).rearrange("p (s k t) -> p k s t", k=KD, t=P)[:, k]
                        cols = slice(s0 * P, (s0 + ns) * P)
                        hi = XET.hi[:, k, cols].rearrange("p (s t) -> p s t", t=P)
                        ins = sub_rounded(nc.vector, XET.lo[:, k, cols].rearrange("p (s t) -> p s t", t=P), src, hi)
                    ins.then_inc(s_ext_lo, 1)

            def prod(e, z):
                m = P if z % 2 == 0 else IR
                dve.wait_ge(s_esg, 4 * e + z + 1)
                dve.wait_ge(s_eup, 1 + 6 * e + (2, 3, 5, 6)[z])
                dve.wait_ge(s_ehhi, 1 + 4 * e + max(z - 1, 0))
                dve.wait_ge(s_ehlo, 1 + 4 * e + max(z - 1, 0))
                b, p0 = ((1, 0), (2, 64), (0, 0), (1, 64))[z]
                nc.vector.tensor_tensor(HF[0:m, z % 2, 0:HALF], SG[0:m, z % 2, 0:HALF],
                                        ps[p0:p0 + m, b * CHUNK:b * CHUNK + HALF], ALU.mult).then_inc(s_eprod, 1)

            def h_lo(e, z):
                m = P if z % 2 == 0 else IR
                cols = slice((z // 2) * HALF, (z // 2 + 1) * HALF)
                dve.wait_ge(s_ehhi, 1 + 4 * e + z + 1)
                sub_rounded(nc.vector, EH[1][z % 2][0:m, cols], HF[0:m, z % 2, 0:HALF],
                            EH[0][z % 2][0:m, cols]).then_inc(s_ehlo, 1)

            def hidden(e):
                for z in range(4):
                    prod(e, z)
                    if z:
                        h_lo(e, z - 1)
                h_lo(e, 3)

            weights_up(0)
            weights_down(0)
            rows(0)
            with dve.Fori(0, E - 1) as e:
                hidden(e)
                rows(e + 1)
                weights_up(e + 1)
                weights_down(e + 1)
            hidden(E - 1)

            def combine(j, r):
                t, s = (NT // 2) * j + r, r % 4
                c = (NCH // 2) * j + r // CT
                x = X[:, bass.ds(t, 1), :]
                dve.wait_ge(s_gat[s], 32 * (2 * j + r // 4 + 1))
                dve.wait_ge(s_y, NCH // 2 + j)
                for k in range(TOP_K):
                    dve.wait_ge(s_comb, 1 + 2 * t + k)
                    nc.vector.scalar_tensor_tensor(out=x, in0=G[:, s, k, :], scalar=CW[:, bass.ds(c, 1), k * CT + r % CT],
                                                   in1=x, op0=ALU.mult, op1=ALU.add).then_inc(s_comb, 1)

            with dve.Fori(0, NCH // 2) as j:
                n = NCH // 2 + j
                for q in range(NJ):
                    dve_prod(dve, n, q)
                    if q:
                        dve_hlo(dve, n, q - 1)
                    if q >= 2:
                        combine(j, 2 * (q - 2))
                        combine(j, 2 * (q - 2) + 1)
                dve_hlo(dve, n, NJ - 1)
                dve.wait_ge(s_comb, 1 + NT * (j + 1))
                dve_y(dve, n)

        @block.tensor
        def _(pe):
            open_at_one(pe, s_edn, s_eup)

            def logitsT(c):
                pe.wait_ge(ln.s_lo, 2 * c + 2)
                for k in range(KD):
                    for z, m in enumerate((XT.hi, XT.lo)):
                        ins = nc.tensor.matmul(bank(LTB[c], p=64), RT[:, k, :], m[:, k, c * CHUNK:(c + 1) * CHUNK],
                                               start=(k == 0 and z == 0), stop=(k == KD - 1 and z == 1))
                ins.then_inc(s_ltp, 1)

            def logits(c):
                pe.wait_ge(s_lt, c + 1)
                for a in range(CT):
                    at = LGB[c] * CHUNK + a * E
                    ins = nc.tensor.matmul(ps[:, at:at + E], LT[:, c % 2, a * P:(a + 1) * P], C.fold[:], start=True, stop=True)
                ins.then_inc(s_lgp, 1)

            def positions(c):
                pe.wait_ge(s_chosen, c + 1)
                pe.wait_ge(s_rank, 6 * min(c, 1) + 1)
                if c:
                    pe.wait_ge(s_carry, c)
                u = c % 2
                for a in range(CT):
                    at = POB[c] * CHUNK + a * E
                    o = ps[:, at:at + E]
                    nc.tensor.matmul(o, C.before[:], M[u][:, a, :], start=True, stop=False)
                    for b in range(a):
                        nc.tensor.matmul(o, C.ones[:], M[u][:, b, :], start=False, stop=False)
                    ins = nc.tensor.matmul(o, C.ones[:], CARRY[u][:], start=False, stop=True)
                ins.then_inc(s_pos, 1)

            pe.wait_ge(s_rt, 3)
            if fill_xbuf:
                pe.wait_ge(s_const, 3)
            ln.transpose(nc, pe, C, ps, 0, TPB[0])
            ln.transpose(nc, pe, C, ps, 1, TPB[1])
            logitsT(0)
            logitsT(1)
            logits(0)
            logits(1)

            def slot(k, n, q):
                if q in (0, 2, 4) and n == 0:
                    pe.wait_ge(s_su_lo, q // 2 + 1)
                pe_up(pe, n, q)
                if k == 2:
                    pe.wait_ge(s_slot, 1 + 6)
                    ln.transpose(nc, pe, C, ps, 2, TPB[2])
                elif k == 3:
                    logitsT(2)
                elif k == 6:
                    logitsT(3)
                if k == 2:
                    pe.wait_ge(s_sd_lo, 2)
                    pe.wait_ge(s_rank, 6 + 1)
                if k >= 2:
                    pe_down(pe, (k - 2) // NJ, (k - 2) % NJ)
                if k == 1:
                    positions(0)
                    positions(1)
                elif k == 3:
                    logits(2)
                elif k == 4:
                    positions(2)
                elif k == 5:
                    pe.wait_ge(s_slot, 1 + 11)
                    pe.wait_ge(s_rank, 6 * 2 + 1)
                    ln.transpose(nc, pe, C, ps, 3, TPB[3])
                elif k == 6:
                    logits(3)
                elif k == 7:
                    positions(3)

            at_slot(slot)
            for q in range(NJ - 2, NJ):
                pe_down(pe, 1, q)

            def transposes(e):
                pe.wait_ge(s_xe, 16 * (e + 1))
                pe.wait_ge(s_ext_lo, 1 + 3 * e)
                for g, (s0, ns) in enumerate(TG):
                    for s in range(ns):
                        for k in range(KD):
                            at = (4 + g) * CHUNK + s * D + k * P
                            ins = nc.tensor.transpose(ps[:, at:at + P], XE[:, s0 + s, k * P:(k + 1) * P], C.ident[:])
                    ins.then_inc(s_etp, 1)

            def up(e):
                pe.wait_ge(s_ewu_lo, e + 1)
                pe.wait_ge(s_ext_lo, 1 + 3 * e + 3)
                for z, (col, m, b) in enumerate([(0, P, 0), (P, P, 1), (2 * P, 64 + IR, 2),
                                                 (0, P, 3), (P, P, 0), (2 * P, 64 + IR, 1)]):
                    h = z // 3
                    pe.wait_ge(s_eprod, 1 + 4 * e + (1 if z >= 4 else 0))
                    if z == 3:
                        pe.wait_ge(s_eo, 1 + ST * e)
                    for k in range(KD):
                        ins = matmul3(nc, bank(b, HALF, m), pair(WU, slice(None), k, slice(col, col + m)),
                                      pair(XET, slice(None), k, slice(h * HALF, (h + 1) * HALF)), k == 0, k == KD - 1)
                    ins.then_inc(s_eup, 1)

            def down(e):
                pe.wait_ge(s_ewd_lo, e + 1)
                pe.wait_ge(s_ehlo, 1 + 4 * e + 4)
                for s in range(ST):
                    pe.wait_ge(s_eo, 1 + ST * e + max(s - 1, 0))
                    o = bank(7 - 4 * (s % 2), D)
                    for i, m in enumerate((P, IR)):
                        ins = matmul3(nc, o, (EH[0][i][0:m, s * P:(s + 1) * P], EH[1][i][0:m, s * P:(s + 1) * P]),
                                      pair(WD, slice(0, m), i), i == 0, i == 1)
                    ins.then_inc(s_edn, 1)

            pe.wait_ge(s_prod, 2 * NJ)
            pe.wait_ge(s_y, 2)
            pe.wait_ge(s_slot, 1 + 5 * NCH)
            transposes(0)
            with pe.Fori(0, E - 1) as e:
                up(e)
                transposes(e + 1)
                down(e)
            up(E - 1)
            down(E - 1)
            pe.wait_ge(s_eo, 1 + ST * E)
            pe.wait_ge(s_eprod, 1 + 4 * E)
            with pe.Fori(NCH // 2, NCH) as n:
                for q in range(NJ):
                    pe_up(pe, n, q)
                    if q >= 2:
                        pe_down(pe, n, q - 2)
                for q in range(NJ - 2, NJ):
                    pe_down(pe, n, q)


def attention_block(sems, nc, tag, ps, C, X, io):
    T, D = X.shape[1] * P, X.shape[2]
    HD = io["L0_attn_Wq"].shape[1]
    NB, S = io["L0_attn_x"].shape[0:2]
    NH = HD // D_HEAD
    KD = D // P
    HG = 4
    NG = NH // HG
    NPAIR = NB // 2
    NIT = NG * NPAIR
    GW = HG * D_HEAD
    NCH = T // CHUNK
    SCALE = 1.0 / float(D_HEAD) ** 0.5
    assert 2 * S == CHUNK == GW and S == 2 * P and KD == 2 and NCH == NPAIR and D == 2 * P

    with ExitStack() as ctx:
        sb = lambda name, shape, dt=F32: ctx.enter_context(nc.sbuf_tensor(tag + name, shape, dt))
        sem = lambda name: sems.new(tag + name)
        ln = LayerNorm(ctx, sems, nc, tag, D, 2)
        XT = Split(ctx, nc, tag + "xT", [P, KD, T])
        XV = Split(ctx, nc, tag + "xT_pair", [P, KD, CHUNK])
        RK = sb("raw_k", [P, HG, KD, D_HEAD])
        RV = sb("raw_v", [P, KD, GW])
        RO = sb("raw_o", [P, HG, D])
        RQ = sb("raw_q", [P, 2, KD, CHUNK])
        WQ = Split(ctx, nc, tag + "wq", [P, KD, HD])
        WK = Split(ctx, nc, tag + "wk", [P, HG, KD, D_HEAD])
        WV = Split(ctx, nc, tag + "wv", [P, KD, GW])
        WO = Split(ctx, nc, tag + "wo", [P, HG, D])
        BIAS = sb("bias", [P, 3, NH])
        BROW = sb("bias_rows", [3 * NH, P])
        BO = sb("bo", [P, D])
        Q = Split(ctx, nc, tag + "q", [P, 2, HG * S])
        QF = sb("q_full", [P, 2, CHUNK])
        K = Split(ctx, nc, tag + "k", [P, CHUNK])
        V = Split(ctx, nc, tag + "v", [P, CT, GW])
        PR = sb("weights", [P, 2, 2, 3 * P])
        PT = Split(ctx, nc, tag + "weightsT", [P, 2, 3 * P])
        O = Split(ctx, nc, tag + "headT", [P, CHUNK])
        MX = sb("max", [P, 2, 3])
        NM = sb("neg_max", [P, 2, 2])
        SUM = sb("sum", [P, 2, 2])
        RS = sb("rsum", [P, 2, 2, 2])

        s_bias, s_bt, s_bcol = sem("bias_in"), sem("biasT_psum"), sem("bias_cols")
        s_rk = [sem(f"raw_k_in{j}") for j in range(HG)]
        s_wq_in = [sem(f"wq_in{u}") for u in range(2)]
        s_wq_hi, s_wq_lo = sem("wq_hi"), sem("wq_lo")
        s_rv, s_ro = sem("raw_v_in"), sem("raw_o_in")
        s_wk, s_wv, s_wo = sem("wk"), sem("wv"), sem("wo")
        s_bo = sem("bo_added")
        s_xv = sem("xv_in")
        s_sc = sem("scores")
        s_mx, s_nm = sem("max"), sem("neg_max")
        s_exp = sem("exp")
        s_rs = sem("rsum")
        s_norm = sem("norm")
        s_pt = sem("weightsT_psum")
        s_pt_hi, s_pt_lo = sem("weightsT_hi"), sem("weightsT_lo")
        s_pr, s_pr_hi, s_pr_lo = sem("proj_psum"), sem("proj_hi"), sem("proj_lo")
        s_qf = sem("q_full")
        s_eh = sem("out_steps")
        s_ya = sem("y_added")

        bank = lambda b, n=CHUNK: ps[:, b * CHUNK:b * CHUNK + n]
        SB, TB, YB, PB = (0, 1), (2, 3), 4, 6
        QB = HD // D_HEAD
        QT = S // QB
        NQ = QB * 2 * HG * QT // CHUNK
        QC = QB // NQ
        NPR = 2 * HG + CT + NQ
        assert NPR % 2 == 0 and HG == CT == NQ == 4

        def key_tile(it, j, first=False):
            return NQ + NPR * it + (0, 2 + CT, 4 + CT, 6 + CT)[j] + (first and j == 0)

        def query_tile(it):
            return 1 if isinstance(it, int) and it == 0 else NPR * it - 1

        def head_tile(it, j, last=False):
            return NQ + NPR * it + (1, 3 + CT, 5 + CT, 7 + CT + NQ)[j] - ((1 + NQ) * (last and j == HG - 1))

        def value_tile(it):
            return NQ + NPR * it + 2

        bank_of = lambda m: PB + m % 2
        q_full = lambda r: QF[:, r % 2, :].rearrange("p (c b i) -> p c b i", c=QC, b=2)
        q_cols = lambda q, r: q[:].rearrange("p b (i c) -> p c b i", c=QB)[:, r * QC:(r + 1) * QC]

        block = ctx.enter_context(nc.Block())

        @block.sync
        def _(sp):
            def load_k(g, j):
                sp.dma_start(RK[:, j, :, :], io["L0_attn_Wk"][:, bass.ds(g * GW + j * D_HEAD, D_HEAD)]
                             .rearrange("(k p) n -> p k n", p=P)).then_inc(s_rk[j], 16)

            def load_v(g):
                sp.dma_start(RV[:], io["L0_attn_Wv"][:, bass.ds(g * GW, GW)]
                             .rearrange("(k p) n -> p k n", p=P)).then_inc(s_rv, 16)

            def load_o(g):
                sp.dma_start(RO[:], io["L0_attn_Wo"][bass.ds(g * GW, GW), :]
                             .rearrange("(h p) n -> p h n", p=P)).then_inc(s_ro, 16)

            def load_pair(p):
                cols = bass.ds(p * CHUNK, CHUNK)
                for to, at in ((XV.hi, XT.hi), (XV.lo, XT.lo)):
                    sp.dma_start(to[:].bitcast(F32), at[:, :, cols].bitcast(F32)).then_inc(s_xv, 16)

            def load_q(r):
                sp.dma_start(RQ[:, r % 2, :, :], io["L0_attn_Wq"][:, r * QC * P:(r + 1) * QC * P]
                             .rearrange("(k p) n -> p k n", p=P)).then_inc(s_wq_in[r % 2], 16)

            load_q(0)
            load_q(1)
            for j in range(HG):
                load_k(0, j)
            load_v(0)
            load_o(0)
            for z, name in enumerate(("L0_attn_bq", "L0_attn_bk", "L0_attn_bv")):
                sp.dma_start(BROW[z * NH:(z + 1) * NH, :], io[name].rearrange("(h p) -> h p", p=P)).then_inc(s_bias, 16)
            sp.dma_start(BO[:], io["L0_attn_bo"][None, :].broadcast_to([P, D])).then_inc(s_bias, 16)
            for r in range(2, NQ):
                sp.wait_ge(s_wq_lo, r - 1)
                load_q(r)
            sp.wait_ge(ln.s_lo, 2)
            sp.wait_ge(ln.s_hi, 2)
            load_pair(0)

            def pairs(g, n):
                with sp.Fori(0, n) as p:
                    sp.wait_ge(s_pr, value_tile(NPAIR * g + p) + CT)
                    sp.wait_ge(ln.s_lo, 2 * NCH)
                    load_pair((p + 1) % NPAIR)

            with sp.Fori(0, NG - 1) as g:
                sp.wait_ge(s_wk, 2 * HG * (g + 1))
                for j in range(HG):
                    load_k(g + 1, j)
                sp.wait_ge(s_wv, 2 * (g + 1))
                load_v(g + 1)
                pairs(g, NPAIR)
                sp.wait_ge(s_wo, 2 * HG * (g + 1))
                load_o(g + 1)
            pairs(NG - 1, NPAIR - 1)
            sp.wait_ge(s_xv, 32 * NIT)

        @block.gpsimd
        def _(pool):
            def split(dst_hi, dst_lo, raw, sem, count):
                nc.gpsimd.tensor_copy(dst_hi, raw).then_inc(sem, 1)
                pool.wait_ge(sem, count + 1)
                sub_rounded(nc.gpsimd, dst_lo, raw, dst_hi).then_inc(sem, 1)

            def split_k(g, j):
                hold(pool, s_rk[j], 16 * (g + 1))
                split(WK.hi[:, j], WK.lo[:, j], RK[:, j], s_wk, 2 * (HG * g + j))

            def split_v(g):
                hold(pool, s_rv, 16 * (g + 1))
                split(WV.hi[:], WV.lo[:], RV[:], s_wv, 2 * g)

            def split_o(g, j):
                hold(pool, s_ro, 16 * (g + 1))
                split(WO.hi[:, j], WO.lo[:, j], RO[:, j], s_wo, 2 * (HG * g + j))

            def norms(n, u):
                for b in range(2):
                    hold(pool, s_rs, 2 * n + b + 1)
                    for t, cols in enumerate((slice(0, P), slice(P, 3 * P))):
                        nc.gpsimd.tensor_scalar(PR[:, u, b, cols], PR[:, u, b, cols], RS[:, u, b, t:t + 1], None,
                                                ALU.mult).then_inc(s_norm, 1)

            for i in range(NCH // 2):
                for u in range(2):
                    ln.inverse_root(nc.gpsimd, C, 2 * i + u)
                if i == 0:
                    for j in range(HG):
                        split_k(0, j)
                    split_v(0)
                for u in range(2):
                    c = 2 * i + u
                    pool.wait_ge(s_bias, 64)
                    pool.wait_ge(ln.s_xn, c + 1)
                    x = X[:, c * CT:(c + 1) * CT, :]
                    nc.gpsimd.tensor_tensor(x, x, BO[:, None, :].broadcast_to([P, CT, D]), ALU.add).then_inc(s_bo, 1)
            split_o(0, 0)

            def group(g, last):
                n0 = HG * NPAIR * g
                for j in range(HG):
                    norms(n0 + j, j % 2)
                    if j:
                        pool.wait_ge(s_eh, HG + n0 + j - HG + 1)
                        split_o(g, j)
                with pool.Fori(1, NPAIR - 1) as p:
                    for j in range(HG):
                        norms(n0 + HG * p + j, j % 2)
                for j in range(HG):
                    n = n0 + HG * (NPAIR - 1) + j
                    norms(n, j % 2)
                    if not last:
                        split_k(g + 1, j)
                        if j == 1:
                            split_v(g + 1)
                        if j == HG - 1:
                            pool.wait_ge(s_eh, HG + n - 2)
                            split_o(g + 1, 0)

            with pool.Fori(0, NG - 1) as g:
                group(g, False)
            group(NG - 1, True)

        @block.scalar
        def _(act):
            for i in range(NCH // 2):
                for r in range(i * NQ // 2, (i + 1) * NQ // 2):
                    act.wait_ge(s_wq_in[r % 2], 16 * (r // 2 + 1))
                    cols = slice(r * QC * P, (r + 1) * QC * P)
                    nc.scalar.activation(WQ.hi[:, :, cols], RQ[:, r % 2, :, :], ACT.Copy).then_inc(s_wq_hi, 1)
                for u in range(2):
                    ln.split_hi(nc, act, XT, ps, 2 * i + u, 4 + 2 * u)
            act.wait_ge(s_bcol, 1)

            def weightsT(n):
                for b in range(2):
                    act.wait_ge(s_pt, 2 * n + b + 1)
                    nc.scalar.activation(PT.hi[:, b, :], bank(TB[b], 3 * P), ACT.Copy).then_inc(s_pt_hi, 1)

            def exps(n, u):
                if not (isinstance(n, int) and n < 2):
                    act.wait_ge(s_pt, 2 * n - 2)
                hold(act, s_nm, n + 1)
                for b in range(2):
                    for t, cols in enumerate((slice(0, P), slice(P, 3 * P))):
                        src = bank(SB[b], 3 * P)[:, cols]
                        nc.scalar.activation(PR[:, u, b, cols], src, ACT.Exp, bias=NM[:, b, t:t + 1], scale=SCALE,
                                             accum_out=SUM[:, b, t:t + 1]).then_inc(s_exp, 1)

            def keys(m, b, h):
                hold(act, s_pr, m + 1)
                nc.scalar.activation(K.hi[:], bank(b), ACT.Identity, bias=BIAS[:, 1, bass.ds(h, 1)]).then_inc(s_pr_hi, 1)

            def queries(it):
                for r in range(NQ):
                    act.wait_ge(s_qf, NQ * it + r + 1)
                    nc.scalar.activation(q_cols(Q.hi, r), q_full(r), ACT.Copy).then_inc(s_pr_hi, 1)

            def head(m, b, h):
                hold(act, s_pr, m + 1)
                nc.scalar.activation(O.hi[:], bank(b), ACT.Identity, bias=BIAS[:, 2, bass.ds(h, 1)]).then_inc(s_pr_hi, 1)

            def values(it):
                for a in range(CT):
                    act.wait_ge(s_pr, value_tile(it) + a + 1)
                    nc.scalar.activation(V.hi[:, a, :], bank(bank_of(value_tile(0) + a)), ACT.Copy).then_inc(s_pr_hi, 1)

            def steps(it, first, last):
                g = it // NPAIR
                for j in range(HG):
                    n = HG * it + j
                    if not (first and j == 0):
                        weightsT(n - 1)
                    exps(n, j % 2)
                    if not (last and j == HG - 1):
                        keys(key_tile(it, j, first), bank_of(key_tile(0, j, first)),
                             g * HG + j + 1 if j < HG - 1 else ((it + 1) // NPAIR) * HG)
                        if j == HG - 1:
                            queries(it + 1)
                    if not (first and j == 0):
                        head(head_tile(it, j, last), bank_of(head_tile(0, j, last)),
                             g * HG + j - 1 if j else ((it - 1) // NPAIR) * HG + HG - 1)
                    if j == 0:
                        values(it)

            keys(0, bank_of(0), 0)
            queries(0)
            steps(0, True, False)
            with act.Fori(1, NIT - 1) as it:
                steps(it, False, False)
            steps(NIT - 1, False, True)
            weightsT(HG * NIT - 1)
            m = head_tile(NIT - 1, HG - 1, True) + 1
            head(m, bank_of(m), NH - 1)

        @block.vector
        def _(dve):
            for i in range(NCH // 2):
                for u in range(2):
                    ln.moments(nc.vector, X, 2 * i + u)
                for u in range(2):
                    ln.normalise(nc.vector, X, 2 * i + u)
                for u in range(2):
                    ln.split_lo(nc, dve, XT, ps, 2 * i + u, 4 + 2 * u)
                for r in range(i * NQ // 2, (i + 1) * NQ // 2):
                    cols = slice(r * QC * P, (r + 1) * QC * P)
                    dve.wait_ge(s_wq_hi, r + 1)
                    sub_rounded(nc.vector, WQ.lo[:, :, cols], RQ[:, r % 2, :, :],
                                WQ.hi[:, :, cols]).then_inc(s_wq_lo, 1)
            dve.wait_ge(s_bt, 1)
            nc.vector.tensor_copy(BIAS[:].rearrange("p z h -> p (z h)"), bank(TB[0], 3 * NH)).then_inc(s_bcol, 1)
            dve.wait_ge(s_bcol, 1)

            def weightsT(n):
                for b in range(2):
                    dve.wait_ge(s_pt_hi, 2 * n + b + 1)
                    sub_rounded(nc.vector, PT.lo[:, b, :], bank(TB[b], 3 * P), PT.hi[:, b, :]).then_inc(s_pt_lo, 1)

            def maxes(n):
                dve.wait_ge(s_sc, n + 1)
                nc.vector.tensor_reduce(MX[:], ps[:, 0:2 * CHUNK].rearrange("p (b n) -> p b n", b=2)[:, :, 0:3 * P]
                                        .rearrange("p b (t s) -> p b t s", s=P), AX_X, ALU.max).then_inc(s_mx, 1)
                dve.wait_ge(s_mx, 2 * n + 1)
                nc.vector.tensor_tensor(MX[:, :, 1], MX[:, :, 1], MX[:, :, 2], ALU.max).then_inc(s_mx, 1)
                dve.wait_ge(s_mx, 2 * n + 2)
                nc.vector.tensor_scalar(NM[:], MX[:, :, 0:2], -SCALE, None, ALU.mult).then_inc(s_nm, 1)

            def sums(n, u):
                for b in range(2):
                    dve.wait_ge(s_exp, 4 * n + 2 * b + 2)
                    nc.vector.reciprocal(RS[:, u, b, :], SUM[:, b, :]).then_inc(s_rs, 1)

            def biased_lo(m, lo, b, bias, hi):
                dve.wait_ge(s_pr_hi, m + 1)
                nc.vector.scalar_tensor_tensor(out=lo, in0=bank(b), scalar=bias, in1=hi.bitcast(F32),
                                               op0=ALU.add, op1=ALU.subtract).then_inc(s_pr_lo, 1)

            def query_bias(it, r):
                m = query_tile(it) + r
                dve.wait_ge(s_pr, m + 1)
                if not (isinstance(it, int) and it == 0 and r == 0):
                    dve.wait_ge(s_pr_lo, m - 1)
                nc.vector.tensor_tensor(QF[:, r % 2, :].rearrange("p (c t) -> p c t", c=QC),
                                        bank(bank_of(query_tile(0) + r)).rearrange("p (c t) -> p c t", c=QC),
                                        BIAS[:, 0, r * QC:(r + 1) * QC, None].broadcast_to([P, QC, CHUNK // QC]),
                                        ALU.add).then_inc(s_qf, 1)

            def queries(it):
                query_bias(it, 0)
                for r in range(NQ):
                    if r < NQ - 1:
                        query_bias(it, r + 1)
                    dve.wait_ge(s_pr_hi, query_tile(it) + r + 1)
                    sub_rounded(nc.vector, q_cols(Q.lo, r), q_full(r), q_cols(Q.hi, r)).then_inc(s_pr_lo, 1)

            def head(m, b, h):
                biased_lo(m, O.lo[:], b, BIAS[:, 2, bass.ds(h, 1)], O.hi[:])

            def values(it):
                for a in range(CT):
                    dve.wait_ge(s_pr_hi, value_tile(it) + a + 1)
                    sub_rounded(nc.vector, V.lo[:, a, :], bank(bank_of(value_tile(0) + a)), V.hi[:, a, :]).then_inc(s_pr_lo, 1)

            def add_y(it):
                if isinstance(it, int) and it == 0:
                    dve.wait_ge(s_bo, NCH)
                dve.wait_ge(s_eh, HG + HG * (it + 1))
                x = X[:, bass.ds((it % NPAIR) * CT, CT), :].rearrange("p c d -> p (c d)")
                nc.vector.tensor_tensor(x, x, ps[:, YB * CHUNK:(YB + 2) * CHUNK], ALU.add).then_inc(s_ya, 1)

            def keys(m, b, h):
                biased_lo(m, K.lo[:], b, BIAS[:, 1, bass.ds(h, 1)], K.hi[:])

            def steps(it, first, last):
                g = it // NPAIR
                for j in range(HG):
                    n = HG * it + j
                    maxes(n)
                    if not (first and j == 0):
                        weightsT(n - 1)
                    sums(n, j % 2)
                    if not (last and j == HG - 1):
                        keys(key_tile(it, j, first), bank_of(key_tile(0, j, first)),
                             g * HG + j + 1 if j < HG - 1 else ((it + 1) // NPAIR) * HG)
                        if j == HG - 1:
                            queries(it + 1)
                    if j == 1 and not first:
                        add_y(it - 1)
                    if not (first and j == 0):
                        head(head_tile(it, j, last), bank_of(head_tile(0, j, last)),
                             g * HG + j - 1 if j else ((it - 1) // NPAIR) * HG + HG - 1)
                    if j == 0:
                        values(it)

            keys(0, bank_of(0), 0)
            queries(0)
            steps(0, True, False)
            with dve.Fori(1, NIT - 1) as it:
                steps(it, False, False)
            steps(NIT - 1, False, True)
            weightsT(HG * NIT - 1)
            m = head_tile(NIT - 1, HG - 1, True) + 1
            head(m, bank_of(m), NH - 1)
            add_y(NIT - 1)

        @block.tensor
        def _(pe):
            open_at_one(pe, *[s_eh] * HG)
            pe.wait_ge(s_bias, 64)
            nc.tensor.transpose(bank(TB[0], 3 * NH), BROW[:], C.ident[0:3 * NH, 0:3 * NH]).then_inc(s_bt, 1)
            for i in range(NCH // 2):
                for u in range(2):
                    if i:
                        pe.wait_ge(ln.s_lo, 2 * (2 * i + u) - 2)
                    ln.transpose(nc, pe, C, ps, 2 * i + u, 4 + 2 * u)

            def scores(n, j, count):
                pe.wait_ge(s_pr_lo, count)
                if not (isinstance(n, int) and n == 0):
                    pe.wait_ge(s_exp, 4 * n)
                for b in range(2):
                    q = lambda t: pair(Q, slice(None), b, slice(j * S + t * P, j * S + (t + 1) * P))
                    k = lambda t: pair(K, slice(None), slice(b * S, b * S + (t + 1) * P))
                    for t in range(2):
                        at = SB[b] * CHUNK + t * P
                        o, width = ps[:, at:at + (t + 1) * P], (t + 1) * P
                        matmul3(nc, o, q(t), k(t), True, False)
                        ins = nc.tensor.matmul(o[:, width - P:width], C.ident_bf[:], C.causal[:], start=False, stop=True)
                ins.then_inc(s_sc, 1)

            def keys(m, b, j, p):
                if not (isinstance(m, int) and m == 0):
                    pe.wait_ge(s_pr_lo, m - 1)
                for k in range(KD):
                    ins = matmul3(nc, bank(b), pair(WK, slice(None), j, k),
                                  pair(XT, slice(None), k, bass.ds(p * CHUNK, CHUNK)), k == 0, k == KD - 1)
                ins.then_inc(s_pr, 1)

            def queries(it):
                m = query_tile(it)
                p, g = it % NPAIR, it // NPAIR
                xt = [a[:].rearrange("p k (q b g i) -> p k q b g i", q=NPAIR, b=2, g=NG) for a in (XT.hi, XT.lo)]
                for r in range(NQ):
                    if r >= 2:
                        pe.wait_ge(s_qf, NQ * it + r - 1)
                    elif not (isinstance(it, int) and it == 0 and r == 0):
                        pe.wait_ge(s_pr_lo, m + r - 1)
                    for c in range(QC):
                        o = bank(bank_of(query_tile(0) + r))[:, c * P:(c + 1) * P]
                        col = (r * QC + c) * P
                        for k in range(KD):
                            moving = tuple(a[:, k, bass.ds(p, 1), :, bass.ds(g, 1), :] for a in xt)
                            ins = matmul3(nc, o, pair(WQ, slice(None), k, slice(col, col + P)), moving,
                                          k == 0, k == KD - 1)
                    ins.then_inc(s_pr, 1)

            pe.wait_ge(s_bcol, 1)

            def head(n, j, m, b):
                pe.wait_ge(s_pt_lo, 2 * n + 2)
                pe.wait_ge(s_pr_lo, m - 1)
                for z in range(2):
                    v = lambda t: pair(V, slice(None), 2 * z + t, slice(j * D_HEAD, (j + 1) * D_HEAD))
                    o = bank(b)[:, z * S:(z + 1) * S]
                    matmul3(nc, o, v(0), pair(PT, slice(None), z, slice(0, S)), True, False)
                    ins = matmul3(nc, o[:, P:S], v(1), pair(PT, slice(None), z, slice(S, 3 * P)), False, True)
                ins.then_inc(s_pr, 1)

            def values(it):
                pe.wait_ge(s_xv, 32 * (it + 1))
                for a in range(CT):
                    m = value_tile(it) + a
                    pe.wait_ge(s_pr_lo, m - 1)
                    for k in range(KD):
                        ins = matmul3(nc, bank(bank_of(value_tile(0) + a)), pair(XV, slice(None), k, slice(a * P, (a + 1) * P)),
                                      pair(WV, slice(None), k), k == 0, k == KD - 1)
                    ins.then_inc(s_pr, 1)

            def transposes(n, u):
                if not (isinstance(n, int) and n == 0):
                    pe.wait_ge(s_pt_lo, 2 * n)
                for b in range(2):
                    pe.wait_ge(s_norm, 4 * n + 2 * b + 2)
                    for i in range(3):
                        at = TB[b] * CHUNK + i * P
                        ins = nc.tensor.transpose(ps[:, at:at + P], PR[:, u, b, i * P:(i + 1) * P], C.ident[:])
                    ins.then_inc(s_pt, 1)

            def outputs(n, j, m):
                pe.wait_ge(s_pr_lo, m + 1)
                for a in range(CT):
                    o = ps[:, YB * CHUNK + a * D:YB * CHUNK + (a + 1) * D]
                    ins = matmul3(nc, o, pair(O, slice(None), slice(a * P, (a + 1) * P)), pair(WO, slice(None), j),
                                  j == 0 and a % 2 == 0, j == HG - 1 and a % 2 == 1, skip_group_check=True)
                ins.then_inc(s_eh, 1)

            def steps(it, first, last):
                g = it // NPAIR
                for j in range(HG):
                    n = HG * it + j
                    scores(n, j, key_tile(it, j - 1, first) + 1 if j else query_tile(it) + NQ)
                    if not (first and j == 0):
                        transposes(n - 1, (j - 1) % 2)
                    if not (last and j == HG - 1):
                        m, b = key_tile(it, j, first), bank_of(key_tile(0, j, first))
                        if j < HG - 1:
                            pe.wait_ge(s_wk, 2 * (HG * g + j + 2))
                            keys(m, b, j + 1, it % NPAIR)
                        else:
                            pe.wait_ge(s_wk, 2 * (HG * ((it + 1) // NPAIR) + 1))
                            keys(m, b, 0, (it + 1) % NPAIR)
                            queries(it + 1)
                    if j >= 2:
                        if j == 2 and not first:
                            pe.wait_ge(s_ya, it)
                        pe.wait_ge(s_wo, 2 * (HG * g + j - 1))
                        outputs(n - 2, j - 2, head_tile(it, j - 1))
                    elif not first:
                        pe.wait_ge(s_wo, 2 * (HG * ((it - 1) // NPAIR) + j + 3))
                        outputs(n - 2, j + 2, head_tile(it, 0) if j else head_tile(it - 1, HG - 1))
                    if j == 1:
                        pe.wait_ge(s_pr_lo, value_tile(it) + CT)
                    if not (first and j == 0):
                        head(n - 1, (j - 1) % HG, head_tile(it, j, last), bank_of(head_tile(0, j, last)))
                    if j == 0:
                        pe.wait_ge(s_wv, 2 * (g + 1))
                        values(it)

            pe.wait_ge(s_wk, 2)
            pe.wait_ge(ln.s_lo, 2 * NCH)
            keys(0, bank_of(0), 0, 0)
            pe.wait_ge(s_wq_lo, NQ)
            queries(0)
            steps(0, True, False)
            with pe.Fori(1, NIT - 1) as it:
                steps(it, False, False)
            steps(NIT - 1, False, True)
            m = head_tile(NIT - 1, HG - 1, True)
            transposes(HG * NIT - 1, (HG - 1) % 2)
            outputs(HG * NIT - 2, HG - 2, m)
            head(HG * NIT - 1, HG - 1, m + 1, bank_of(m + 1))
            outputs(HG * NIT - 1, HG - 1, m + 1)


def macaron(nc, io, out):
    x = io["L0_attn_x"].rearrange("b t d -> (b t) d")
    T, D = x.shape
    w = {k: io["L0_ffn_" + k] for k in ("router", "w_up_gate", "w_down", "shared_w_up_gate", "shared_w_down")}
    E = w["router"].shape[1]
    CAP = -(-int(T * TOP_K * CAP_FACTOR) // E)
    o = out.rearrange("b t d -> (b t) d")
    xbuf = nc.dram_tensor("expert_in", (E * CAP, D), F32, kind="Internal").ap()
    ybuf = nc.dram_tensor("expert_out", (E * CAP, D), F32, kind="Internal").ap()
    with ExitStack() as ctx:
        ps = ctx.enter_context(nc.psum_tensor("ps", [P, 8 * CHUNK], F32))
        X = ctx.enter_context(nc.sbuf_tensor("x", [P, T // P, D], F32))
        C = Consts(ctx, nc, E)
        first_sems = Sems(nc)
        ffn_block(first_sems, nc, "f1_", ps, C, X, w, x, None, xbuf, ybuf, True)
        first_sems.clear()
        attention_block(Sems(nc), nc, "at_", ps, C, X, io)
        ffn_block(Sems(nc), nc, "f2_", ps, C, X, w, None, o, xbuf, ybuf, False)


_INS = ["L0_attn_x", "L0_attn_Wq", "L0_attn_bq", "L0_attn_Wk", "L0_attn_bk", "L0_attn_Wv", "L0_attn_bv",
        "L0_attn_Wo", "L0_attn_bo", "L0_ffn_router", "L0_ffn_w_up_gate", "L0_ffn_w_down",
        "L0_ffn_shared_w_up_gate", "L0_ffn_shared_w_down"]


def kernel(**inputs):
    import numpy as _np
    import concourse.bacc as _bacc
    from concourse import mybir as _mybir
    from concourse.bass_utils import run_bass_kernel_spmd as _run

    nc = _bacc.Bacc("TRN2", target_bir_lowering=False, num_devices=1)
    arrays, io = {}, {}
    for name in _INS:
        a = _np.ascontiguousarray(inputs[name])
        arrays["in_" + name] = a
        io[name] = nc.dram_tensor("in_" + name, a.shape, _mybir.dt.from_np(a.dtype), kind="ExternalInput").ap()
    out = nc.dram_tensor("out", arrays["in_L0_attn_x"].shape, _mybir.dt.float32, kind="ExternalOutput").ap()
    macaron(nc, io, out)
    r = _run(nc, [arrays], core_ids=[0])
    return r.results[0]["out"]
```

```python
from contextlib import ExitStack

import concourse.bass as bass
from concourse import mybir

P = 128
F32 = mybir.dt.float32
F32R = mybir.dt.float32r
BF16 = mybir.dt.bfloat16
U32 = mybir.dt.uint32
ALU = mybir.AluOpType
ACT = mybir.ActivationFunctionType
AX_X = mybir.AxisListType.X

LN_EPS = 1e-5
MASKED = -3.0e38
CHUNK = 512
CT = CHUNK // P
CAP_FACTOR = 1.25
TOP_K = 2
D_HEAD = 128


class Split:

    def __init__(self, ctx, nc, name, shape):
        self.hi = ctx.enter_context(nc.sbuf_tensor(name + "_hi", shape, F32R))
        self.lo = ctx.enter_context(nc.sbuf_tensor(name + "_lo", shape, F32R))


def matmul3(nc, out, stationary, moving, first, last, **kw):
    (s_hi, s_lo), (m_hi, m_lo) = stationary, moving
    nc.tensor.matmul(out, s_hi, m_hi, start=first, stop=False, **kw)
    nc.tensor.matmul(out, s_hi, m_lo, start=False, stop=False, **kw)
    return nc.tensor.matmul(out, s_lo, m_hi, start=False, stop=last, **kw)


def pair(split, *at):
    return split.hi[at], split.lo[at]


def sub_rounded(eng, out_lo, full, hi):
    return eng.tensor_tensor(out_lo, full, hi.bitcast(F32), ALU.subtract)


def open_at_one(eng, *sems):
    for s in sems:
        eng.nop().then_inc(s, 1)


def wait_past(eng, sem, count):
    if not (isinstance(count, int) and count <= 0):
        eng.wait_ge(sem, count)


def hold(eng, sem, value):
    eng.wait_ge(sem, value)
    eng.nop(nofuse=True)


class Consts:

    def __init__(self, ctx, nc, n_experts):
        sb = lambda name, shape, dt: ctx.enter_context(nc.sbuf_tensor(name, shape, dt))
        self.ident = sb("ident", [P, P], F32)
        self.ident_bf = sb("ident_bf", [P, P], BF16)
        self.before = sb("before", [P, P], BF16)
        self.ones = sb("ones", [P, P], BF16)
        self.causal = sb("causal", [P, P], BF16)
        self.fold = sb("fold", [64, n_experts], F32)
        self.expert_id = sb("expert_id", [P, n_experts], F32)
        self.minus_half = sb("minus_half", [P, CT], F32)
        self.zeros = sb("zeros", [P, 2 * P], F32)

    def build(self, pool, sem):
        E = self.expert_id.shape[1]
        pool.memset(self.ident[:], 0.0)
        pool.memset(self.ident_bf[:], 0.0)
        pool.memset(self.before[:], 1.0)
        pool.memset(self.ones[:], 1.0)
        pool.memset(self.causal[:], 0.0)
        pool.memset(self.fold[:], 0.0)
        pool.memset(self.minus_half[:], -0.5)
        pool.iota(self.expert_id[:], pattern=[[1, E]], base=0, channel_multiplier=0,
                  allow_small_or_imprecise_dtypes=True)
        pool.memset(self.zeros[:], 0.0).then_inc(sem, 1)
        pool.wait_ge(sem, 1)
        for m in (self.ident, self.ident_bf):
            pool.affine_select(out=m[:], in_=m[:], compare_op=ALU.not_equal, fill=1.0, base=0,
                               pattern=[[-1, P]], channel_multiplier=1)
        pool.affine_select(out=self.before[:], in_=self.before[:], compare_op=ALU.is_gt, fill=0.0,
                           base=0, pattern=[[1, P]], channel_multiplier=-1)
        pool.affine_select(out=self.causal[:], in_=self.causal[:], compare_op=ALU.is_ge, fill=MASKED,
                           base=0, pattern=[[-1, P]], channel_multiplier=1)
        pool.affine_select(out=self.fold[:], in_=self.fold[:], compare_op=ALU.not_equal, fill=1.0,
                           base=0, pattern=[[-1, E]], channel_multiplier=1).then_inc(sem, 1)
        pool.wait_ge(sem, 2)
        pool.affine_select(out=self.fold[:], in_=self.fold[:], compare_op=ALU.not_equal, fill=1.0,
                           base=-32, pattern=[[-1, E]], channel_multiplier=1).then_inc(sem, 1)


class Sems:

    def __init__(self, nc):
        self.nc, self.all = nc, []

    def new(self, name):
        self.all.append(self.nc.alloc_semaphore(name))
        return self.all[-1]

    def clear(self):
        self.nc.clear_and_free_semaphores(self.all)
        self.nc.all_engine_barrier()


class LayerNorm:

    def __init__(self, ctx, sems, nc, tag, D, n_xn, xn_ctx=None):
        sb = lambda name, shape: ctx.enter_context(nc.sbuf_tensor(tag + name, shape, F32))
        self.stats = [sb(f"stats{u}", [P, CT, 6]) for u in range(2)]
        self.mean_var = [sb(f"mean_var{u}", [P, CT, 2]) for u in range(2)]
        self.var_eps = [sb(f"var_eps{u}", [P, CT]) for u in range(2)]
        self.rstd = [sb(f"rstd{u}", [P, CT]) for u in range(2)]
        self.xn = [(xn_ctx or ctx).enter_context(nc.sbuf_tensor(f"{tag}xn{u}", [P, CT, D], F32)) for u in range(n_xn)]
        sem = lambda name: sems.new(tag + name)
        self.s_step = sem("ln_step")
        self.s_rstd = sem("ln_rstd")
        self.s_xn = sem("ln_xn")
        self.s_tp = sem("xT_psum")
        self.s_hi = sem("xT_hi")
        self.s_lo = sem("xT_lo")
        self.KD = D // P

    def moments(self, dve, X, c):
        u = c % 2
        for a in range(CT):
            ins = dve.bn_stats(self.stats[u][:, a, :], X[:, c * CT + a, :])
        ins.then_inc(self.s_step, 1)
        dve.wait_ge(self.s_step, 3 * c + 1)
        for a in range(CT):
            ins = dve.bn_aggr(self.mean_var[u][:, a, :], self.stats[u][:, a, :])
        ins.then_inc(self.s_step, 1)
        dve.wait_ge(self.s_step, 3 * c + 2)
        dve.tensor_scalar(self.var_eps[u][:], self.mean_var[u][:, :, 1], LN_EPS, None,
                          ALU.add).then_inc(self.s_step, 1)

    def normalise(self, dve, X, c):
        u = c % 2
        if c >= len(self.xn):
            dve.wait_ge(self.s_tp, 2 * (c - len(self.xn) + 1))
        dve.wait_ge(self.s_rstd, c + 1)
        for a in range(CT):
            ins = dve.tensor_scalar(self.xn[c % len(self.xn)][:, a, :], X[:, c * CT + a, :],
                                    self.mean_var[u][:, a, 0:1], self.rstd[u][:, a:a + 1],
                                    ALU.subtract, ALU.mult)
        ins.then_inc(self.s_xn, 1)

    def inverse_root(self, pool, consts, c):
        pool.wait_ge(self.s_step, 3 * c + 3)
        pool.tensor_tensor(self.rstd[c % 2][:], self.var_eps[c % 2][:], consts.minus_half[:],
                           ALU.pow).then_inc(self.s_rstd, 1)

    def transpose(self, nc, pe, consts, ps, c, bank):
        pe.wait_ge(self.s_xn, c + 1)
        for k in range(self.KD):
            for a in range(CT):
                at = (bank + k) * CHUNK + a * P
                xn = self.xn[c % len(self.xn)]
                ins = nc.tensor.transpose(ps[:, at:at + P], xn[:, a, k * P:(k + 1) * P], consts.ident[:])
            ins.then_inc(self.s_tp, 1)

    def split_hi(self, nc, act, XT, ps, c, bank):
        for k in range(self.KD):
            act.wait_ge(self.s_tp, 2 * c + k + 1)
            b = (bank + k) * CHUNK
            nc.scalar.activation(XT.hi[:, k, c * CHUNK:(c + 1) * CHUNK], ps[:, b:b + CHUNK], ACT.Copy).then_inc(self.s_hi, 1)

    def split_lo(self, nc, dve, XT, ps, c, bank):
        for k in range(self.KD):
            dve.wait_ge(self.s_hi, 2 * c + k + 1)
            b = (bank + k) * CHUNK
            cols = slice(c * CHUNK, (c + 1) * CHUNK)
            sub_rounded(nc.vector, XT.lo[:, k, cols], ps[:, b:b + CHUNK], XT.hi[:, k, cols]).then_inc(self.s_lo, 1)


def ffn_block(sems, nc, tag, ps, C, X, w, x_in, out, xbuf, ybuf, fill_xbuf):
    D, E = w["router"].shape
    I = w["w_down"].shape[1]
    J = w["shared_w_down"].shape[0]
    NT = X.shape[1]
    T = NT * P
    NCH = NT // CT
    KD = D // P
    CAP = -(-int(T * TOP_K * CAP_FACTOR) // E)
    ST = CAP // P
    assert CAP % P == 0 and KD == 2 and NCH % 2 == 0
    JF, JR = J // P, J % P
    NJ = JF + 1
    IR = I - P
    UPW = 2 * P + 64 + IR
    HALF = CAP // 2
    NOSLOT = 4 * E * CAP
    UPS = 2 * NJ - 1
    GB = 8
    HS = 3
    SUG = NJ // 2

    with ExitStack() as ctx:
        sb = lambda name, shape, dt=F32: ctx.enter_context(nc.sbuf_tensor(tag + name, shape, dt))
        sem = lambda name: sems.new(tag + name)
        ln = LayerNorm(ctx, sems, nc, tag, D, NCH)
        XT = Split(ctx, nc, tag + "xT", [P, KD, T])
        raw_up = sb("raw_up", [P, KD, 2 * J])
        raw_dn = sb("raw_down", [P, NJ, D])
        SU = Split(ctx, nc, tag + "sh_up", [P, KD, 2 * J])
        SD = Split(ctx, nc, tag + "sh_down", [P, NJ, D])
        raw_r = sb("raw_router", [P, KD, E])
        RT = sb("router", [P, KD, 64], F32R)
        H = Split(ctx, nc, tag + "hidden", [P, HS * CHUNK])
        SG = sb("silu", [P, 2, CHUNK])
        HF = sb("prod", [P, 2, CHUNK])
        SILU0 = sb("silu_of_0", [P, 1])
        LT = sb("logitsT", [64, 2, CHUNK])
        LG = sb("logits", [P, CT, E])
        TOP = sb("top8", [P, CT, 8])
        IX = sb("top8_ix", [P, CT, 8], U32)
        IXF = sb("expert_of", [P, TOP_K, CT])
        OH = [sb(f"onehot{u}", [P, TOP_K * CT, E]) for u in range(2)]
        BASE = [sb(f"slot_base{u}", [P, TOP_K * CT]) for u in range(2)]
        M = [sb(f"chosen{u}", [P, CT, E], BF16) for u in range(2)]
        CARRY = [sb(f"carry{c}", [P, E], BF16) for c in range(NCH)]
        MS = sb("chosen_sum", [P, E])
        PK = sb("pos", [P, TOP_K * CT])
        POS = sb("onehot_pos", [P, TOP_K * CT, E])
        OVER = sb("over", [P, TOP_K * CT])
        SLOT = sb("slot", [P, TOP_K * CT])
        SCI = [sb(f"scatter_ix{c}", [P, TOP_K * CT], U32) for c in range(NCH)]
        GIX = sb("gather_ix_all", [P, NCH, TOP_K * CT], U32)
        VALID = sb("valid", [P, NCH, TOP_K * CT])
        GAP = sb("gap", [P, NCH, CT])
        CW = sb("combine_w", [P, NCH, TOP_K * CT])
        G = sb("gathered", [P, GB, TOP_K, D])
        raw_wu = sb("raw_wu", [P, KD, UPW])
        raw_wd = sb("raw_wd", [P, 2, D])
        WU = Split(ctx, nc, tag + "ex_up", [P, KD, UPW])
        WD = Split(ctx, nc, tag + "ex_down", [P, 2, D])
        XE = sb("ex_rows", [P, ST, D])
        XET = Split(ctx, nc, tag + "ex_xT", [P, KD, CAP])
        OE = sb("ex_out", [P, ST, D])

        s_const = sem("const")
        s_x = [sem(f"x{c}") for c in range(NCH)]
        s_wr = sem("w_router")
        s_wu_raw, s_wd_raw = sem("sh_up_raw"), sem("sh_down_raw")
        s_fill = sem("fill")
        s_rt = sem("router_split")
        s_su_hi, s_su_lo = sem("sh_up_hi"), sem("sh_up_lo")
        s_su_late = sem("sh_up_lo_late")
        s_sd_hi, s_sd_lo = sem("sh_down_hi"), sem("sh_down_lo")
        s_ltp, s_lt, s_lgp = sem("logitsT_psum"), sem("logitsT"), sem("logits_psum")
        s_rank, s_chosen = sem("rank"), sem("chosen")
        s_carry = sem("carry")
        s_pos, s_slot = sem("pos_psum"), sem("slot")
        s_scat = [sem(f"scatter{c}") for c in range(NCH)]
        s_up = sem("up_psum")
        s_sg, s_prod, s_hhi, s_hlo = sem("silu"), sem("prod"), sem("h_hi"), sem("h_lo")
        s_dn, s_y = sem("down_psum"), sem("y")
        s_ex_pad = sem("ex_pad")
        s_ewu, s_ewd, s_xe = sem("ex_wu_raw"), sem("ex_wd_raw"), sem("ex_rows")
        s_ewu_hi, s_ewu_lo, s_ewd_hi, s_ewd_lo = sem("ex_wu_hi"), sem("ex_wu_lo"), sem("ex_wd_hi"), sem("ex_wd_lo")
        s_etp, s_ext_hi, s_ext_lo = sem("ex_xT_psum"), sem("ex_xT_hi"), sem("ex_xT_lo")
        s_eup = sem("ex_up_psum")
        s_esg, s_eprod, s_ehhi, s_ehlo = sem("ex_silu"), sem("ex_prod"), sem("ex_h_hi"), sem("ex_h_lo")
        s_edn, s_eo = sem("ex_down_psum"), sem("ex_out")
        s_ybuf = sem("ybuf")
        s_oe_free = sem("oe_free")
        s_exp, s_cw = sem("gap_exp"), sem("combine_w")
        s_gat = [sem(f"gather{s}") for s in range(GB)]
        s_comb = sem("combined")
        s_out = sem("out")

        bank = lambda b, n=CHUNK, p=P: ps[0:p, b * CHUNK:b * CHUNK + n]
        EH = [[m[:, i * CAP:(i + 1) * CAP] for i in range(2)] for m in (H.hi, H.lo)]
        hcols = lambda q: slice(q % HS * CHUNK, (q % HS + 1) * CHUNK)
        assert NJ % HS == 0 and NJ % 2 == 0 and 2 * CAP <= HS * CHUNK
        jrows = lambda q: P if q < JF else JR
        TG = [(0, 2), (2, 2), (4, 1)]
        EOB = (7, 3, 0, 1, 2)
        assert ST == 5
        TPB, LTB, LGB, POB = (6, 4, 6, 6), (6, 4, 6, 6), (7, 5, 7, 7), (6, 7, 6, 6)
        upc = 2 * (2 * P)
        assert NCH == 4 and 2 * NJ >= 12 and SUG == 3

        def pe_up(pe, n, q):
            wait_past(pe, s_prod, NJ * n + q - 1)
            tiles = [(q * 2 * P, P, 2 * (q % 2)), (q * 2 * P + P, P, 2 * (q % 2) + 1)] if q < JF else \
                    [(q * 2 * P, 2 * JR, 2 * (q % 2))]
            for col, m, b in tiles:
                for k in range(KD):
                    ins = matmul3(nc, bank(b, p=m), pair(SU, slice(None), k, slice(col, col + m)),
                                  pair(XT, slice(None), k, bass.ds(n * CHUNK, CHUNK)),
                                  k == 0, k == KD - 1)
                ins.then_inc(s_up, 1)

        def pe_down(pe, n, q):
            pe.wait_ge(s_hlo, NJ * n + q + 1)
            if q == 0:
                wait_past(pe, s_y, n)
            m = jrows(q)
            for a in range(CT):
                cols = slice(q % HS * CHUNK + a * P, q % HS * CHUNK + (a + 1) * P)
                ins = matmul3(nc, ps[:, 4 * CHUNK + a * D:4 * CHUNK + (a + 1) * D], pair(H, slice(0, m), cols),
                              pair(SD, slice(0, m), q), q == 0 and a % 2 == 0, q == NJ - 1 and a % 2 == 1,
                              skip_group_check=True)
            ins.then_inc(s_dn, 1)

        def act_silu(act, n, q):
            act.wait_ge(s_up, UPS * n + 2 * q + 1)
            wait_past(act, s_prod, NJ * n + q - 1)
            m = jrows(q)
            nc.scalar.activation(SG[0:m, q % 2, :], bank(2 * (q % 2), p=m), ACT.Silu).then_inc(s_sg, 1)

        def act_hhi(act, n, q):
            wait_past(act, s_dn, NJ * n + q - HS + 1)
            act.wait_ge(s_prod, NJ * n + q + 1)
            m = jrows(q)
            nc.scalar.activation(H.hi[0:m, hcols(q)], HF[0:m, q % 2, :], ACT.Copy).then_inc(s_hhi, 1)

        def dve_prod(dve, n, q):
            dve.wait_ge(s_sg, NJ * n + q + 1)
            dve.wait_ge(s_up, UPS * n + min(2 * q + 2, UPS))
            wait_past(dve, s_hlo, NJ * n + q - 1)
            b = 2 * (q % 2)
            up = ps[0:P, (b + 1) * CHUNK:(b + 2) * CHUNK] if q < JF else ps[JR:2 * JR, b * CHUNK:(b + 1) * CHUNK]
            m = jrows(q)
            nc.vector.tensor_tensor(HF[0:m, q % 2, :], SG[0:m, q % 2, :], up, ALU.mult).then_inc(s_prod, 1)

        def dve_hlo(dve, n, q):
            dve.wait_ge(s_hhi, NJ * n + q + 1)
            m = jrows(q)
            sub_rounded(nc.vector, H.lo[0:m, hcols(q)], HF[0:m, q % 2, :],
                        H.hi[0:m, hcols(q)]).then_inc(s_hlo, 1)

        def dve_y(dve, n):
            dve.wait_ge(s_dn, NJ * (n + 1))
            x = X[:, bass.ds(n * CT, CT), :].rearrange("p c d -> p (c d)")
            nc.vector.scalar_tensor_tensor(out=x, in0=ps[:, 4 * CHUNK:6 * CHUNK], scalar=0.5, in1=x,
                                           op0=ALU.mult, op1=ALU.add).then_inc(s_y, 1)

        def at_slot(engine_slot, n0=0):
            for k in range(2 * NJ):
                engine_slot(k, n0 + k // NJ, k % NJ)

        def up_cols(g):
            return slice(g * upc, min((g + 1) * upc, 2 * J))

        block = ctx.enter_context(nc.Block())

        @block.sync
        def _(sp):
            def load_x(c):
                if x_in is not None:
                    sp.dma_start(X[:, c * CT:(c + 1) * CT, :],
                                 x_in[c * CHUNK:(c + 1) * CHUNK, :].rearrange("(a p) d -> p a d", p=P)).then_inc(s_x[c], 16)

            load_x(0)
            sp.dma_start(raw_r[:], w["router"].rearrange("(k p) e -> p k e", p=P)).then_inc(s_wr, 16)
            load_x(1)
            for k in range(KD):
                for z in range(2):
                    src = w["shared_w_up_gate"][k * P:(k + 1) * P, z * J:(z + 1) * J]
                    sp.dma_start(raw_up[:, k, 0:2 * P * JF].rearrange("p (j z n) -> p j z n", z=2, n=P)[:, :, z, :],
                                 src[:, 0:P * JF].rearrange("p (j n) -> p j n", n=P)).then_inc(s_wu_raw, 16)
                    sp.dma_start(raw_up[:, k, 2 * P * JF + z * JR:2 * P * JF + (z + 1) * JR],
                                 src[:, P * JF:J]).then_inc(s_wu_raw, 16)
            load_x(2)
            load_x(3)
            sp.dma_start(raw_dn[:, 0:JF, :], w["shared_w_down"][0:JF * P, :].rearrange("(j p) d -> p j d", p=P)
                         ).then_inc(s_wd_raw, 16)
            sp.dma_start(raw_dn[0:JR, JF, :], w["shared_w_down"][JF * P:J, :]).then_inc(s_wd_raw, 16)
            if fill_xbuf:
                sp.wait_ge(s_const, 1)
                rows = E * CAP // P
                half = rows // 2
                for z in range(2):
                    sp.dma_start(xbuf[z * half * P:(z + 1) * half * P, :].rearrange("(p r) d -> p r d", p=P),
                                 C.zeros[:, None, :].broadcast_to([P, half, D])).then_inc(s_fill, 16)

            def load_up(e):
                src = w["w_up_gate"][bass.ds(e, 1), :, :].rearrange("a (k p) n -> p (a k) n", p=P)
                for dst, at, n in ((0, 0, P), (P, I, P), (2 * P, P, IR), (2 * P + 64, I + P, IR)):
                    sp.dma_start(raw_wu[:, :, dst:dst + n], src[:, :, at:at + n]).then_inc(s_ewu, 16)

            def load_down(e):
                src = w["w_down"][bass.ds(e, 1), :, :].rearrange("a i d -> (a i) d")
                sp.dma_start(raw_wd[:, 0, :], src[0:P, :]).then_inc(s_ewd, 16)
                sp.dma_start(raw_wd[0:IR, 1, :], src[P:I, :]).then_inc(s_ewd, 16)

            def load_rows(e):
                sp.dma_start(XE[:], xbuf[bass.ds(e * CAP, CAP), :].rearrange("(s p) d -> p s d", p=P)).then_inc(s_xe, 16)

            sp.wait_ge(s_ex_pad, 2)
            load_up(0)
            load_down(0)
            for c in range(NCH):
                sp.wait_ge(s_scat[c], 16 * TOP_K * CT)
            load_rows(0)
            with sp.Fori(0, E - 1) as e:
                sp.wait_ge(s_etp, 3 * e + 3)
                load_rows(e + 1)
                sp.wait_ge(s_ewu_hi, e + 1)
                sp.wait_ge(s_ewu_lo, e + 1)
                load_up(e + 1)
                sp.wait_ge(s_ewd_hi, e + 1)
                sp.wait_ge(s_ewd_lo, e + 1)
                load_down(e + 1)
            if out is not None:
                dst = out.rearrange("(c p) d -> p c d", p=P)
                for t0, t1 in ((0, NT // 2), (NT // 2, NT - CT), (NT - CT, NT)):
                    sp.wait_ge(s_comb, 2 * t1)
                    if t1 == NT:
                        sp.wait_ge(s_y, NCH)
                    sp.dma_start(dst[:, t0:t1, :], X[:, t0:t1, :]).then_inc(s_out, 16)
                sp.wait_ge(s_out, 48)

        @block.gpsimd
        def _(pool):
            open_at_one(pool, s_oe_free)
            if fill_xbuf:
                C.build(pool, s_const)
                pool.wait_ge(s_const, 3)
            nc.gpsimd.memset(raw_wu[:, :, 2 * P:UPW], 0.0).then_inc(s_ex_pad, 1)
            nc.gpsimd.memset(raw_wd[:, 1, :], 0.0).then_inc(s_ex_pad, 1)
            ln.inverse_root(nc.gpsimd, C, 0)
            ln.inverse_root(nc.gpsimd, C, 1)

            def up_lo(g):
                pool.wait_ge(s_su_hi, g + 1)
                sub_rounded(nc.gpsimd, SU.lo[:, :, up_cols(g)], raw_up[:, :, up_cols(g)],
                            SU.hi[:, :, up_cols(g)]).then_inc(s_su_late, 1)

            up_lo(1)
            pool.wait_ge(s_sd_hi, 2)
            sub_rounded(nc.gpsimd, SD.lo[:, 0:JF, :], raw_dn[:, 0:JF, :], SD.hi[:, 0:JF, :]).then_inc(s_sd_lo, 1)
            sub_rounded(nc.gpsimd, SD.lo[0:JR, JF, :], raw_dn[0:JR, JF, :], SD.hi[0:JR, JF, :]).then_inc(s_sd_lo, 1)
            ln.inverse_root(nc.gpsimd, C, 2)
            up_lo(2)
            if fill_xbuf:
                pool.wait_ge(s_fill, 32)
            for c in range(NCH):
                pool.wait_ge(s_slot, 1 + 5 * c + 5)
                for k in range(TOP_K):
                    for a in range(CT):
                        z = k * CT + a
                        nc.gpsimd.indirect_dma_start(
                            out=xbuf, out_offset=bass.IndirectOffsetOnAxis(ap=SCI[c][:, z:z + 1], axis=0),
                            in_=ln.xn[c][:, a, :], in_offset=None,
                            bounds_check=E * CAP - 1, oob_is_err=False).then_inc(s_scat[c], 16)
                if c == 0:
                    ln.inverse_root(nc.gpsimd, C, 3)

            def weights_up(e):
                pool.wait_ge(s_ewu_hi, e + 1)
                sub_rounded(nc.gpsimd, WU.lo[:], raw_wu[:], WU.hi[:]).then_inc(s_ewu_lo, 1)

            def expert(e):
                pool.wait_ge(s_ewd_hi, e + 1)
                sub_rounded(nc.gpsimd, WD.lo[:], raw_wd[:], WD.hi[:]).then_inc(s_ewd_lo, 1)
                if not isinstance(e, int):
                    weights_up(e + 1)
                pool.wait_ge(s_ybuf, 16 * (e + 1))
                pool.nop().then_inc(s_oe_free, 1)

            weights_up(0)
            with pool.Fori(0, E - 1) as e:
                expert(e)
            expert(E - 1)
            for t in range(NT):
                wait_past(pool, s_comb, 2 * (t // 2 * 2 - GB + 2))
                for k in range(TOP_K):
                    nc.gpsimd.indirect_dma_start(
                        out=G[:, t % GB, k, :], out_offset=None, in_=ybuf,
                        in_offset=bass.IndirectOffsetOnAxis(ap=GIX[:, t // CT, k * CT + t % CT:k * CT + t % CT + 1], axis=0),
                        bounds_check=E * CAP - 1, oob_is_err=True).then_inc(s_gat[t % GB], 16)

        @block.scalar
        def _(act):
            open_at_one(act, *[s_eo] * 3, s_ehhi)

            def split_hi(dst, src):
                return nc.scalar.activation(dst, src, ACT.Copy)

            def up_hi(g):
                act.wait_ge(s_wu_raw, 16 * 4 * KD)
                split_hi(SU.hi[:, :, up_cols(g)], raw_up[:, :, up_cols(g)]).then_inc(s_su_hi, 1)

            def logits(c):
                act.wait_ge(s_ltp, c + 1)
                nc.scalar.activation(LT[:, c % 2, :], bank(LTB[c], p=64), ACT.Copy).then_inc(s_lt, 1)

            ln.split_hi(nc, act, XT, ps, 0, TPB[0])
            ln.split_hi(nc, act, XT, ps, 1, TPB[1])
            up_hi(0)
            logits(0)
            logits(1)
            up_hi(1)

            def slot(k, n, q):
                act_silu(act, n, q)
                if k == 0:
                    act.wait_ge(s_wd_raw, 32)
                    split_hi(SD.hi[:, 0:JF, :], raw_dn[:, 0:JF, :]).then_inc(s_sd_hi, 1)
                    split_hi(SD.hi[0:JR, JF, :], raw_dn[0:JR, JF, :]).then_inc(s_sd_hi, 1)
                    up_hi(2)
                if k:
                    act_hhi(act, (k - 1) // NJ, (k - 1) % NJ)
                if k in (4, 7):
                    logits({4: 2, 7: 3}[k])
                if k in (3, 6):
                    c = {3: 2, 6: 3}[k]
                    ln.split_hi(nc, act, XT, ps, c, TPB[c])

            at_slot(slot)
            act_hhi(act, 1, NJ - 1)
            act.wait_ge(s_slot, 1 + 5 * NCH)
            nc.scalar.activation(GAP[:], GAP[:], ACT.Exp).then_inc(s_exp, 1)
            nc.scalar.activation(SILU0[:], C.zeros[:, 0:1], ACT.Silu)

            def weights_up(e):
                act.wait_ge(s_ewu, 64 * (e + 1))
                act.wait_ge(s_eup, 1 + 6 * e)
                split_hi(WU.hi[:], raw_wu[:]).then_inc(s_ewu_hi, 1)

            def weights_down(e):
                act.wait_ge(s_ewd, 32 * (e + 1))
                act.wait_ge(s_edn, 1 + ST * e)
                split_hi(WD.hi[:], raw_wd[:]).then_inc(s_ewd_hi, 1)

            def rows(e):
                for g, (s0, ns) in enumerate(TG):
                    act.wait_ge(s_etp, 3 * e + g + 1)
                    src = bank(4 + g, ns * D).rearrange("p (s k t) -> p k s t", k=KD, t=P)
                    dst = XET.hi[:, :, s0 * P:(s0 + ns) * P].rearrange("p k (s t) -> p k s t", t=P)
                    split_hi(dst, src).then_inc(s_ext_hi, 1)

            def silu(e, z):
                m = P if z % 2 == 0 else IR
                act.wait_ge(s_eup, 1 + 6 * e + (1, 3, 4, 6)[z])
                act.wait_ge(s_eprod, 1 + 4 * e + max(z - 1, 0))
                nc.scalar.activation(SG[0:m, z % 2, 0:HALF], bank((0, 2, 3, 1)[z], HALF, m), ACT.Silu).then_inc(s_esg, 1)

            def h_hi(e, z):
                m = P if z % 2 == 0 else IR
                if z == 0:
                    act.wait_ge(s_edn, 1 + ST * e)
                act.wait_ge(s_eprod, 1 + 4 * e + z + 1)
                cols = slice((z // 2) * HALF, (z // 2 + 1) * HALF)
                split_hi(EH[0][z % 2][0:m, cols], HF[0:m, z % 2, 0:HALF]).then_inc(s_ehhi, 1)

            def hidden(e):
                for z in range(4):
                    silu(e, z)
                    if z:
                        h_hi(e, z - 1)
                    if z == 1:
                        weights_down(e)
                h_hi(e, 3)

            def outs(e):
                act.wait_ge(s_oe_free, 1 + e)
                for s in range(ST):
                    act.wait_ge(s_edn, 1 + ST * e + s + 1)
                    nc.scalar.activation(OE[:, s, :], bank(EOB[s], D), ACT.Copy).then_inc(s_eo, 1)
                act.wait_ge(s_eo, 3 + ST * (e + 1))
                act.dma_start(ybuf[bass.ds(e * CAP, CAP), :].rearrange("(s p) d -> p s d", p=P), OE[:]).then_inc(s_ybuf, 16)

            weights_up(0)
            rows(0)
            with act.Fori(0, E - 1) as e:
                hidden(e)
                weights_up(e + 1)
                rows(e + 1)
                outs(e)
            hidden(E - 1)
            outs(E - 1)
            act.wait_ge(s_edn, 1 + ST * E)

            def late_slot(k, n, q):
                act_silu(act, n, q)
                if k:
                    act_hhi(act, 2 + (k - 1) // NJ, (k - 1) % NJ)

            at_slot(late_slot, 2)
            act_hhi(act, NCH - 1, NJ - 1)

        @block.vector
        def _(dve):
            open_at_one(dve, s_eprod, s_ehlo, s_ext_lo, s_slot)
            def moments(c):
                if x_in is not None:
                    dve.wait_ge(s_x[c], 16)
                ln.moments(nc.vector, X, c)

            def rank(c, u):
                dve.wait_ge(s_lgp, c + 1)
                lg = bank(LGB[c], CT * E).rearrange("p (a e) -> p a e", e=E)
                nc.vector.tensor_copy(LG[:], lg).then_inc(s_rank, 1)
                hold(dve, s_rank, 6 * c + 1)
                for a in range(CT):
                    ins = nc.vector.max(TOP[:, a, :], LG[:, a, :])
                ins.then_inc(s_rank, 1)
                hold(dve, s_rank, 6 * c + 2)
                for a in range(CT):
                    ins = nc.vector.max_index(IX[:, a, :], TOP[:, a, :], LG[:, a, :])
                ins.then_inc(s_rank, 1)
                nc.vector.tensor_tensor(GAP[:, c, :], TOP[:, :, 1], TOP[:, :, 0], ALU.subtract)
                dve.wait_ge(s_rank, 6 * c + 3)
                nc.vector.tensor_copy(IXF[:], IX[:, :, 0:TOP_K].rearrange("p a k -> p k a")).then_inc(s_rank, 1)
                dve.wait_ge(s_rank, 6 * c + 4)
                ixf = IXF[:].rearrange("p k a -> p (k a)")
                nc.vector.tensor_scalar(BASE[u][:], ixf, float(CAP), None, ALU.mult)
                nc.vector.tensor_tensor(OH[u][:], C.expert_id[:, None, :].broadcast_to([P, TOP_K * CT, E]),
                                        ixf[:, :, None].broadcast_to([P, TOP_K * CT, E]), ALU.is_equal).then_inc(s_rank, 1)
                dve.wait_ge(s_rank, 6 * c + 5)
                nc.vector.tensor_tensor(M[u][:], OH[u][:, 0:CT, :], OH[u][:, CT:2 * CT, :], ALU.add).then_inc(s_chosen, 1)
                dve.wait_ge(s_chosen, c + 1)
                nc.vector.tensor_reduce(MS[:], M[u][:].rearrange("p a e -> p e a"), AX_X, ALU.add).then_inc(s_rank, 1)
                if c < NCH - 1:
                    dve.wait_ge(s_rank, 6 * c + 6)
                    nc.vector.tensor_tensor(CARRY[c + 1][:], CARRY[c][:], MS[:], ALU.add).then_inc(s_carry, 1)

            def slots(c, u):
                dve.wait_ge(s_pos, c + 1)
                pos = bank(POB[c], CT * E).rearrange("p (a e) -> p a e", e=E)
                nc.vector.tensor_tensor(POS[:].rearrange("p (k a) e -> p k a e", a=CT),
                                        OH[u][:].rearrange("p (k a) e -> p k a e", a=CT),
                                        pos[:, None, :, :].broadcast_to([P, TOP_K, CT, E]), ALU.mult).then_inc(s_slot, 1)
                dve.wait_ge(s_slot, 1 + 5 * c + 1)
                nc.vector.tensor_reduce(PK[:], POS[:], AX_X, ALU.add).then_inc(s_slot, 1)
                dve.wait_ge(s_slot, 1 + 5 * c + 2)
                nc.vector.tensor_scalar(OVER[:], PK[:], float(CAP), float(NOSLOT), ALU.is_ge, ALU.mult)
                nc.vector.tensor_scalar(VALID[:, c, :], PK[:], float(CAP), None, ALU.is_lt)
                nc.vector.scalar_tensor_tensor(out=SLOT[:], in0=PK[:], scalar=float(CAP - 1), in1=BASE[u][:],
                                               op0=ALU.min, op1=ALU.add).then_inc(s_slot, 1)
                dve.wait_ge(s_slot, 1 + 5 * c + 3)
                nc.vector.tensor_copy(GIX[:, c, :], SLOT[:]).then_inc(s_slot, 1)
                nc.vector.tensor_tensor(SCI[c][:], SLOT[:], OVER[:], ALU.add).then_inc(s_slot, 1)

            moments(0)
            moments(1)
            ln.normalise(nc.vector, X, 0)
            ln.normalise(nc.vector, X, 1)
            nc.vector.memset(RT[:].bitcast(F32), 0.0)
            nc.vector.memset(CARRY[0][:], 0.0).then_inc(s_rt, 1)
            dve.wait_ge(s_rt, 1)
            dve.wait_ge(s_wr, 16)
            nc.vector.tensor_copy(RT[:, :, 0:E], raw_r[:]).then_inc(s_rt, 1)
            dve.wait_ge(s_rt, 2)
            sub_rounded(nc.vector, RT[:, :, 32:32 + E], raw_r[:], RT[:, :, 0:E]).then_inc(s_rt, 1)
            ln.split_lo(nc, dve, XT, ps, 0, TPB[0])
            ln.split_lo(nc, dve, XT, ps, 1, TPB[1])
            dve.wait_ge(s_su_hi, 1)
            sub_rounded(nc.vector, SU.lo[:, :, up_cols(0)], raw_up[:, :, up_cols(0)], SU.hi[:, :, up_cols(0)]
                        ).then_inc(s_su_lo, 1)
            rank(0, 0)
            rank(1, 1)

            def slot(k, n, q):
                if k == 5:
                    rank(2, 0)
                elif k == 6:
                    slots(2, 0)
                elif k == 7:
                    ln.split_lo(nc, dve, XT, ps, 3, TPB[3])
                elif k == 8:
                    dve_y(dve, 0)
                    rank(3, 1)
                elif k == 9:
                    slots(3, 1)
                dve_prod(dve, n, q)
                if k:
                    dve_hlo(dve, (k - 1) // NJ, (k - 1) % NJ)
                if k == 0:
                    moments(2)
                elif k == 1:
                    slots(0, 0)
                    slots(1, 1)
                elif k == 2:
                    ln.normalise(nc.vector, X, 2)
                elif k == 3:
                    ln.split_lo(nc, dve, XT, ps, 2, TPB[2])
                    moments(3)
                elif k == 5:
                    ln.normalise(nc.vector, X, 3)

            at_slot(slot)
            dve_hlo(dve, 1, NJ - 1)
            dve_y(dve, 1)

            gap = GAP[:].rearrange("p c a -> p (c a)")
            inv = LG[:].rearrange("p a e -> p (a e)")[:, 0:NT]
            dve.wait_ge(s_exp, 1)
            nc.vector.tensor_scalar(inv, gap, 1.0, None, ALU.add).then_inc(s_cw, 1)
            dve.wait_ge(s_cw, 1)
            nc.vector.reciprocal(inv, inv).then_inc(s_cw, 1)
            dve.wait_ge(s_cw, 2)
            inv_c = inv.rearrange("p (c a) -> p c a", a=CT)
            nc.vector.scalar_tensor_tensor(out=CW[:, :, 0:CT], in0=inv_c, scalar=0.5, in1=VALID[:, :, 0:CT],
                                           op0=ALU.mult, op1=ALU.mult)
            nc.vector.tensor_tensor(gap, gap, inv, ALU.mult).then_inc(s_cw, 1)
            dve.wait_ge(s_cw, 3)
            nc.vector.scalar_tensor_tensor(out=CW[:, :, CT:2 * CT], in0=GAP[:], scalar=0.5, in1=VALID[:, :, CT:2 * CT],
                                           op0=ALU.mult, op1=ALU.mult).then_inc(s_cw, 1)

            def rows(e):
                for g, (s0, ns) in enumerate(TG):
                    dve.wait_ge(s_ext_hi, 3 * e + g + 1)
                    cols = slice(s0 * P, (s0 + ns) * P)
                    src = bank(4 + g, ns * D).rearrange("p (s k t) -> p k s t", k=KD, t=P)
                    hi, lo = (m[:, :, cols].rearrange("p k (s t) -> p k s t", t=P) for m in (XET.hi, XET.lo))
                    sub_rounded(nc.vector, lo, src, hi).then_inc(s_ext_lo, 1)

            def prod(e, z):
                m = P if z % 2 == 0 else IR
                dve.wait_ge(s_esg, 4 * e + z + 1)
                dve.wait_ge(s_eup, 1 + 6 * e + (2, 3, 5, 6)[z])
                dve.wait_ge(s_ehhi, 1 + 4 * e + max(z - 1, 0))
                dve.wait_ge(s_ehlo, 1 + 4 * e + max(z - 1, 0))
                b, p0 = ((1, 0), (2, 64), (0, 0), (1, 64))[z]
                nc.vector.tensor_tensor(HF[0:m, z % 2, 0:HALF], SG[0:m, z % 2, 0:HALF],
                                        ps[p0:p0 + m, b * CHUNK:b * CHUNK + HALF], ALU.mult).then_inc(s_eprod, 1)

            def h_lo(e, z):
                m = P if z % 2 == 0 else IR
                cols = slice((z // 2) * HALF, (z // 2 + 1) * HALF)
                dve.wait_ge(s_ehhi, 1 + 4 * e + z + 1)
                sub_rounded(nc.vector, EH[1][z % 2][0:m, cols], HF[0:m, z % 2, 0:HALF],
                            EH[0][z % 2][0:m, cols]).then_inc(s_ehlo, 1)

            def hidden(e):
                for z in range(4):
                    prod(e, z)
                    if z:
                        h_lo(e, z - 1)
                h_lo(e, 3)

            rows(0)
            with dve.Fori(0, E - 1) as e:
                hidden(e)
                rows(e + 1)
            hidden(E - 1)

            def combine(tiles):
                for k in range(TOP_K):
                    for t in tiles:
                        if k == 0:
                            dve.wait_ge(s_gat[t % GB], 32 * (t // GB + 1))
                            if t // CT < NCH - 1:
                                dve.wait_ge(s_y, t // CT + 1)
                        else:
                            dve.wait_ge(s_comb, 2 * tiles[0] + tiles.index(t) + 1)
                        x = X[:, t, :]
                        nc.vector.scalar_tensor_tensor(out=x, in0=G[:, t % GB, k, :], in1=x, op0=ALU.mult, op1=ALU.add,
                                                       scalar=CW[:, t // CT, k * CT + t % CT:k * CT + t % CT + 1]
                                                       ).then_inc(s_comb, 1)

            def late_slot(k, n, q):
                dve_prod(dve, n, q)
                if k:
                    dve_hlo(dve, 2 + (k - 1) // NJ, (k - 1) % NJ)
                if k == NJ + 1:
                    dve_y(dve, 2)
                if 3 <= k < 11:
                    combine((2 * (k - 3), 2 * (k - 3) + 1))

            dve.wait_ge(s_cw, 4)
            at_slot(late_slot, 2)
            dve_hlo(dve, NCH - 1, NJ - 1)
            dve.wait_ge(s_comb, 2 * NT)
            dve_y(dve, NCH - 1)

        @block.tensor
        def _(pe):
            open_at_one(pe, s_edn, s_eup)

            def logitsT(c):
                pe.wait_ge(ln.s_lo, 2 * c + 2)
                for k in range(KD):
                    for z, m in enumerate((XT.hi, XT.lo)):
                        ins = nc.tensor.matmul(bank(LTB[c], p=64), RT[:, k, :], m[:, k, c * CHUNK:(c + 1) * CHUNK],
                                               start=(k == 0 and z == 0), stop=(k == KD - 1 and z == 1))
                ins.then_inc(s_ltp, 1)

            def logits(c):
                pe.wait_ge(s_lt, c + 1)
                for a in range(CT):
                    at = LGB[c] * CHUNK + a * E
                    ins = nc.tensor.matmul(ps[:, at:at + E], LT[:, c % 2, a * P:(a + 1) * P], C.fold[:], start=True, stop=True)
                ins.then_inc(s_lgp, 1)

            def positions(c):
                pe.wait_ge(s_chosen, c + 1)
                pe.wait_ge(s_rank, 6 * min(c, 1) + 1)
                if c:
                    pe.wait_ge(s_carry, c)
                u = c % 2
                for a in range(CT):
                    at = POB[c] * CHUNK + a * E
                    o = ps[:, at:at + E]
                    nc.tensor.matmul(o, C.before[:], M[u][:, a, :], start=True, stop=False)
                    for b in range(a):
                        nc.tensor.matmul(o, C.ones[:], M[u][:, b, :], start=False, stop=False)
                    ins = nc.tensor.matmul(o, C.ones[:], CARRY[c][:], start=False, stop=True)
                ins.then_inc(s_pos, 1)

            if fill_xbuf:
                pe.wait_ge(s_const, 3)
            ln.transpose(nc, pe, C, ps, 0, TPB[0])
            ln.transpose(nc, pe, C, ps, 1, TPB[1])
            pe.wait_ge(s_rt, 3)
            logitsT(0)
            logitsT(1)
            logits(0)
            logits(1)

            def slot(k, n, q):
                if k == 0:
                    pe.wait_ge(s_su_lo, 1)
                elif k in (2, 4):
                    pe.wait_ge(s_su_late, k // 2)
                pe_up(pe, n, q)
                if k == 3:
                    pe.wait_ge(s_slot, 1 + 6)
                    ln.transpose(nc, pe, C, ps, 2, TPB[2])
                elif k == 4:
                    logitsT(2)
                elif k == 7:
                    logitsT(3)
                if k == 2:
                    pe.wait_ge(s_sd_lo, 2)
                    pe.wait_ge(s_rank, 6 + 1)
                if k >= 2:
                    pe_down(pe, (k - 2) // NJ, (k - 2) % NJ)
                if k == 1:
                    positions(0)
                    positions(1)
                elif k == 4:
                    logits(2)
                elif k == 5:
                    positions(2)
                elif k == 6:
                    pe.wait_ge(s_slot, 1 + 11)
                    pe.wait_ge(s_rank, 6 * 2 + 1)
                    ln.transpose(nc, pe, C, ps, 3, TPB[3])
                elif k == 7:
                    logits(3)
                elif k == 8:
                    positions(3)

            at_slot(slot)
            for q in range(NJ - 2, NJ):
                pe_down(pe, 1, q)

            def transposes(e):
                pe.wait_ge(s_xe, 16 * (e + 1))
                pe.wait_ge(s_ext_lo, 1 + 3 * e)
                for g, (s0, ns) in enumerate(TG):
                    for s in range(ns):
                        for k in range(KD):
                            at = (4 + g) * CHUNK + s * D + k * P
                            ins = nc.tensor.transpose(ps[:, at:at + P], XE[:, s0 + s, k * P:(k + 1) * P], C.ident[:])
                    ins.then_inc(s_etp, 1)

            def up(e):
                pe.wait_ge(s_ewu_lo, e + 1)
                pe.wait_ge(s_ext_lo, 1 + 3 * e + 3)
                for z, (col, m, b) in enumerate([(0, P, 0), (P, P, 1), (2 * P, 64 + IR, 2),
                                                 (0, P, 3), (P, P, 0), (2 * P, 64 + IR, 1)]):
                    h = z // 3
                    pe.wait_ge(s_eprod, 1 + 4 * e + (1 if z >= 4 else 0))
                    if z < 3:
                        pe.wait_ge(s_eo, 3 + ST * e - 2 + z)
                    for k in range(KD):
                        ins = matmul3(nc, bank(b, HALF, m), pair(WU, slice(None), k, slice(col, col + m)),
                                      pair(XET, slice(None), k, slice(h * HALF, (h + 1) * HALF)), k == 0, k == KD - 1)
                    ins.then_inc(s_eup, 1)

            def down(e):
                pe.wait_ge(s_ewd_lo, e + 1)
                for s in range(ST):
                    if s == 0:
                        pe.wait_ge(s_ehlo, 1 + 4 * e + 2)
                    elif (s + 1) * P > HALF >= s * P:
                        pe.wait_ge(s_ehlo, 1 + 4 * e + 4)
                    o = bank(EOB[s], D)
                    for i, m in enumerate((P, IR)):
                        ins = matmul3(nc, o, (EH[0][i][0:m, s * P:(s + 1) * P], EH[1][i][0:m, s * P:(s + 1) * P]),
                                      pair(WD, slice(0, m), i), i == 0, i == 1)
                    ins.then_inc(s_edn, 1)

            pe.wait_ge(s_prod, 2 * NJ)
            pe.wait_ge(s_y, 2)
            pe.wait_ge(s_slot, 1 + 5 * NCH)
            transposes(0)
            with pe.Fori(0, E - 1) as e:
                up(e)
                transposes(e + 1)
                down(e)
            up(E - 1)
            down(E - 1)
            pe.wait_ge(s_eo, 3 + ST * E)
            pe.wait_ge(s_eprod, 1 + 4 * E)

            def late_slot(k, n, q):
                pe_up(pe, n, q)
                if k >= 2:
                    pe_down(pe, 2 + (k - 2) // NJ, (k - 2) % NJ)

            at_slot(late_slot, 2)
            for q in range(NJ - 2, NJ):
                pe_down(pe, NCH - 1, q)


def attention_block(sems, nc, tag, ps, C, X, io):
    T, D = X.shape[1] * P, X.shape[2]
    HD = io["L0_attn_Wq"].shape[1]
    NB, S = io["L0_attn_x"].shape[0:2]
    NH = HD // D_HEAD
    KD = D // P
    HG = 4
    NG = NH // HG
    NPAIR = NB // 2
    NW = 2
    SL = HG * NW
    RG = NPAIR // NW
    NR = NG * RG
    GW = HG * D_HEAD
    NCH = T // CHUNK
    SCALE = 1.0 / float(D_HEAD) ** 0.5
    assert 2 * S == CHUNK == GW and S == 2 * P and KD == 2 and NCH == NPAIR and D == 2 * P

    with ExitStack() as ctx:
        sb = lambda name, shape, dt=F32: ctx.enter_context(nc.sbuf_tensor(tag + name, shape, dt))
        sem = lambda name: sems.new(tag + name)
        setup = ExitStack()
        ln = LayerNorm(ctx, sems, nc, tag, D, 2, setup)
        RQ = setup.enter_context(nc.sbuf_tensor(tag + "raw_q", [P, 2, KD, CHUNK], F32))
        setup.close()
        V = Split(ctx, nc, tag + "v", [P, CT, GW])
        XT = Split(ctx, nc, tag + "xT", [P, KD, T])
        XV = Split(ctx, nc, tag + "xT_pair", [P, KD, CHUNK])
        RK = sb("raw_k", [P, HG, KD, D_HEAD])
        RV = sb("raw_v", [P, KD, GW])
        RO = sb("raw_o", [P, HG, D])
        WQ = Split(ctx, nc, tag + "wq", [P, KD, HD])
        WK = Split(ctx, nc, tag + "wk", [P, HG, KD, D_HEAD])
        WV = Split(ctx, nc, tag + "wv", [P, KD, GW])
        WO = Split(ctx, nc, tag + "wo", [P, HG, D])
        BIAS = sb("bias", [P, 3, NH])
        BROW = sb("bias_rows", [3 * NH, P])
        BO = sb("bo", [P, D])
        Q = Split(ctx, nc, tag + "q", [P, NW, 2, HG * S])
        QS = 2
        QF = sb("q_full", [P, QS, CHUNK])
        K = Split(ctx, nc, tag + "k", [P, CHUNK])
        PR = sb("weights", [P, 2, 2, 3 * P])
        PT = Split(ctx, nc, tag + "weightsT", [P, 2, 3 * P])
        O = Split(ctx, nc, tag + "headT", [P, 2, CHUNK])
        EXP0 = sb("exp_of_0", [P, 1])
        MX = sb("max", [P, 2, 3])
        NM = sb("neg_max", [P, 2, 2])
        SUM = sb("sum", [P, 2, 2])
        RS = sb("rsum", [P, 2, 2, 2])

        s_bo_in = sem("bo_in")
        s_bias, s_bt, s_bcol = sem("bias_in"), sem("biasT_psum"), sem("bias_cols")
        s_rk = [sem(f"raw_k_in{j}") for j in range(HG)]
        s_wq_in = [sem(f"wq_in{u}") for u in range(2)]
        s_wq_hi, s_wq_lo, s_wq_lo_late = sem("wq_hi"), sem("wq_lo"), sem("wq_lo_late")
        s_rv, s_ro = sem("raw_v_in"), sem("raw_o_in")
        s_wk, s_wv, s_wo = sem("wk"), sem("wv"), sem("wo")
        s_bo = sem("bo_added")
        s_xv = sem("xv_in")
        s_sc = sem("scores")
        s_mx, s_nm = sem("max"), sem("neg_max")
        s_exp = sem("exp")
        s_rs = sem("rsum")
        s_norm = (sem("norm0"), sem("norm1"))
        s_pt = sem("weightsT_psum")
        s_pt_hi, s_pt_lo = sem("weightsT_hi"), sem("weightsT_lo")
        s_pr, s_pr_hi, s_pr_lo = sem("proj_psum"), sem("proj_hi"), sem("proj_lo")
        s_qf = sem("q_full")
        s_eh = sem("out_steps")
        s_ya = sem("y_added")

        bank = lambda b, n=CHUNK: ps[:, b * CHUNK:b * CHUNK + n]
        SB, TB, YB, PB = (0, 1), (2, 3), 4, 6
        LNB = (4, 0, 2, 4)
        QB = HD // D_HEAD
        QT = S // QB
        NQ = QB * 2 * NW * HG * QT // CHUNK
        QC = QB // NQ
        NPR = 2 * SL + NW * CT + NQ
        QR = HD // CHUNK
        assert NPR % 2 == 0 and NW == 2 and NQ == 2 * QR

        def key_tile(d, s, first=False):
            return NQ + NPR * d + 2 * s + CT * ((s > 0) + (s > HG)) + (first and s == 0)

        def query_tile(d):
            return 1 if isinstance(d, int) and d == 0 else key_tile(d - 1, SL - 1) + 1

        def head_tile(d, s, last=False):
            if s < SL - 1:
                return key_tile(d, s) + 1
            return key_tile(d, s) + (0 if last else 1 + NQ)

        def value_tile(d, w):
            return key_tile(d, w * HG) + 2

        bank_of = lambda m: PB + m % 2

        def head_of(d, s):
            if s < 0:
                return ((d - 1) // RG) * HG + HG - 1
            if s == SL:
                return ((d + 1) // RG) * HG
            return (d // RG) * HG + s % HG

        q_quarter = lambda r: slice(r * CHUNK, (r + 1) * CHUNK)
        q_full = lambda r: QF[:, r % QS, :].rearrange("p (c b i) -> p c b i", c=QC, b=2 * NW)
        q_cols = lambda q, r: q[:].rearrange("p w b (i c) -> p c (w b) i", c=QB)[:, r * QC:(r + 1) * QC]

        block = ctx.enter_context(nc.Block())

        @block.sync
        def _(sp):
            def load_k(g, j):
                sp.dma_start(RK[:, j, :, :], io["L0_attn_Wk"][:, bass.ds(g * GW + j * D_HEAD, D_HEAD)]
                             .rearrange("(k p) n -> p k n", p=P)).then_inc(s_rk[j], 16)

            def load_v(g):
                sp.dma_start(RV[:], io["L0_attn_Wv"][:, bass.ds(g * GW, GW)]
                             .rearrange("(k p) n -> p k n", p=P)).then_inc(s_rv, 16)

            def load_o(g):
                sp.dma_start(RO[:], io["L0_attn_Wo"][bass.ds(g * GW, GW), :]
                             .rearrange("(h p) n -> p h n", p=P)).then_inc(s_ro, 16)

            def load_pair(p):
                cols = bass.ds(p * CHUNK, CHUNK)
                for to, at in ((XV.hi, XT.hi), (XV.lo, XT.lo)):
                    sp.dma_start(to[:].bitcast(F32), at[:, :, cols].bitcast(F32)).then_inc(s_xv, 16)

            def load_q(r):
                sp.dma_start(RQ[:, r % 2, :, :], io["L0_attn_Wq"][:, q_quarter(r)]
                             .rearrange("(k p) n -> p k n", p=P)).then_inc(s_wq_in[r % 2], 16)

            load_q(0)
            load_k(0, 0)
            for z, name in enumerate(("L0_attn_bq", "L0_attn_bk", "L0_attn_bv")):
                sp.dma_start(BROW[z * NH:(z + 1) * NH, :], io[name].rearrange("(h p) -> h p", p=P)).then_inc(s_bias, 16)
            load_q(1)
            for j in range(1, HG):
                load_k(0, j)
            load_v(0)
            sp.dma_start(BO[:], io["L0_attn_bo"][None, :].broadcast_to([P, D])).then_inc(s_bo_in, 16)
            load_o(0)
            for r in range(2, QR):
                sp.wait_ge(s_wq_lo, r - 1)
                load_q(r)
            sp.wait_ge(ln.s_lo, 2)
            sp.wait_ge(ln.s_hi, 2)
            load_pair(0)

            def next_pairs(g, n):
                for p in range(n):
                    sp.wait_ge(s_pr, value_tile(RG * g + p // NW, p % NW) + CT)
                    sp.wait_ge(ln.s_lo, 2 * NCH)
                    load_pair((p + 1) % NPAIR)

            with sp.Fori(0, NG - 1) as g:
                sp.wait_ge(s_wk, 2 * HG * (g + 1))
                for j in range(HG):
                    load_k(g + 1, j)
                sp.wait_ge(s_wv, 2 * (g + 1))
                load_v(g + 1)
                next_pairs(g, NPAIR)
                sp.wait_ge(s_wo, 2 * HG * (g + 1))
                load_o(g + 1)
            next_pairs(NG - 1, NPAIR - 1)
            sp.wait_ge(s_xv, 32 * NW * NR)

        @block.gpsimd
        def _(pool):
            def split(dst_hi, dst_lo, raw, sem, count):
                nc.gpsimd.tensor_copy(dst_hi, raw).then_inc(sem, 1)
                pool.wait_ge(sem, count + 1)
                sub_rounded(nc.gpsimd, dst_lo, raw, dst_hi).then_inc(sem, 1)

            def split_k(g, j):
                hold(pool, s_rk[j], 16 * (g + 1))
                split(WK.hi[:, j], WK.lo[:, j], RK[:, j], s_wk, 2 * (HG * g + j))

            def split_v(g):
                hold(pool, s_rv, 16 * (g + 1))
                split(WV.hi[:], WV.lo[:], RV[:], s_wv, 2 * g)

            def split_o(g, j):
                hold(pool, s_ro, 16 * (g + 1))
                split(WO.hi[:, j], WO.lo[:, j], RO[:, j], s_wo, 2 * (HG * g + j))

            def norms(n, u):
                hold(pool, s_rs, 2 * n + 1)
                for t, cols in enumerate((slice(0, P), slice(P, 3 * P))):
                    nc.gpsimd.tensor_scalar(PR[:, u, 0, cols], PR[:, u, 0, cols], RS[:, u, 0, t:t + 1], None,
                                            ALU.mult).then_inc(s_norm[0], 1)

            ln.inverse_root(nc.gpsimd, C, 0)
            ln.inverse_root(nc.gpsimd, C, 1)
            split_k(0, 0)
            for r in range(QR // 2, QR):
                pool.wait_ge(s_wq_hi, r + 1)
                sub_rounded(nc.gpsimd, WQ.lo[:, :, q_quarter(r)], RQ[:, r % 2, :, :], WQ.hi[:, :, q_quarter(r)]
                            ).then_inc(s_wq_lo_late, 1)
                ln.inverse_root(nc.gpsimd, C, r)
            split_k(0, 1)
            split_v(0)
            split_k(0, 2)
            split_k(0, 3)

            def add_bo(c):
                pool.wait_ge(s_bo_in, 16)
                pool.wait_ge(ln.s_xn, c + 1)
                x = X[:, c * CT:(c + 1) * CT, :]
                nc.gpsimd.tensor_tensor(x, x, BO[:, None, :].broadcast_to([P, CT, D]), ALU.add).then_inc(s_bo, 1)

            def group(g, first, last):
                n0 = HG * NPAIR * g
                for j in range(HG):
                    norms(n0 + j, j % 2)
                    if first and j == 0:
                        split_o(0, 0)
                    if j:
                        pool.wait_ge(s_eh, HG + n0 + j - HG + 1)
                        split_o(g, j)
                    if first:
                        add_bo(j)
                with pool.Fori(1, NPAIR - 1) as p:
                    for j in range(HG):
                        norms(n0 + HG * p + j, j % 2)
                for j in range(HG):
                    n = n0 + HG * (NPAIR - 1) + j
                    norms(n, j % 2)
                    if not last:
                        split_k(g + 1, j)
                        if j == 2:
                            split_v(g + 1)
                        if j == HG - 1:
                            pool.wait_ge(s_eh, HG + n - 2)
                            split_o(g + 1, 0)

            group(0, True, False)
            with pool.Fori(1, NG - 1) as g:
                group(g, False, False)
            group(NG - 1, False, True)

        @block.scalar
        def _(act):
            def split_q(r):
                act.wait_ge(s_wq_in[r % 2], 16 * (r // 2 + 1))
                nc.scalar.activation(WQ.hi[:, :, q_quarter(r)], RQ[:, r % 2, :, :], ACT.Copy).then_inc(s_wq_hi, 1)

            nc.scalar.activation(EXP0[:], C.zeros[:, 0:1], ACT.Exp)
            split_q(0)
            ln.split_hi(nc, act, XT, ps, 0, LNB[0])
            ln.split_hi(nc, act, XT, ps, 1, LNB[1])
            split_q(1)
            act.wait_ge(s_bcol, 1)

            def weightsT(n):
                for b in range(2):
                    act.wait_ge(s_pt, 2 * n + b + 1)
                    nc.scalar.activation(PT.hi[:, b, :], bank(TB[b], 3 * P), ACT.Copy).then_inc(s_pt_hi, 1)

            def exps(n, u, b):
                if b == 0:
                    if not (isinstance(n, int) and n < 2):
                        act.wait_ge(s_pt, 2 * n - 2)
                    hold(act, s_nm, n + 1)
                for t, cols in enumerate((slice(0, P), slice(P, 3 * P))):
                    src = bank(SB[b], 3 * P)[:, cols]
                    nc.scalar.activation(PR[:, u, b, cols], src, ACT.Exp, bias=NM[:, b, t:t + 1], scale=SCALE,
                                         accum_out=SUM[:, b, t:t + 1]).then_inc(s_exp, 1)

            def norms(n, u):
                hold(act, s_rs, 2 * n + 2)
                for t, cols in enumerate((slice(0, P), slice(P, 3 * P))):
                    nc.scalar.activation(PR[:, u, 1, cols], PR[:, u, 1, cols], ACT.Copy, scale=RS[:, u, 1, t:t + 1]
                                         ).then_inc(s_norm[1], 1)

            def keys(m, b, h):
                hold(act, s_pr, m + 1)
                nc.scalar.activation(K.hi[:], bank(b), ACT.Identity, bias=BIAS[:, 1, bass.ds(h, 1)]).then_inc(s_pr_hi, 1)

            def queries(d):
                for r in range(NQ):
                    act.wait_ge(s_qf, NQ * d + r + 1)
                    nc.scalar.activation(q_cols(Q.hi, r), q_full(r), ACT.Copy).then_inc(s_pr_hi, 1)
                    if isinstance(d, int) and d == 0 and r < QR // 2:
                        split_q(QR // 2 + r)

            def head(m, b, h, u):
                hold(act, s_pr, m + 1)
                nc.scalar.activation(O.hi[:, u, :], bank(b), ACT.Identity, bias=BIAS[:, 2, bass.ds(h, 1)]).then_inc(s_pr_hi, 1)

            def values(d, w, tiles):
                for a in tiles:
                    act.wait_ge(s_pr, value_tile(d, w) + a + 1)
                    nc.scalar.activation(V.hi[:, a, :], bank(bank_of(value_tile(0, w) + a)), ACT.Copy).then_inc(s_pr_hi, 1)

            def round(d, first, last):
                for s in range(SL):
                    n = SL * d + s
                    if s % HG == 1:
                        values(d, s // HG, (2,))
                    if not (first and s == 0):
                        weightsT(n - 1)
                    exps(n, s % 2, 0)
                    if s % HG == 1:
                        values(d, s // HG, (3,))
                    if not (last and s == SL - 1):
                        keys(key_tile(d, s, first), bank_of(key_tile(0, s, first)), head_of(d, s + 1))
                    exps(n, s % 2, 1)
                    if s % HG:
                        norms(n, s % 2)
                    if s == SL - 1 and not last:
                        queries(d + 1)
                    if not (first and s == 0):
                        head(head_tile(d, s, last), bank_of(head_tile(0, s, last)), head_of(d, s - 1), (s - 1) % 2)
                    if s % HG == 0:
                        norms(n, s % 2)
                        values(d, s // HG, (0, 1))

            keys(0, bank_of(0), 0)
            queries(0)
            ln.split_hi(nc, act, XT, ps, 2, LNB[2])
            ln.split_hi(nc, act, XT, ps, 3, LNB[3])
            round(0, True, False)
            with act.Fori(1, NR - 1) as d:
                round(d, False, False)
            round(NR - 1, False, True)
            weightsT(SL * NR - 1)
            m = head_tile(NR - 1, SL - 1, True) + 1
            head(m, bank_of(m), NH - 1, (HG - 1) % 2)

        @block.vector
        def _(dve):
            def split_q(r):
                dve.wait_ge(s_wq_hi, r + 1)
                sub_rounded(nc.vector, WQ.lo[:, :, q_quarter(r)], RQ[:, r % 2, :, :], WQ.hi[:, :, q_quarter(r)]
                            ).then_inc(s_wq_lo, 1)

            ln.moments(nc.vector, X, 0)
            ln.moments(nc.vector, X, 1)
            ln.normalise(nc.vector, X, 0)
            ln.normalise(nc.vector, X, 1)
            split_q(0)
            dve.wait_ge(s_bt, 1)
            nc.vector.tensor_copy(BIAS[:].rearrange("p z h -> p (z h)"), bank(TB[0], 3 * NH)).then_inc(s_bcol, 1)
            dve.wait_ge(s_bcol, 1)
            ln.split_lo(nc, dve, XT, ps, 0, LNB[0])
            ln.split_lo(nc, dve, XT, ps, 1, LNB[1])
            split_q(1)
            ln.moments(nc.vector, X, 2)
            ln.moments(nc.vector, X, 3)

            def weightsT(n):
                for b in range(2):
                    dve.wait_ge(s_pt_hi, 2 * n + b + 1)
                    sub_rounded(nc.vector, PT.lo[:, b, :], bank(TB[b], 3 * P), PT.hi[:, b, :]).then_inc(s_pt_lo, 1)

            def maxes(n):
                dve.wait_ge(s_sc, n + 1)
                nc.vector.tensor_reduce(MX[:], ps[:, 0:2 * CHUNK].rearrange("p (b n) -> p b n", b=2)[:, :, 0:3 * P]
                                        .rearrange("p b (t s) -> p b t s", s=P), AX_X, ALU.max).then_inc(s_mx, 1)
                dve.wait_ge(s_mx, 2 * n + 1)
                nc.vector.tensor_tensor(MX[:, :, 1], MX[:, :, 1], MX[:, :, 2], ALU.max).then_inc(s_mx, 1)
                dve.wait_ge(s_mx, 2 * n + 2)
                nc.vector.tensor_scalar(NM[:], MX[:, :, 0:2], -SCALE, None, ALU.mult).then_inc(s_nm, 1)

            def sums(n, u, b):
                dve.wait_ge(s_exp, 4 * n + 2 * b + 2)
                nc.vector.reciprocal(RS[:, u, b, :], SUM[:, b, :]).then_inc(s_rs, 1)

            def biased_lo(m, lo, b, bias, hi):
                dve.wait_ge(s_pr_hi, m + 1)
                nc.vector.scalar_tensor_tensor(out=lo, in0=bank(b), scalar=bias, in1=hi.bitcast(F32),
                                               op0=ALU.add, op1=ALU.subtract).then_inc(s_pr_lo, 1)

            def query_bias(d, r):
                m = query_tile(d) + r
                dve.wait_ge(s_pr, m + 1)
                if r >= QS:
                    dve.wait_ge(s_pr_lo, m - QS + 1)
                nc.vector.tensor_tensor(QF[:, r % QS, :].rearrange("p (c t) -> p c t", c=QC),
                                        bank(bank_of(query_tile(0) + r)).rearrange("p (c t) -> p c t", c=QC),
                                        BIAS[:, 0, r * QC:(r + 1) * QC, None].broadcast_to([P, QC, CHUNK // QC]),
                                        ALU.add).then_inc(s_qf, 1)

            def queries(d):
                query_bias(d, 0)
                for r in range(NQ):
                    if r < NQ - 1:
                        query_bias(d, r + 1)
                    dve.wait_ge(s_pr_hi, query_tile(d) + r + 1)
                    sub_rounded(nc.vector, q_cols(Q.lo, r), q_full(r), q_cols(Q.hi, r)).then_inc(s_pr_lo, 1)
                    if isinstance(d, int) and d == 0 and r in (2, 4):
                        ln.normalise(nc.vector, X, 1 + r // 2)

            def head(m, b, h, u):
                biased_lo(m, O.lo[:, u, :], b, BIAS[:, 2, bass.ds(h, 1)], O.hi[:, u, :])

            def values(d, w, tiles):
                for a in tiles:
                    dve.wait_ge(s_pr_hi, value_tile(d, w) + a + 1)
                    sub_rounded(nc.vector, V.lo[:, a, :], bank(bank_of(value_tile(0, w) + a)), V.hi[:, a, :]
                                ).then_inc(s_pr_lo, 1)

            def add_y(it):
                if isinstance(it, int) and it == 0:
                    dve.wait_ge(s_bo, NCH)
                dve.wait_ge(s_eh, HG + HG * (it + 1))
                x = X[:, bass.ds((it % NPAIR) * CT, CT), :].rearrange("p c d -> p (c d)")
                nc.vector.tensor_tensor(x, x, ps[:, YB * CHUNK:(YB + 2) * CHUNK], ALU.add).then_inc(s_ya, 1)

            def keys(m, b, h):
                biased_lo(m, K.lo[:], b, BIAS[:, 1, bass.ds(h, 1)], K.hi[:])

            def round(d, first, last):
                for s in range(SL):
                    n = SL * d + s
                    maxes(n)
                    if s % HG == 1:
                        values(d, s // HG, (2,))
                    if not (first and s == 0):
                        weightsT(n - 1)
                    sums(n, s % 2, 0)
                    if s % HG == 1:
                        values(d, s // HG, (3,))
                    if not (last and s == SL - 1):
                        keys(key_tile(d, s, first), bank_of(key_tile(0, s, first)), head_of(d, s + 1))
                    sums(n, s % 2, 1)
                    if s == SL - 1 and not last:
                        queries(d + 1)
                    if s % HG == 1 and not (first and s == 1):
                        add_y(NW * d + s // HG - 1)
                    if not (first and s == 0):
                        head(head_tile(d, s, last), bank_of(head_tile(0, s, last)), head_of(d, s - 1), (s - 1) % 2)
                    if s % HG == 0:
                        values(d, s // HG, (0, 1))

            keys(0, bank_of(0), 0)
            queries(0)
            ln.split_lo(nc, dve, XT, ps, 2, LNB[2])
            ln.split_lo(nc, dve, XT, ps, 3, LNB[3])
            round(0, True, False)
            with dve.Fori(1, NR - 1) as d:
                round(d, False, False)
            round(NR - 1, False, True)
            weightsT(SL * NR - 1)
            m = head_tile(NR - 1, SL - 1, True) + 1
            head(m, bank_of(m), NH - 1, (HG - 1) % 2)
            add_y(NW * NR - 1)

        @block.tensor
        def _(pe):
            open_at_one(pe, *[s_eh] * HG)
            pe.wait_ge(s_bias, 48)
            nc.tensor.transpose(bank(TB[0], 3 * NH), BROW[:], C.ident[0:3 * NH, 0:3 * NH]).then_inc(s_bt, 1)
            ln.transpose(nc, pe, C, ps, 0, LNB[0])
            ln.transpose(nc, pe, C, ps, 1, LNB[1])

            def scores(n, w, j, count):
                pe.wait_ge(s_pr_lo, count)
                if not (isinstance(n, int) and n == 0):
                    pe.wait_ge(s_exp, 4 * n)
                for b in range(2):
                    q = lambda t: pair(Q, slice(None), w, b, slice(j * S + t * P, j * S + (t + 1) * P))
                    k = lambda t: pair(K, slice(None), slice(b * S, b * S + (t + 1) * P))
                    for t in range(2):
                        at = SB[b] * CHUNK + t * P
                        matmul3(nc, ps[:, at:at + (t + 1) * P], q(t), k(t), t == 0, False, skip_group_check=True)
                    o = bank(SB[b], 4 * P).rearrange("p (t s) -> p t s", s=2 * P)[:, :, 0:P]
                    ins = nc.tensor.matmul(o, C.ident_bf[:], C.causal[:, None, :].broadcast_to([P, 2, P]),
                                           start=False, stop=True, skip_group_check=True)
                ins.then_inc(s_sc, 1)

            def keys(m, b, j, p):
                if not (isinstance(m, int) and m == 0):
                    pe.wait_ge(s_pr_lo, m - 1)
                for k in range(KD):
                    ins = matmul3(nc, bank(b), pair(WK, slice(None), j, k),
                                  pair(XT, slice(None), k, bass.ds(p * CHUNK, CHUNK)), k == 0, k == KD - 1)
                ins.then_inc(s_pr, 1)

            def queries(d):
                group, pairs = d // RG, d % RG
                xt = [a[:].rearrange("p k (q b g i) -> p k q b g i", q=RG, b=2 * NW, g=NG) for a in (XT.hi, XT.lo)]
                for r in range(NQ):
                    m = query_tile(d) + r
                    if isinstance(d, int) and d == 0 and r % 2 == 0:
                        if r < QR:
                            pe.wait_ge(s_wq_lo, r // 2 + 1)
                        else:
                            pe.wait_ge(s_wq_lo_late, r // 2 + 1 - QR // 2)
                    if r >= 2:
                        pe.wait_ge(s_qf, NQ * d + r - 1)
                    elif not (isinstance(d, int) and d == 0 and r == 0):
                        pe.wait_ge(s_pr_lo, m - 1)
                    width = CHUNK // QC
                    for c in range(QC):
                        o = bank(bank_of(query_tile(0) + r))[:, c * width:(c + 1) * width]
                        col = (r * QC + c) * P
                        for k in range(KD):
                            moving = tuple(a[:, k, bass.ds(pairs, 1), :, bass.ds(group, 1), :] for a in xt)
                            ins = matmul3(nc, o, pair(WQ, slice(None), k, slice(col, col + P)), moving,
                                          k == 0, k == KD - 1)
                    ins.then_inc(s_pr, 1)

            pe.wait_ge(s_bcol, 1)

            def head(n, j, m, b):
                pe.wait_ge(s_pt_lo, 2 * n + 2)
                pe.wait_ge(s_pr_lo, m - 1)
                for z in range(2):
                    v = lambda t: pair(V, slice(None), 2 * z + t, slice(j * D_HEAD, (j + 1) * D_HEAD))
                    o = bank(b)[:, z * S:(z + 1) * S]
                    matmul3(nc, o, v(0), pair(PT, slice(None), z, slice(0, S)), True, False)
                    ins = matmul3(nc, o[:, P:S], v(1), pair(PT, slice(None), z, slice(S, 3 * P)), False, True)
                ins.then_inc(s_pr, 1)

            def values(d, w, tiles):
                pe.wait_ge(s_xv, 32 * (NW * d + w + 1))
                for a in tiles:
                    m = value_tile(d, w) + a
                    pe.wait_ge(s_pr_lo, m - 1)
                    for k in range(KD):
                        ins = matmul3(nc, bank(bank_of(value_tile(0, w) + a)), pair(XV, slice(None), k, slice(a * P, (a + 1) * P)),
                                      pair(WV, slice(None), k), k == 0, k == KD - 1)
                    ins.then_inc(s_pr, 1)

            def transposes(n, u):
                if not (isinstance(n, int) and n == 0):
                    pe.wait_ge(s_pt_lo, 2 * n)
                for b in range(2):
                    pe.wait_ge(s_norm[b], 2 * n + 2)
                    for i in range(3):
                        at = TB[b] * CHUNK + i * P
                        ins = nc.tensor.transpose(ps[:, at:at + P], PR[:, u, b, i * P:(i + 1) * P], C.ident[:])
                    ins.then_inc(s_pt, 1)

            def outputs(j, tiles):
                for a in tiles:
                    o = ps[:, YB * CHUNK + a * D:YB * CHUNK + (a + 1) * D]
                    ins = matmul3(nc, o, pair(O, slice(None), j % 2, slice(a * P, (a + 1) * P)), pair(WO, slice(None), j),
                                  j == 0 and a % 2 == 0, j == HG - 1 and a % 2 == 1, skip_group_check=True)
                if CT - 1 in tiles:
                    ins.then_inc(s_eh, 1)

            def round(d, first, last):
                g = d // RG
                for s in range(SL):
                    n, j, w = SL * d + s, s % HG, s // HG
                    scores(n, w, j, key_tile(d, s - 1, first) + 1 if s else query_tile(d) + NQ)
                    if j == 1:
                        values(d, w, (2,))
                    if first and s == 1:
                        pe.wait_ge(ln.s_lo, 2 * NCH)
                    if not (first and s == 0):
                        transposes(n - 1, (s - 1) % 2)
                    if j == 1:
                        values(d, w, (3,))
                    if not (last and s == SL - 1):
                        at = (key_tile(d, s, first), bank_of(key_tile(0, s, first)))
                        if s < SL - 1:
                            pe.wait_ge(s_wk, 2 * (head_of(d, s + 1) + 1))
                            keys(*at, (j + 1) % HG, (d % RG) * NW + (s + 1) // HG)
                        else:
                            pe.wait_ge(s_wk, 2 * (head_of(d, SL) + 1))
                            keys(*at, 0, ((d + 1) % RG) * NW)
                            queries(d + 1)
                    if not (first and s < 2):
                        if j == 2 and not (first and s == 2):
                            pe.wait_ge(s_ya, NW * d + w)
                        pe.wait_ge(s_wo, 2 * ((g if s >= 2 else (d - 1) // RG) * HG + (s - 2) % HG + 1))
                        pe.wait_ge(s_pr_lo, (head_tile(d, s - 1) if s else head_tile(d - 1, SL - 1)) + 1)
                        outputs((s - 2) % HG, (0, 1, 2) if j == 0 else range(CT))
                    if j == 1:
                        pe.wait_ge(s_pr_lo, value_tile(d, w) + CT)
                    if not (first and s == 0):
                        head(n - 1, (s - 1) % HG, head_tile(d, s, last), bank_of(head_tile(0, s, last)))
                    if j == 0 and not (first and s == 0):
                        outputs((s - 2) % HG, (3,))
                    if j == 0:
                        pe.wait_ge(s_wv, 2 * (g + 1))
                        values(d, w, (0, 1))

            pe.wait_ge(s_wk, 2)
            pe.wait_ge(ln.s_lo, 2)
            keys(0, bank_of(0), 0, 0)
            pe.wait_ge(ln.s_lo, 4)
            queries(0)
            ln.transpose(nc, pe, C, ps, 2, LNB[2])
            ln.transpose(nc, pe, C, ps, 3, LNB[3])
            round(0, True, False)
            with pe.Fori(1, NR - 1) as d:
                round(d, False, False)
            round(NR - 1, False, True)
            n = SL * NR - 1
            m = head_tile(NR - 1, SL - 1, True)
            transposes(n, (SL - 1) % 2)
            pe.wait_ge(s_pr_lo, m + 1)
            outputs(HG - 2, range(CT))
            head(n, HG - 1, m + 1, bank_of(m + 1))
            pe.wait_ge(s_pr_lo, m + 2)
            outputs(HG - 1, range(CT))


def macaron(nc, io, out):
    x = io["L0_attn_x"].rearrange("b t d -> (b t) d")
    T, D = x.shape
    w = {k: io["L0_ffn_" + k] for k in ("router", "w_up_gate", "w_down", "shared_w_up_gate", "shared_w_down")}
    E = w["router"].shape[1]
    CAP = -(-int(T * TOP_K * CAP_FACTOR) // E)
    o = out.rearrange("b t d -> (b t) d")
    xbuf = nc.dram_tensor("expert_in", (E * CAP, D), F32, kind="Internal").ap()
    ybuf = nc.dram_tensor("expert_out", (E * CAP, D), F32, kind="Internal").ap()
    with ExitStack() as ctx:
        ps = ctx.enter_context(nc.psum_tensor("ps", [P, 8 * CHUNK], F32))
        X = ctx.enter_context(nc.sbuf_tensor("x", [P, T // P, D], F32))
        C = Consts(ctx, nc, E)
        first_sems = Sems(nc)
        ffn_block(first_sems, nc, "f1_", ps, C, X, w, x, None, xbuf, ybuf, True)
        first_sems.clear()
        attention_block(Sems(nc), nc, "at_", ps, C, X, io)
        ffn_block(Sems(nc), nc, "f2_", ps, C, X, w, None, o, xbuf, ybuf, False)


_INS = ["L0_attn_x", "L0_attn_Wq", "L0_attn_bq", "L0_attn_Wk", "L0_attn_bk", "L0_attn_Wv", "L0_attn_bv",
        "L0_attn_Wo", "L0_attn_bo", "L0_ffn_router", "L0_ffn_w_up_gate", "L0_ffn_w_down",
        "L0_ffn_shared_w_up_gate", "L0_ffn_shared_w_down"]


def kernel(**inputs):
    import numpy as _np
    import concourse.bacc as _bacc
    from concourse import mybir as _mybir
    from concourse.bass_utils import run_bass_kernel_spmd as _run

    nc = _bacc.Bacc("TRN2", target_bir_lowering=False, num_devices=1)
    arrays, io = {}, {}
    for name in _INS:
        a = _np.ascontiguousarray(inputs[name])
        arrays["in_" + name] = a
        io[name] = nc.dram_tensor("in_" + name, a.shape, _mybir.dt.from_np(a.dtype), kind="ExternalInput").ap()
    out = nc.dram_tensor("out", arrays["in_L0_attn_x"].shape, _mybir.dt.float32, kind="ExternalOutput").ap()
    macaron(nc, io, out)
    r = _run(nc, [arrays], core_ids=[0])
    return r.results[0]["out"]
```
